# Optimizing a Trainium2 kernel written in Bass

```python
import numpy as np
import jax
import jax.numpy as jnp

def _softmax(x, axis=-1):
    return jax.nn.softmax(x, axis=axis)

def _gelu(x):
    return jax.nn.gelu(x, approximate=True)

def _silu(x):
    return jax.nn.silu(x)

def _sigmoid(x):
    return jax.nn.sigmoid(x)

def _layernorm(x, axis=-1, eps=1e-05):
    m = jnp.mean(x, axis=axis, keepdims=True)
    v = jnp.var(x, axis=axis, keepdims=True)
    return (x - m) / jnp.sqrt(v + eps)

def _scatter_add(tgt, idx, src, axis=0):
    return tgt.at[idx].add(src)

def _segment_sum(src, seg, n):
    return jax.ops.segment_sum(src, seg, n)
kernel_name = 'mk_recurrent_d2_jaxref_r4_5d000d'

def setup_inputs(seed: int=0):
    np.random.seed(seed)
    _w = jnp.asarray

    def _L0_attn_setup():
        import jax, jax.numpy as jnp
        import numpy as np
        HID = 256
        NH = 16
        HD = HID // NH
        RANK = 16
        B, L = (2, 512)
        key = jax.random.key(seed)
        ks = jax.random.split(key, 9)
        s = 0.02
        return {'x': jax.random.normal(ks[0], (B, L, HID), dtype=jnp.float32), 'Wq': jax.random.normal(ks[1], (HID, HID), dtype=jnp.float32) * s, 'Wk': jax.random.normal(ks[2], (HID, HID), dtype=jnp.float32) * s, 'Wv': jax.random.normal(ks[3], (HID, HID), dtype=jnp.float32) * s, 'Wg': jax.random.normal(ks[4], (HID, HID), dtype=jnp.float32) * s, 'Wgk1': jax.random.normal(ks[5], (HID, RANK), dtype=jnp.float32) * s, 'Wgk2': jax.random.normal(ks[6], (RANK, HID), dtype=jnp.float32) * s, 'bgk2': jnp.zeros((HID,), dtype=jnp.float32), 'gamma': jnp.ones((HID,), dtype=jnp.float32), 'beta': jnp.zeros((HID,), dtype=jnp.float32), 'Wout': jax.random.normal(ks[7], (HID, HID), dtype=jnp.float32) * s}
    _L0_attn_in = _L0_attn_setup()

    def _L0_ffn_setup():
        import jax, jax.numpy as jnp
        import numpy as np
        D_MODEL = 256
        N_EXPERTS = 8
        TOP_K = 2
        BOTTLENECK = 64
        B, S = (2, 1024)
        ADAPTER_SCALE = 0.5

        def _moe_forward(x, w_gate, w_noise, Wd, bd, Wu, bu):
            b, s, d = x.shape
            xf = x.reshape(-1, d)
            T = xf.shape[0]
            clean_logits = xf @ w_gate
            logits = clean_logits
            k1 = min(TOP_K + 1, N_EXPERTS)
            top_logits, top_idx = jax.lax.top_k(logits, k1)
            top_k_logits = top_logits[:, :TOP_K]
            top_k_idx = top_idx[:, :TOP_K]
            top_k_gates = jax.nn.softmax(top_k_logits, axis=-1)
            rows = jnp.arange(T)[:, None]
            gates = jnp.zeros((T, N_EXPERTS), dtype=top_k_gates.dtype)
            gates = gates.at[rows, top_k_idx].set(top_k_gates)
            h = jax.nn.relu(jnp.einsum('td,edb->teb', xf, Wd) + bd[None, :, :])
            y = jnp.einsum('teb,ebd->ted', h, Wu) + bu[None, :, :]
            y = ADAPTER_SCALE * y
            out = jnp.einsum('te,ted->td', gates, y)
            return out.reshape(b, s, d)
        key = jax.random.key(seed)
        ks = jax.random.split(key, 8)
        sd = 0.02
        x = jax.random.normal(ks[0], (B, S, D_MODEL), dtype=jnp.float32)
        w_gate = jax.random.normal(ks[1], (D_MODEL, N_EXPERTS), dtype=jnp.float32) * sd
        w_noise = jax.random.normal(ks[2], (D_MODEL, N_EXPERTS), dtype=jnp.float32) * sd
        Wd = jax.random.normal(ks[3], (N_EXPERTS, D_MODEL, BOTTLENECK), dtype=jnp.float32) * sd
        bd = jnp.zeros((N_EXPERTS, BOTTLENECK), dtype=jnp.float32)
        Wu = jax.random.normal(ks[4], (N_EXPERTS, BOTTLENECK, D_MODEL), dtype=jnp.float32) * sd
        bu = jnp.zeros((N_EXPERTS, D_MODEL), dtype=jnp.float32)
        return {'x': x, 'w_gate': w_gate, 'w_noise': w_noise, 'Wd': Wd, 'bd': bd, 'Wu': Wu, 'bu': bu}
    _L0_ffn_in = _L0_ffn_setup()

    def _L1_attn_setup():
        import jax, jax.numpy as jnp
        import numpy as np
        DIM = 256
        NUM_HEADS = 16
        NUM_KV_HEADS = 2
        HEAD_DIM = DIM // NUM_HEADS
        REPEATS = NUM_HEADS // NUM_KV_HEADS
        WINDOW = 64
        HALF = WINDOW // 2
        BATCH, SEQ = (2, 512)
        key = jax.random.key(seed)
        ks = jax.random.split(key, 9)
        sc = 1.0 / np.sqrt(DIM)
        return {'x': jax.random.normal(ks[0], (BATCH, SEQ, DIM), jnp.float32), 'Wq': jax.random.normal(ks[1], (DIM, NUM_HEADS * HEAD_DIM), jnp.float32) * sc, 'bq': jax.random.normal(ks[2], (NUM_HEADS * HEAD_DIM,), jnp.float32) * 0.01, 'Wk': jax.random.normal(ks[3], (DIM, NUM_KV_HEADS * HEAD_DIM), jnp.float32) * sc, 'bk': jax.random.normal(ks[4], (NUM_KV_HEADS * HEAD_DIM,), jnp.float32) * 0.01, 'Wv': jax.random.normal(ks[5], (DIM, NUM_KV_HEADS * HEAD_DIM), jnp.float32) * sc, 'bv': jax.random.normal(ks[6], (NUM_KV_HEADS * HEAD_DIM,), jnp.float32) * 0.01, 'Wo': jax.random.normal(ks[7], (DIM, DIM), jnp.float32) * sc, 'bo': jax.random.normal(ks[8], (DIM,), jnp.float32) * 0.01}
    _L1_attn_in = _L1_attn_setup()

    def _L1_ffn_setup():
        import jax, jax.numpy as jnp
        import numpy as np

        def _bitlinear(x, w_latent):
            scale = jax.lax.stop_gradient(jnp.clip(jnp.mean(jnp.abs(w_latent), axis=1, keepdims=True), 1e-05, None))
            tern = jnp.clip(jnp.round(w_latent / scale), -1.0, 1.0)
            w = w_latent + jax.lax.stop_gradient(tern - w_latent)
            return x @ (w * scale).T
        key = jax.random.key(seed)
        ks = jax.random.split(key, 6)
        dim, hidden, rank = (256, 1024, 16)
        B, S = (4, 1024)
        x = jax.random.normal(ks[0], (B, S, dim), dtype=jnp.float32)
        w_fc = 0.02 * jax.random.normal(ks[1], (hidden, dim), dtype=jnp.float32)
        w_proj = 0.02 * jax.random.normal(ks[2], (dim, hidden), dtype=jnp.float32)
        u = 0.02 * jax.random.normal(ks[3], (hidden, rank), dtype=jnp.float32)
        v = 0.02 * jax.random.normal(ks[4], (rank, dim), dtype=jnp.float32)
        fast_b = jax.random.normal(ks[5], (rank, rank), dtype=jnp.float32)
        gate = jnp.float32(0.05)
        return {'x': x, 'fast_b': fast_b, 'w_fc': w_fc, 'w_proj': w_proj, 'u': u, 'v': v, 'gate': gate}
    _L1_ffn_in = _L1_ffn_setup()
    _d = {'L0_attn_x': _L0_attn_in['x'], 'L0_attn_Wq': _L0_attn_in['Wq'], 'L0_attn_Wk': _L0_attn_in['Wk'], 'L0_attn_Wv': _L0_attn_in['Wv'], 'L0_attn_Wg': _L0_attn_in['Wg'], 'L0_attn_Wgk1': _L0_attn_in['Wgk1'], 'L0_attn_Wgk2': _L0_attn_in['Wgk2'], 'L0_attn_bgk2': _L0_attn_in['bgk2'], 'L0_attn_gamma': _L0_attn_in['gamma'], 'L0_attn_beta': _L0_attn_in['beta'], 'L0_attn_Wout': _L0_attn_in['Wout'], 'L0_ffn_w_gate': _L0_ffn_in['w_gate'], 'L0_ffn_w_noise': _L0_ffn_in['w_noise'], 'L0_ffn_Wd': _L0_ffn_in['Wd'], 'L0_ffn_bd': _L0_ffn_in['bd'], 'L0_ffn_Wu': _L0_ffn_in['Wu'], 'L0_ffn_bu': _L0_ffn_in['bu'], 'L1_attn_Wq': _L1_attn_in['Wq'], 'L1_attn_bq': _L1_attn_in['bq'], 'L1_attn_Wk': _L1_attn_in['Wk'], 'L1_attn_bk': _L1_attn_in['bk'], 'L1_attn_Wv': _L1_attn_in['Wv'], 'L1_attn_bv': _L1_attn_in['bv'], 'L1_attn_Wo': _L1_attn_in['Wo'], 'L1_attn_bo': _L1_attn_in['bo'], 'L1_ffn_fast_b': _L1_ffn_in['fast_b'], 'L1_ffn_w_fc': _L1_ffn_in['w_fc'], 'L1_ffn_w_proj': _L1_ffn_in['w_proj'], 'L1_ffn_u': _L1_ffn_in['u'], 'L1_ffn_v': _L1_ffn_in['v'], 'L1_ffn_gate': _L1_ffn_in['gate']}
    _x0 = _d['L0_attn_x']
    _d['L0_attn_x'] = jax.random.normal(jax.random.fold_in(jax.random.key(seed), 1), (16, 1024, 256), dtype=_x0.dtype)
    del _x0
    return _d

def reference(L0_attn_x, L0_attn_Wq, L0_attn_Wk, L0_attn_Wv, L0_attn_Wg, L0_attn_Wgk1, L0_attn_Wgk2, L0_attn_bgk2, L0_attn_gamma, L0_attn_beta, L0_attn_Wout, L0_ffn_w_gate, L0_ffn_w_noise, L0_ffn_Wd, L0_ffn_bd, L0_ffn_Wu, L0_ffn_bu, L1_attn_Wq, L1_attn_bq, L1_attn_Wk, L1_attn_bk, L1_attn_Wv, L1_attn_bv, L1_attn_Wo, L1_attn_bo, L1_ffn_fast_b, L1_ffn_w_fc, L1_ffn_w_proj, L1_ffn_u, L1_ffn_v, L1_ffn_gate):

    def _L0_attn_ref(x, Wq, Wk, Wv, Wg, Wgk1, Wgk2, bgk2, gamma, beta, Wout):
        import jax, jax.numpy as jnp
        import numpy as np
        HID = 256
        NH = 16
        HD = HID // NH
        RANK = 16
        B, L = (2, 512)
        Bb, Ll, Hid = x.shape
        H, Dh = (NH, HD)
        q = (x @ Wq).reshape(Bb, Ll, H, Dh)
        k = (x @ Wk).reshape(Bb, Ll, H, Dh)
        v = (x @ Wv).reshape(Bb, Ll, H, Dh)
        gk = (jax.nn.log_sigmoid(x @ Wgk1 @ Wgk2 + bgk2) / 16.0).reshape(Bb, Ll, H, Dh)
        qT = jnp.transpose(q, (1, 0, 2, 3))
        kT = jnp.transpose(k, (1, 0, 2, 3))
        vT = jnp.transpose(v, (1, 0, 2, 3))
        gT = jnp.transpose(gk, (1, 0, 2, 3))

        def step(state, inp):
            qt, kt, vt, gt = inp
            gate = jnp.exp(gt)
            state = state * gate[..., None] + vt[..., None] * kt[..., None, :]
            out_t = jnp.einsum('bhvk,bhk->bhv', state, qt)
            return (state, out_t)
        state0 = jnp.zeros((Bb, H, Dh, Dh), dtype=x.dtype)
        _, outs = jax.lax.scan(step, state0, (qT, kT, vT, gT))
        out = jnp.transpose(outs, (1, 0, 2, 3)).reshape(Bb, Ll, Hid)
        mu = out.mean(-1, keepdims=True)
        var = out.var(-1, keepdims=True)
        out = (out - mu) / jnp.sqrt(var + 1e-05) * gamma + beta
        out = out * jax.nn.silu(x @ Wg)
        return out @ Wout

    def _L0_ffn_ref(x, w_gate, w_noise, Wd, bd, Wu, bu):
        import jax, jax.numpy as jnp
        import numpy as np
        D_MODEL = 256
        N_EXPERTS = 8
        TOP_K = 2
        BOTTLENECK = 64
        B, S = (2, 1024)
        ADAPTER_SCALE = 0.5

        def _moe_forward(x, w_gate, w_noise, Wd, bd, Wu, bu):
            b, s, d = x.shape
            xf = x.reshape(-1, d)
            T = xf.shape[0]
            clean_logits = xf @ w_gate
            logits = clean_logits
            k1 = min(TOP_K + 1, N_EXPERTS)
            top_logits, top_idx = jax.lax.top_k(logits, k1)
            top_k_logits = top_logits[:, :TOP_K]
            top_k_idx = top_idx[:, :TOP_K]
            top_k_gates = jax.nn.softmax(top_k_logits, axis=-1)
            rows = jnp.arange(T)[:, None]
            gates = jnp.zeros((T, N_EXPERTS), dtype=top_k_gates.dtype)
            gates = gates.at[rows, top_k_idx].set(top_k_gates)
            h = jax.nn.relu(jnp.einsum('td,edb->teb', xf, Wd) + bd[None, :, :])
            y = jnp.einsum('teb,ebd->ted', h, Wu) + bu[None, :, :]
            y = ADAPTER_SCALE * y
            out = jnp.einsum('te,ted->td', gates, y)
            return out.reshape(b, s, d)
        return _moe_forward(x, w_gate, w_noise, Wd, bd, Wu, bu)

    def _L1_attn_ref(x, Wq, bq, Wk, bk, Wv, bv, Wo, bo):
        import jax, jax.numpy as jnp
        import numpy as np
        DIM = 256
        NUM_HEADS = 16
        NUM_KV_HEADS = 2
        HEAD_DIM = DIM // NUM_HEADS
        REPEATS = NUM_HEADS // NUM_KV_HEADS
        WINDOW = 64
        HALF = WINDOW // 2
        BATCH, SEQ = (2, 512)
        b, s, _ = x.shape
        q = (x @ Wq + bq).reshape(b, s, NUM_HEADS, HEAD_DIM).transpose(0, 2, 1, 3)
        k = (x @ Wk + bk).reshape(b, s, NUM_KV_HEADS, HEAD_DIM).transpose(0, 2, 1, 3)
        v = (x @ Wv + bv).reshape(b, s, NUM_KV_HEADS, HEAD_DIM).transpose(0, 2, 1, 3)
        kp = jnp.pad(k, ((0, 0), (0, 0), (HALF, HALF), (0, 0)))
        vp = jnp.pad(v, ((0, 0), (0, 0), (HALF, HALF), (0, 0)))
        idx = jnp.arange(s)[:, None] + jnp.arange(WINDOW)[None, :]
        k_win = kp[:, :, idx]
        v_win = vp[:, :, idx]
        qg = q.reshape(b, NUM_KV_HEADS, REPEATS, s, HEAD_DIM)
        scores = jnp.einsum('bgrsd,bgswd->bgrsw', qg, k_win)
        probs = jax.nn.softmax(scores, axis=-1)
        out = jnp.einsum('bgrsw,bgswd->bgrsd', probs, v_win)
        out = out.reshape(b, NUM_HEADS, s, HEAD_DIM).transpose(0, 2, 1, 3).reshape(b, s, DIM)
        return out @ Wo + bo

    def _L1_ffn_ref(x, fast_b, w_fc, w_proj, u, v, gate):
        import jax, jax.numpy as jnp
        import numpy as np

        def _bitlinear(x, w_latent):
            scale = jax.lax.stop_gradient(jnp.clip(jnp.mean(jnp.abs(w_latent), axis=1, keepdims=True), 1e-05, None))
            tern = jnp.clip(jnp.round(w_latent / scale), -1.0, 1.0)
            w = w_latent + jax.lax.stop_gradient(tern - w_latent)
            return x @ (w * scale).T
        h = _bitlinear(x, w_fc) + gate * (x @ v.T @ fast_b.T @ u.T)
        r = jnp.maximum(h, 0.0)
        return _bitlinear(r * r, w_proj)
    x = L0_attn_x
    xn = _layernorm(x, axis=-1)
    s = _L0_attn_ref(xn, L0_attn_Wq, L0_attn_Wk, L0_attn_Wv, L0_attn_Wg, L0_attn_Wgk1, L0_attn_Wgk2, L0_attn_bgk2, L0_attn_gamma, L0_attn_beta, L0_attn_Wout)
    g = _silu(_L0_ffn_ref(xn, L0_ffn_w_gate, L0_ffn_w_noise, L0_ffn_Wd, L0_ffn_bd, L0_ffn_Wu, L0_ffn_bu))
    x = x + s * g
    xn = _layernorm(x, axis=-1)
    s = _L1_attn_ref(xn, L1_attn_Wq, L1_attn_bq, L1_attn_Wk, L1_attn_bk, L1_attn_Wv, L1_attn_bv, L1_attn_Wo, L1_attn_bo)
    g = _silu(_L1_ffn_ref(xn, L1_ffn_fast_b, L1_ffn_w_fc, L1_ffn_w_proj, L1_ffn_u, L1_ffn_v, L1_ffn_gate))
    x = x + s * g
    return x

_drawn_inputs = setup_inputs


def setup_inputs(seed=0):
    import zlib

    import numpy as np

    out = dict(_drawn_inputs(seed))
    spreads = {'L0_attn_bgk2': (0.0, 0.8),
     'L0_attn_gamma': (1.0, 0.6),
     'L0_attn_beta': (0.0, 0.8),
     'L0_ffn_bd': (0.0, 0.8),
     'L0_ffn_bu': (0.0, 0.8)}
    factors = {'L0_attn_Wq': 8.0,
     'L0_attn_Wk': 8.0,
     'L0_attn_Wv': 8.0,
     'L0_attn_Wg': 8.0,
     'L0_attn_Wgk1': 8.0,
     'L0_attn_Wgk2': 8.0,
     'L0_attn_Wout': 8.0,
     'L0_ffn_w_gate': 8.0,
     'L0_ffn_Wd': 8.0,
     'L0_ffn_Wu': 8.0,
     'L1_attn_Wq': 4.541,
     'L1_attn_bq': 8.0,
     'L1_attn_Wk': 4.507,
     'L1_attn_bk': 64.0,
     'L1_attn_Wv': 4.406,
     'L1_attn_bv': 8.0,
     'L1_attn_Wo': 4.405,
     'L1_attn_bo': 64.0,
     'L1_ffn_fast_b': 8.0,
     'L1_ffn_w_fc': 5.565,
     'L1_ffn_w_proj': 4.42,
     'L1_ffn_u': 8.0,
     'L1_ffn_v': 8.0}
    for name, (base, spread) in spreads.items():
        noise = np.random.default_rng([zlib.crc32(name.encode()), seed]).standard_normal(out[name].shape)
        drawn = base * np.exp(spread * noise) if base else spread * noise
        out[name] = jnp.asarray(drawn.astype(out[name].dtype))
    for name, factor in factors.items():
        out[name] = (out[name] * factor).astype(out[name].dtype)
    return out
```

```python
from contextlib import ExitStack

import numpy as np
import concourse.bass as bass
from concourse import mybir

F32 = mybir.dt.float32
F32R = mybir.dt.float32r
BF16 = mybir.dt.bfloat16
U32 = mybir.dt.uint32
ALU = mybir.AluOpType
ACT = mybir.ActivationFunctionType
AX = mybir.AxisListType

P = 128
D = 256
KD = D // P
S = 1024
NC = S // P
NG = S // 512
H = 16
DH = D // H
HH = H // 2
E = 8
BN = 64
EB = E * BN
RANK = 16
QB = 64
WIN = 64
HALF = WIN // 2
KW = 192
HID = 1024
MT = HID // P
EPS = 1e-5
BIG = -1e30
DV = DH + 1


def build_program(nc, a, out, n_seq):
    ctx = ExitStack()
    ctx.enter_context(nc.allow_non_contiguous_dma(reason="small transposed weights"))

    def sb(name, shape, dt=F32):
        return ctx.enter_context(nc.sbuf_tensor(name, shape, dt))

    def sem(name):
        return ctx.enter_context(nc.semaphore(name))

    x_dram = a["L0_attn_x"].rearrange("b (c p) d -> (b c) p d", p=P)
    out_dram = out.rearrange("b (c p) d -> (b c) p d", p=P)

    ident = sb("ident", [P, P])
    ident_bf = sb("ident_bf", [P, P], BF16)
    causal = sb("causal", [P, P])
    cum_mid = sb("cum_mid", [P, P])
    first_half = sb("first_half", [P, P])
    second_half = sb("second_half", [P, P])
    head_block = sb("head_block", [P, P])
    head_mask = sb("head_mask", [P, HH])
    expert_no = sb("expert_no", [P, E])
    minus_half = sb("minus_half", [P, NC])
    same_q = sb("same_q", [P, QB], BF16)
    block_ones = sb("block_ones", [P, 2, P], BF16)
    block_band = sb("block_band", [P, 2, P], BF16)
    chunk_band = sb("chunk_band", [P, KW], BF16)

    w_vg = sb("w_vg", [P, KD, 2 * D])
    w_k = sb("w_k", [P, KD, D])
    w_q = sb("w_q", [P, KD, D])
    w_z = sb("w_z", [P, KD, D])
    w_out = sb("w_out", [P, KD, D])
    w_gate = sb("w_gate", [P, KD, E])
    w_down = sb("w_down", [P, KD, EB])
    w_up = sb("w_up", [P, EB // P, D])
    b_up = sb("b_up", [P, D])
    bc_gk = sb("bc_gk", [P, D])
    bc_gamma = sb("bc_gamma", [P, D])
    bc_beta = sb("bc_beta", [P, D])
    bc_down = sb("bc_down", [P, EB])
    gk1_t = sb("gk1_t", [RANK, D])
    gk2 = sb("gk2", [RANK, D])

    x = sb("x", [P, NC, D])
    xn = sb("xn", [P, NC, D])
    SH = S + 2 * HALF
    xt2 = sb("xt2", [P, KD, SH])
    xt = xt2[:, :, HALF:HALF + S]
    qt = sb("qt", [P, KD, S])
    k2 = sb("k2", [P, 2, SH])
    kt = k2[:, :, HALF:HALF + S]
    zb = sb("zb", [P, NC, D])
    gk = sb("gk", [P, NC, D])
    zact = sb("zact", [P, 2, D])
    stats = sb("stats", [P, NC, 6])
    moments = sb("moments", [P, NC, 2])
    veps = sb("veps", [P, NC])
    rstd = sb("rstd", [P, NC])
    logits = sb("logits", [P, NC, E])
    top = sb("top", [P, NC, E])
    top_i = sb("top_i", [P, NC, E], U32)
    top_f = sb("top_f", [P, NC, 2])
    gdiff = sb("gdiff", [P, NC])
    gexp = sb("gexp", [P, NC])
    gden = sb("gden", [P, NC])
    g_top = sb("g_top", [P, 2, NC])
    g_hit = sb("g_hit", [P, 2, NC, E])
    gates = sb("gates", [P, NC, P])

    qx = sb("qx", [P, H, P])
    am = sb("am", [P, H, P])
    ktok = sb("ktok", [P, D])
    vt = sb("vt", [P, HH, 4, DH])
    decay_in = sb("decay_in", [P, D])
    decay_out = sb("decay_out", [P, D])
    decay_state = sb("decay_state", [P, 2, D])
    end_mask = sb("end_mask", [P, 2, P])
    tanh_g = sb("tanh_g", [P, D])
    silu_g = sb("silu_g", [P, D])
    hb = sb("hb", [P, EB])
    hg = sb("hg", [P, EB])
    hgt = sb("hgt", [P, EB // P, P])
    gates_t = sb("gates_t", [P, NC, P])
    state = sb("state", [P, 2, P])
    state_mid = sb("state_mid", [P, 2, P])
    state_sum = sb("state_sum", [P, 2, P])
    ot = sb("ot", [P, 2, P])
    o_tok = sb("o_tok", [P, D])
    o_stats = sb("o_stats", [P, 6])
    o_mom = sb("o_mom", [P, 2])
    o_veps = sb("o_veps", [P, 1])
    o_rstd = sb("o_rstd", [P, 1])
    o_norm = sb("o_norm", [P, D])
    o_gam = sb("o_gam", [P, D])
    o_bet = sb("o_bet", [P, D])
    y_tok = sb("y_tok", [P, D])
    yt = sb("yt", [P, KD, P])
    tanh_f = sb("tanh_f", [P, D])
    f_gate = sb("f_gate", [P, D])
    sf = sb("sf", [P, D])

    w_q2 = sb("w_q2", [P, KD, D])
    w_kv2 = sb("w_kv2", [P, KD, 2, 2 * DH])
    w_k2r = sb("w_k2r", [P, KD, 2, HH, DH])
    w_o2 = sb("w_o2", [P, KD, D])
    b_q2 = sb("b_q2", [P, 2])
    b_k2 = sb("b_k2", [P, 2])
    bc_v2 = sb("bc_v2", [P, 2 * DH])
    bc_o2 = sb("bc_o2", [P, D])
    v_nat = sb("v_nat", [RANK, D])
    fb_t = sb("fb_t", [RANK, RANK])
    ffn_gate = sb("ffn_gate", [P, 1])
    w_low = sb("w_low", [P, KD, P])
    scale_fc = sb("scale_fc", [P, MT])
    scale_pj = sb("scale_pj", [P, KD])
    thr = sb("thr", [P, 2, MT])
    rscale = sb("rscale", [P, MT])
    u_nat = sb("u_nat", [P, MT, RANK])
    u_hi = sb("u_hi", [P, MT, RANK], F32R)
    u_lo = sb("u_lo", [P, MT, RANK])
    fc_t = sb("fc_t", [P, KD, HID], F32R)
    pj_t = sb("pj_t", [P, MT, D], F32R)
    u_t = sb("u_t", [P, HID], F32R)

    xh = sb("xh", [P, KD, 512], F32R)
    xl = sb("xl", [P, KD, 512], F32R)
    q2 = qt
    k2_bf = sb("k2_bf", [P, 2, SH], BF16)
    v2 = sb("v2", [P, 2 * NC, 2, DV])
    qx_bf = gates_t[:].rearrange("p c t -> p (c t)").bitcast(BF16).rearrange("p (h t) -> p h t", t=P)
    neg_max = sb("neg_max", [P, H])
    diag_max = hg[:].bitcast(BF16).rearrange("p (h q) -> p h q", q=QB)
    pr = xn[:, 0:4, :].rearrange("p c d -> p (c d)").rearrange("p (b h q) -> p b h q", b=2, q=QB)
    rden = sb("rden", [P, H])
    o2 = sb("o2", [P, D])
    o2t = sb("o2t", [P, KD, P])
    attn2 = zb
    t_hi = hb[:].bitcast(F32R)
    t_st = sb("t_st", [P, 512], F32R)
    relu = am[:, 0:8, :].rearrange("p h t -> p (h t)").rearrange("p (b t) -> p b t", b=2)
    sq = am[:, 8:16, :].rearrange("p h t -> p (h t)").rearrange("p (b t) -> p b t", b=2)
    sq_hi = sb("sq_hi", [P, 2, 512], F32R)
    sq_lo = sb("sq_lo", [P, 2, 512], F32R)
    ft = gk[:, 0:4, :].rearrange("p c d -> p (c d)").rearrange("p (o t) -> p o t", o=KD)
    fc_nat, fc_ter, pj_nat, pj_ter = x, xn, qt, kt
    u_st = gates

    bank = [ctx.enter_context(nc.psum_tensor(f"bank{i}", [P, 512], F32)) for i in range(8)]

    w_sem, cst, prep, prep_done = sem("w_sem"), sem("cst"), sem("prep"), sem("prep_done")

    loads = [
        (w_vg[:, :, 0:D], a["L0_attn_Wv"].rearrange("(k p) n -> p k n", p=P)),
        (w_vg[:, :, D:2 * D], a["L0_attn_Wg"].rearrange("(k p) n -> p k n", p=P)),
        (w_k[:], a["L0_attn_Wk"].rearrange("(k p) n -> p k n", p=P)),
        (w_q[:], a["L0_attn_Wq"].rearrange("(k p) n -> p k n", p=P)),
        (w_out[:], a["L0_attn_Wout"].rearrange("(k p) n -> p k n", p=P)),
        (w_gate[:], a["L0_ffn_w_gate"].rearrange("(k p) n -> p k n", p=P)),
        (w_up[:], a["L0_ffn_Wu"].rearrange("(j e) b d -> (e b) j d", e=2)),
        (b_up[0:E, :], a["L0_ffn_bu"]),
        (bc_gk[:], a["L0_attn_bgk2"].partition_broadcast(P)),
        (bc_gamma[:], a["L0_attn_gamma"].partition_broadcast(P)),
        (bc_beta[:], a["L0_attn_beta"].partition_broadcast(P)),
        (bc_down[:], a["L0_ffn_bd"].rearrange("e b -> (e b)").partition_broadcast(P)),
        (gk1_t[:], a["L0_attn_Wgk1"].rearrange("n r -> r n")),
        (gk2[:], a["L0_attn_Wgk2"]),
    ]
    loads += [
        (w_q2[:], a["L1_attn_Wq"].rearrange("(k p) n -> p k n", p=P)),
        (w_kv2[:, :, 0, :], a["L1_attn_Wk"].rearrange("(k p) n -> p k n", p=P)),
        (w_kv2[:, :, 1, :], a["L1_attn_Wv"].rearrange("(k p) n -> p k n", p=P)),
        (w_o2[:], a["L1_attn_Wo"].rearrange("(k p) n -> p k n", p=P)),
        (b_q2[:], a["L1_attn_bq"].rearrange("(k p) -> p k", p=P)),
        (bc_v2[:], a["L1_attn_bv"].partition_broadcast(P)),
        (bc_o2[:], a["L1_attn_bo"].partition_broadcast(P)),
        (v_nat[:], a["L1_ffn_v"]),
        (fb_t[:], a["L1_ffn_fast_b"].rearrange("j i -> i j")),
        (ffn_gate[:], a["L1_ffn_gate"].partition_broadcast(P)),
        (u_nat[:], a["L1_ffn_u"].rearrange("(m p) r -> p m r", p=P)),
        (fc_nat[:], a["L1_ffn_w_fc"].rearrange("(m p) d -> p m d", p=P)),
        (pj_nat[:], a["L1_ffn_w_proj"].rearrange("(o p) h -> p o h", p=P)),
    ]
    for h in range(HH):
        loads.append((b_k2[h * DH:(h + 1) * DH, :], a["L1_attn_bk"].rearrange("(g d) -> d g", g=2)))
    for k in range(KD):
        loads.append((w_down[:, k, :].rearrange("p (e b) -> p e b", e=E),
                      a["L0_ffn_Wd"][:, k * P:(k + 1) * P, :].rearrange("e p b -> p e b")))

    with nc.Block() as block:

        @block.gpsimd
        def _(pool):
            done = [0]

            def link(ins):
                done[0] += 1
                ins.then_inc(cst, 1)
                pool.wait_ge(cst, done[0])

            def band(tile, lo, hi, width):
                link(nc.gpsimd.affine_select(out=tile, in_=tile, compare_op=ALU.is_ge, fill=BIG, base=0,
                                             pattern=[[1, width]], channel_multiplier=-1))
                link(nc.gpsimd.affine_select(out=tile, in_=tile, compare_op=ALU.is_ge, fill=BIG, base=WIN - 1,
                                             pattern=[[-1, width]], channel_multiplier=1))

            for t in (ident, ident_bf, second_half, same_q, block_ones, block_band, chunk_band, gates, vt,
                      state, xt2, k2, k2_bf, w_low):
                link(nc.gpsimd.memset(t[:], 0.0))
            for t in (causal, head_block, head_mask, first_half):
                link(nc.gpsimd.memset(t[:], 1.0))
            link(nc.gpsimd.memset(minus_half[:], -0.5))
            link(nc.gpsimd.memset(v2[:], 1.0))
            for t in (ident, ident_bf):
                link(nc.gpsimd.affine_select(out=t[:], in_=t[:], compare_op=ALU.not_equal, fill=1.0, base=0,
                                             pattern=[[-1, P]], channel_multiplier=1))
            for base in (0, -QB):
                link(nc.gpsimd.affine_select(out=same_q[:], in_=same_q[:], compare_op=ALU.not_equal, fill=1.0,
                                             base=base, pattern=[[-1, QB]], channel_multiplier=1))
            link(nc.gpsimd.affine_select(out=causal[:], in_=causal[:], compare_op=ALU.is_ge, fill=0.0, base=0,
                                         pattern=[[1, P]], channel_multiplier=-1))
            link(nc.gpsimd.tensor_copy(cum_mid[:], causal[:]))
            link(nc.gpsimd.tensor_scalar(cum_mid[0:QB, :], cum_mid[0:QB, :], -1.0, None, ALU.add))
            link(nc.gpsimd.memset(first_half[QB:P, :], 0.0))
            link(nc.gpsimd.memset(second_half[QB:P, :], 1.0))
            blocks = head_block[:].rearrange("p (h d) -> p h d", d=DH)
            for t, tail in ((blocks, [[0, DH]]), (head_mask[:], [])):
                link(nc.gpsimd.affine_select(out=t, in_=t, compare_op=ALU.is_ge, fill=0.0, base=0,
                                             pattern=[[-DH, HH]] + tail, channel_multiplier=1))
                link(nc.gpsimd.affine_select(out=t, in_=t, compare_op=ALU.is_ge, fill=0.0, base=DH - 1,
                                             pattern=[[DH, HH]] + tail, channel_multiplier=-1))
            for b in range(2):
                link(nc.gpsimd.memset(block_ones[QB * b:QB * (b + 1), b, :], 1.0))
                band(block_band[QB * b:QB * (b + 1), b, :], 0, 0, P)
            band(chunk_band[:], 0, 0, KW)
            for e in range(E):
                link(nc.gpsimd.memset(expert_no[:, e:e + 1], float(e)))

        @block.vector
        def _(dve):
            nc.vector.memset(b_up[:], 0.0).then_inc(prep, 1)
            dve.wait_ge(prep_done, 1)
            for k in range(KD):
                nc.vector.tensor_copy(w_z[:, k, :], bank[k][:, 0:D])

        @block.tensor
        def _(pe):
            pe.wait_ge(w_sem, 16 * len(loads))
            for k in range(KD):
                mm = nc.tensor.matmul(bank[k][:, 0:D], gk1_t[:, k * P:(k + 1) * P], gk2[:], start=True, stop=True)
            mm.then_inc(prep_done, 1)

        @block.sync
        def _(sp):
            sp.wait_ge(prep, 1)
            for dst, src in loads:
                sp.dma_start(dst, src).then_inc(w_sem, 16)
            sp.wait_ge(w_sem, 16 * len(loads))

    tern, tern_pe, tern_act, tern_clear = sem("tern"), sem("tern_pe"), sem("tern_act"), sem("tern_clear")
    with nc.Block() as block:

        @block.vector
        def _(dve):
            done = [0]

            def link(ins):
                done[0] += 1
                ins.then_inc(tern, 1)
                dve.wait_ge(tern, done[0])

            for k in range(KD):
                link(nc.vector.tensor_copy(w_k2r[:, k], w_kv2[:, k, 0, :].rearrange("p (g d) -> p g d", g=2)
                                           .unsqueeze(2).broadcast_to([P, 2, HH, DH])))
            for nat, ter, scale, n, width in ((fc_nat, fc_ter, scale_fc, MT, D), (pj_nat, pj_ter, scale_pj, KD, HID)):
                link(nc.vector.tensor_reduce(scale[:], nat[:], AX.X, ALU.add, apply_absolute_value=True))
                link(nc.vector.tensor_scalar(scale[:], scale[:], 1.0 / width, 1e-5, ALU.mult, ALU.max))
                link(nc.vector.tensor_scalar(thr[:, 0, 0:n], scale[:], 0.5, None, ALU.mult))
                link(nc.vector.tensor_scalar(thr[:, 1, 0:n], scale[:], -0.5, None, ALU.mult))
                for m in range(n):
                    link(nc.vector.tensor_scalar(ter[:, m, :], nat[:, m, :], thr[:, 1, m:m + 1], None, ALU.is_lt))
                    link(nc.vector.scalar_tensor_tensor(ter[:, m, :], nat[:, m, :], thr[:, 0, m:m + 1],
                                                        ter[:, m, :], ALU.is_gt, ALU.subtract))
            link(nc.vector.reciprocal(rscale[:], scale_fc[:]))
            link(nc.vector.tensor_tensor(u_nat[:], u_nat[:], rscale[:].unsqueeze(2).broadcast_to([P, MT, RANK]),
                                         ALU.mult))
            link(nc.vector.tensor_copy(u_hi[:], u_nat[:]))
            link(nc.vector.tensor_tensor(u_lo[:], u_nat[:], u_hi[:].bitcast(F32), ALU.subtract))
            for r in (0, 2):
                link(nc.vector.tensor_copy(u_st[:, :, 32 * r:32 * r + RANK], u_hi[:].bitcast(F32)))
                link(nc.vector.tensor_copy(u_st[:, :, 32 * r + 32:32 * r + 32 + RANK], u_lo[:]))
            dve.wait_ge(tern_pe, 1)
            for k in range(KD):
                for r in range(4):
                    link(nc.vector.tensor_scalar(w_low[:, k, 32 * r:32 * r + RANK], bank[k][:, 0:RANK],
                                                 ffn_gate[:], None, ALU.mult))

        n_ternary = 2 + 4 + 2 * MT + 4 + 2 * KD + 4 + 4

        @block.tensor
        def _(pe):
            for k in range(KD):
                mm = nc.tensor.matmul(bank[k][:, 0:RANK], v_nat[:, k * P:(k + 1) * P], fb_t[:], start=True,
                                      stop=True)
            mm.then_inc(tern_pe, 1)
            pe.wait_ge(tern, n_ternary)
            n = 0

            def turn(parts):
                nonlocal n
                if n >= 4:
                    pe.wait_ge(tern_act, n - 3)
                for j, part in enumerate(parts):
                    mm = nc.tensor.transpose(bank[2 + n % 4][:, j * P:(j + 1) * P], part, ident[:])
                mm.then_inc(tern_pe, 1)
                n += 1

            for k in range(KD):
                for m in range(0, MT, 4):
                    turn([fc_ter[:, m + j, k * P:(k + 1) * P] for j in range(4)])
            for m in range(0, MT, 2):
                turn([pj_ter[:, j % 2, (m + j // 2) * P:(m + j // 2 + 1) * P] for j in range(4)])
            for m in range(0, MT, 4):
                turn([u_st[:, m + j, :] for j in range(4)])

        @block.scalar
        def _(act):
            targets = [fc_t[:, k, m * P:(m + 4) * P] for k in range(KD) for m in range(0, MT, 4)]
            targets += [pj_t[:, m:m + 2, :].rearrange("p m d -> p (m d)") for m in range(0, MT, 2)]
            targets += [u_t[:, m * P:(m + 4) * P] for m in range(0, MT, 4)]
            for n, target in enumerate(targets):
                act.wait_ge(tern_pe, n + 2)
                nc.scalar.copy(target, bank[2 + n % 4][:]).then_inc(tern_act, 1)

        @block.gpsimd
        def _(pool):
            pool.wait_ge(tern_act, 10)
            nc.gpsimd.memset(gates[:], 0.0).then_inc(tern_clear, 1)

    names = ("stats_ok veps_ok rstd_ok xn_ok xtp_ok xt_ok zp_ok zb_ok zabs_ok zexp_ok zln_ok gk_ok lg_ok lgc_ok "
             "gsel gexp_ok gates_ok qkp_ok qk_ok vg_ok kp_ok hp_ok hb_ok tg_ok sg_ok hg_ok ktok_ok qx_ok at_ok am_ok "
             "cum_ok re_ok din_ok dout_ok dst_ok vt_ok smid_ok end_ok ds_ok ssum_ok state_ok ot_ok ots_ok otok_ok "
             "o1_ok ost_ok ove_ok ors_ok onorm_ok ogam_ok obet_ok y_ok ytp_ok yt_ok s_ok hgtp_ok hgt_ok gtp_ok gt_ok "
             "f_ok tf_ok f1_ok f2_ok x_ok out_sem "
             "st2 ve2 rs2 xn2_ok xt2p_ok xt2_ok qk2p_ok qk2_ok kbf_ok v2p_ok v2_ok qx2_ok qxb_ok sc_ok max_ok dmax_ok "
             "stp_ok pr_ok pv_ok rden_ok o2_ok o2tp_ok o2t_ok s2p_ok s2_ok xh_ok xl_ok tp_ok thi_ok tst_ok h2p_ok "
             "relu_ok sq_ok sqh_ok sql_ok pj_ok ft_ok ftp_ok tf2_ok f3_ok f4_ok y2_ok").split()
    s = {n: sem(n) for n in names}
    x_in = [sem(f"x_in{c}") for c in range(NC)]
    first, last = s[names[0]].num, x_in[-1].num

    with nc.Fori(0, n_seq) as seq:
        with nc.Block() as block:

            @block.sync
            def _(sp):
                for c in range(NC):
                    sp.dma_start(x[:, c, :], x_dram[bass.ds(seq * NC + c, 1), :, :]
                                 .rearrange("o p d -> (o p) d")).then_inc(x_in[c], 16)
                for c in range(NC):
                    sp.wait_ge(s["y2_ok"], c + 1)
                    sp.dma_start(out_dram[bass.ds(seq * NC + c, 1), :, :].rearrange("o p d -> (o p) d"),
                                 x[:, c, :]).then_inc(s["out_sem"], 16)
                sp.wait_ge(s["out_sem"], 16 * NC)

            @block.gpsimd
            def _(pool):
                pool.wait_ge(s["stats_ok"], 2 * NC)
                nc.gpsimd.tensor_scalar(veps[:], moments[:, :, 1], EPS, None, ALU.add).then_inc(s["veps_ok"], 1)
                pool.wait_ge(s["veps_ok"], 1)
                nc.gpsimd.tensor_tensor(rstd[:], veps[:], minus_half[:], ALU.pow).then_inc(s["rstd_ok"], 1)
                for c in range(NC):
                    if c == 0:
                        pool.wait_ge(s["qk_ok"], 8)
                    else:
                        pool.wait_ge(s["at_ok"], 4 * c)
                    for half in range(2):
                        nc.gpsimd.tensor_tensor(
                            qx[:, half * HH:(half + 1) * HH, :],
                            qt[:, half:half + 1, c * P:(c + 1) * P].broadcast_to([P, HH, P]),
                            head_mask[:].unsqueeze(2).broadcast_to([P, HH, P]), ALU.mult).then_inc(s["qx_ok"], 1)
                    pool.wait_ge(s["dst_ok"], c + 1)
                    if c:
                        pool.wait_ge(s["state_ok"], c)
                    nc.gpsimd.tensor_tensor(
                        end_mask[:], decay_state[:, 1, :].rearrange("p (h f) -> p h f", h=2),
                        head_block[:].unsqueeze(1).broadcast_to([P, 2, P]), ALU.mult).then_inc(s["end_ok"], 1)
                    pool.wait_ge(s["ost_ok"], 2 * c + 2)
                    nc.gpsimd.tensor_scalar(o_veps[:], o_mom[:, 1:2], EPS, None, ALU.add).then_inc(s["ove_ok"], 1)
                    pool.wait_ge(s["ove_ok"], c + 1)
                    nc.gpsimd.tensor_tensor(o_rstd[:], o_veps[:], minus_half[:, 0:1], ALU.pow)\
                      .then_inc(s["ors_ok"], 1)
                    pool.wait_ge(s["onorm_ok"], c + 1)
                    nc.gpsimd.tensor_tensor(o_gam[:], o_norm[:], bc_gamma[:], ALU.mult).then_inc(s["ogam_ok"], 1)
                    pool.wait_ge(s["ogam_ok"], c + 1)
                    if c:
                        pool.wait_ge(s["y_ok"], c)
                    nc.gpsimd.tensor_tensor(o_bet[:], o_gam[:], bc_beta[:], ALU.add).then_inc(s["obet_ok"], 1)

                pool.wait_ge(s["st2"], 2 * NC)
                nc.gpsimd.tensor_scalar(veps[:], moments[:, :, 1], EPS, None, ALU.add).then_inc(s["ve2"], 1)
                pool.wait_ge(s["ve2"], 1)
                nc.gpsimd.tensor_tensor(rstd[:], veps[:], minus_half[:], ALU.pow).then_inc(s["rs2"], 1)
                for c in range(NC):
                    if c == 0:
                        pool.wait_ge(s["qk2_ok"], 8)
                    else:
                        pool.wait_ge(s["stp_ok"], 4 * c)
                    for half in range(2):
                        nc.gpsimd.tensor_tensor(
                            qx[:, half * HH:(half + 1) * HH, :],
                            q2[:, half:half + 1, c * P:(c + 1) * P].broadcast_to([P, HH, P]),
                            head_mask[:].unsqueeze(2).broadcast_to([P, HH, P]), ALU.mult).then_inc(s["qx2_ok"], 1)
                for g in range(NG):
                    pool.wait_ge(s["xh_ok"], g + 1)
                    if g:
                        pool.wait_ge(s["h2p_ok"], MT * g)
                    nc.gpsimd.tensor_tensor(xl[:], xt2[:, :, HALF + g * 512:HALF + (g + 1) * 512],
                                            xh[:].bitcast(F32), ALU.subtract).then_inc(s["xl_ok"], 1)
                    for m in range(MT):
                        n = g * MT + m
                        pool.wait_ge(s["relu_ok"], n + 1)
                        if n >= 2:
                            pool.wait_ge(s["sql_ok"], n - 1)
                        nc.gpsimd.tensor_tensor(sq[:, n % 2, :], relu[:, n % 2, :], relu[:, n % 2, :], ALU.mult)\
                          .then_inc(s["sq_ok"], 1)

            @block.scalar
            def _(act):
                for c in range(NC):
                    act.wait_ge(s["xtp_ok"], c + 1)
                    nc.scalar.copy(xt[:, :, c * P:(c + 1) * P],
                                   bank[5 + c % 2][:, 0:D].rearrange("p (k t) -> p k t", k=KD))\
                      .then_inc(s["xt_ok"], 1)
                for i in range(NC // 2):
                    act.wait_ge(s["zb_ok"], i + 1)
                    if i:
                        act.wait_ge(s["gk_ok"], i)
                    nc.scalar.activation(zact[:], zb[:, 2 * i:2 * i + 2, :], ACT.Abs).then_inc(s["zabs_ok"], 1)
                    act.wait_ge(s["zabs_ok"], i + 1)
                    nc.scalar.activation(zact[:], zact[:], ACT.Exp, scale=-1.0).then_inc(s["zexp_ok"], 1)
                    act.wait_ge(s["zexp_ok"], i + 1)
                    nc.scalar.activation(zact[:], zact[:], ACT.Ln, bias=1.0).then_inc(s["zln_ok"], 1)
                act.wait_ge(s["gsel"], 1)
                nc.scalar.activation(gexp[:], gdiff[:], ACT.Exp).then_inc(s["gexp_ok"], 1)
                for n in range(8):
                    g, which, half = n // 4, n // 2 % 2, n % 2
                    act.wait_ge(s["qkp_ok"], n + 1)
                    nc.scalar.copy((kt if which else qt)[:, half, g * 512:(g + 1) * 512], bank[4 + n % 4][:])\
                      .then_inc(s["qk_ok"], 1)
                for b in range(2):
                    act.wait_ge(s["gtp_ok"], b + 1)
                    nc.scalar.copy(gates_t[:, 4 * b:4 * b + 4, :], bank[2 + b][:].rearrange("p (c t) -> p c t", t=P))\
                      .then_inc(s["gt_ok"], 1)
                for c in range(NC):
                    act.wait_ge(s["vg_ok"], c + 1)
                    if c:
                        act.wait_ge(s["sg_ok"], c)
                    nc.scalar.activation(tanh_g[:], bank[0][:, D:2 * D], ACT.Tanh, scale=0.5)\
                      .then_inc(s["tg_ok"], 1)
                    act.wait_ge(s["kp_ok"], c + 1)
                    if c:
                        act.wait_ge(s["ds_ok"], c)
                    nc.scalar.copy(ktok[:], bank[1][:, 0:D]).then_inc(s["ktok_ok"], 1)
                    if c:
                        act.wait_ge(s["ytp_ok"], c)
                        nc.scalar.copy(yt[:], bank[7][:, 0:D].rearrange("p (k t) -> p k t", k=KD))\
                          .then_inc(s["yt_ok"], 1)
                    act.wait_ge(s["cum_ok"], c + 1)
                    if c:
                        act.wait_ge(s["vt_ok"], c)
                    nc.scalar.activation(decay_in[:], bank[1][:, 0:D], ACT.Exp, scale=-1.0 / 16)\
                      .then_inc(s["din_ok"], 1)
                    if c:
                        act.wait_ge(s["o1_ok"], c)
                    nc.scalar.activation(decay_out[:], bank[1][:, 0:D], ACT.Exp, scale=1.0 / 16)\
                      .then_inc(s["dout_ok"], 1)
                    if c:
                        act.wait_ge(s["end_ok"], c)
                        act.wait_ge(s["smid_ok"], c)
                    nc.scalar.activation(decay_state[:], bank[4][:].rearrange("p (a f) -> p a f", a=2), ACT.Exp,
                                         scale=1.0 / 16).then_inc(s["dst_ok"], 1)
                    act.wait_ge(s["hgtp_ok"], c + 1)
                    nc.scalar.copy(hgt[:], bank[2][:].rearrange("p (j t) -> p j t", t=P)).then_inc(s["hgt_ok"], 1)
                    act.wait_ge(s["ot_ok"], c + 1)
                    nc.scalar.copy(ot[:], bank[7][:, 0:D].rearrange("p (k t) -> p k t", k=KD))\
                      .then_inc(s["ots_ok"], 1)
                    act.wait_ge(s["f_ok"], c + 1)
                    if c:
                        act.wait_ge(s["f1_ok"], c)
                    nc.scalar.activation(tanh_f[:], bank[3][:, 0:D], ACT.Tanh, scale=0.25).then_inc(s["tf_ok"], 1)
                act.wait_ge(s["ytp_ok"], NC)
                nc.scalar.copy(yt[:], bank[7][:, 0:D].rearrange("p (k t) -> p k t", k=KD)).then_inc(s["yt_ok"], 1)

                for c in range(NC):
                    act.wait_ge(s["xt2p_ok"], c + 1)
                    nc.scalar.copy(xt2[:, :, HALF + c * P:HALF + (c + 1) * P],
                                   bank[5 + c % 2][:, 0:D].rearrange("p (k t) -> p k t", k=KD))\
                      .then_inc(s["xt2_ok"], 1)
                for n in range(8):
                    g, which, half = n // 4, n // 2 % 2, n % 2
                    act.wait_ge(s["qk2p_ok"], n + 1)
                    if which:
                        dst, bias = k2[:, half, HALF + g * 512:HALF + (g + 1) * 512], b_k2
                    else:
                        dst, bias = q2[:, half, g * 512:(g + 1) * 512], b_q2
                    nc.scalar.activation(dst, bank[1 + n % 4][:], ACT.Identity, bias=bias[:, half:half + 1])\
                      .then_inc(s["qk2_ok"], 1)

                def attention_turned(c):
                    act.wait_ge(s["o2tp_ok"], c + 1)
                    if c:
                        act.wait_ge(s["s2p_ok"], c)
                    nc.scalar.copy(o2t[:], bank[0][:, 0:D].rearrange("p (k t) -> p k t", k=KD))\
                      .then_inc(s["o2t_ok"], 1)

                for c in range(NC):
                    if c:
                        attention_turned(c - 1)
                    for u in range(4):
                        n = 4 * c + u
                        act.wait_ge(s["stp_ok"], n + 1)
                        if n >= 2:
                            act.wait_ge(s["pv_ok"], n - 1)
                        nc.scalar.activation(pr[:, n % 2], bank[5 + n % 2][:].rearrange("p (h q) -> p h q", q=QB),
                                             ACT.Exp).then_inc(s["pr_ok"], 1)
                attention_turned(NC - 1)
                for g in range(NG):
                    for m in range(MT + 1):
                        n = g * MT + m
                        if m < MT:
                            act.wait_ge(s["h2p_ok"], n + 1)
                            if n >= 2:
                                act.wait_ge(s["sq_ok"], n - 1)
                            nc.scalar.activation(relu[:, n % 2, :], bank[1 + n % 3][:], ACT.Relu,
                                                 scale=scale_fc[:, m:m + 1]).then_inc(s["relu_ok"], 1)
                        if m:
                            act.wait_ge(s["sq_ok"], n)
                            if n >= 3:
                                act.wait_ge(s["pj_ok"], n - 2)
                            nc.scalar.copy(sq_hi[:, (n - 1) % 2, :], sq[:, (n - 1) % 2, :]).then_inc(s["sqh_ok"], 1)
                    act.wait_ge(s["pj_ok"], (g + 1) * MT)
                    if g:
                        act.wait_ge(s["ftp_ok"], 4 * g)
                    for o in range(KD):
                        nc.scalar.activation(ft[:, o, :], bank[5 + o][:], ACT.Identity, scale=scale_pj[:, o:o + 1])\
                          .then_inc(s["ft_ok"], 1)
                    for j in range(4):
                        c = 4 * g + j
                        act.wait_ge(s["ftp_ok"], c + 1)
                        if c:
                            act.wait_ge(s["f3_ok"], c)
                        nc.scalar.activation(tanh_f[:], bank[7 if c % 2 else 4][:, 0:D], ACT.Tanh, scale=0.5)\
                          .then_inc(s["tf2_ok"], 1)

            @block.vector
            def _(dve):
                for c in range(NC):
                    dve.wait_ge(x_in[c], 16)
                    nc.vector.bn_stats(stats[:, c, :], x[:, c, :]).then_inc(s["stats_ok"], 1)
                dve.wait_ge(s["stats_ok"], NC)
                for c in range(NC):
                    nc.vector.bn_aggr(moments[:, c, :], stats[:, c, :]).then_inc(s["stats_ok"], 1)
                dve.wait_ge(s["rstd_ok"], 1)
                for c in range(NC):
                    nc.vector.tensor_scalar(xn[:, c, :], x[:, c, :], moments[:, c, 0:1], rstd[:, c:c + 1],
                                            ALU.subtract, ALU.mult).then_inc(s["xn_ok"], 1)
                for i in range(NC // 2):
                    dve.wait_ge(s["zp_ok"], i + 1)
                    nc.vector.tensor_tensor(zb[:, 2 * i:2 * i + 2, :],
                                            bank[i % 2][:].rearrange("p (a f) -> p a f", a=2),
                                            bc_gk[:].unsqueeze(1).broadcast_to([P, 2, D]), ALU.add)\
                      .then_inc(s["zb_ok"], 1)
                for i in range(NC // 2):
                    dve.wait_ge(s["zln_ok"], i + 1)
                    nc.vector.scalar_tensor_tensor(gk[:, 2 * i:2 * i + 2, :], zb[:, 2 * i:2 * i + 2, :], 0.0,
                                                   zact[:], ALU.min, ALU.subtract).then_inc(s["gk_ok"], 1)

                dve.wait_ge(s["lg_ok"], 1)
                nc.vector.tensor_copy(logits[:], bank[3][:, 0:NC * E].rearrange("p (c e) -> p c e", e=E))\
                  .then_inc(s["lgc_ok"], 1)
                dve.wait_ge(s["lgc_ok"], 1)
                for c in range(NC):
                    nc.vector.max(top[:, c, :], logits[:, c, :]).then_inc(s["lgc_ok"], 1)
                dve.wait_ge(s["lgc_ok"], 1 + NC)
                for c in range(NC):
                    nc.vector.max_index(top_i[:, c, :], top[:, c, :], logits[:, c, :]).then_inc(s["lgc_ok"], 1)
                nc.vector.tensor_sub(gdiff[:], top[:, :, 1], top[:, :, 0]).then_inc(s["gsel"], 1)
                dve.wait_ge(s["lgc_ok"], 1 + 2 * NC)
                nc.vector.tensor_copy(top_f[:], top_i[:, :, 0:2]).then_inc(s["gsel"], 1)
                dve.wait_ge(s["gexp_ok"], 1)
                nc.vector.tensor_scalar(gden[:], gexp[:], 1.0, None, ALU.add).then_inc(s["gsel"], 1)
                dve.wait_ge(s["gsel"], 3)
                nc.vector.reciprocal(g_top[:, 0, :], gden[:]).then_inc(s["gsel"], 1)
                dve.wait_ge(s["gsel"], 4)
                nc.vector.tensor_tensor(g_top[:, 1, :], gexp[:], g_top[:, 0, :], ALU.mult).then_inc(s["gsel"], 1)
                for r in range(2):
                    nc.vector.tensor_tensor(g_hit[:, r], top_f[:, :, r:r + 1].broadcast_to([P, NC, E]),
                                            expert_no[:].unsqueeze(1).broadcast_to([P, NC, E]), ALU.is_equal)\
                      .then_inc(s["gsel"], 1)
                dve.wait_ge(s["gsel"], 7)
                for r in range(2):
                    nc.vector.tensor_tensor(g_hit[:, r], g_hit[:, r],
                                            g_top[:, r, :].unsqueeze(2).broadcast_to([P, NC, E]), ALU.mult)\
                      .then_inc(s["gsel"], 1)
                dve.wait_ge(s["gsel"], 9)
                nc.vector.tensor_add(gates[:, :, 0:E], g_hit[:, 0], g_hit[:, 1]).then_inc(s["gates_ok"], 1)
                dve.wait_ge(s["gates_ok"], 1)

                def finish_chunk(c):
                    dve.wait_ge(s["s_ok"], c + 1)
                    dve.wait_ge(s["f1_ok"], c + 1)
                    nc.vector.scalar_tensor_tensor(sf[:], f_gate[:], 0.125, bank[3][:, D:2 * D], ALU.mult,
                                                   ALU.mult).then_inc(s["f2_ok"], 1)
                    dve.wait_ge(s["f2_ok"], c + 1)
                    nc.vector.tensor_add(x[:, c, :], x[:, c, :], sf[:]).then_inc(s["x_ok"], 1)
                    dve.wait_ge(s["x_ok"], c + 1)
                    nc.vector.bn_stats(stats[:, c, :], x[:, c, :]).then_inc(s["st2"], 1)
                    dve.wait_ge(s["st2"], 2 * c + 1)
                    nc.vector.bn_aggr(moments[:, c, :], stats[:, c, :]).then_inc(s["st2"], 1)

                for c in range(NC):
                    dve.wait_ge(s["hp_ok"], c + 1)
                    nc.vector.tensor_add(hb[:], bank[2][:], bc_down[:]).then_inc(s["hb_ok"], 1)
                    dve.wait_ge(s["tg_ok"], c + 1)
                    if c:
                        dve.wait_ge(s["y_ok"], c)
                    nc.vector.scalar_tensor_tensor(silu_g[:], tanh_g[:], 1.0, bank[0][:, D:2 * D], ALU.add,
                                                   ALU.mult).then_inc(s["sg_ok"], 1)
                    if c:
                        finish_chunk(c - 1)
                        dve.wait_ge(s["hgtp_ok"], c)
                    dve.wait_ge(s["hb_ok"], c + 1)
                    nc.vector.scalar_tensor_tensor(
                        hg[:].rearrange("p (e b) -> p e b", e=E), hb[:].rearrange("p (e b) -> p e b", e=E), 0.0,
                        gates[:, c, 0:E].unsqueeze(2).broadcast_to([P, E, BN]), ALU.max, ALU.mult)\
                      .then_inc(s["hg_ok"], 1)
                    for j in range(4):
                        dve.wait_ge(s["at_ok"], 4 * c + j + 1)
                        if c and j == 0:
                            dve.wait_ge(s["ot_ok"], c)
                        nc.vector.tensor_tensor(am[:, 4 * j:4 * j + 4, :],
                                                bank[5 + j % 2][:].rearrange("p (h t) -> p h t", t=P),
                                                causal[:].unsqueeze(1).broadcast_to([P, 4, P]), ALU.mult)\
                          .then_inc(s["am_ok"], 1)
                    dve.wait_ge(s["din_ok"], c + 1)
                    if c:
                        dve.wait_ge(s["ds_ok"], c)
                    nc.vector.tensor_tensor(
                        vt[:, :, 0:4:3, :], bank[0][:, 0:D].rearrange("p (j e d) -> p j e d", e=2, d=DH),
                        decay_in[:].rearrange("p (j e d) -> p j e d", e=2, d=DH), ALU.mult)\
                      .then_inc(s["vt_ok"], 1)
                    dve.wait_ge(s["dst_ok"], c + 1)
                    if c:
                        dve.wait_ge(s["state_ok"], c)
                    nc.vector.tensor_tensor(state_mid[:], state[:],
                                            decay_state[:, 0, :].rearrange("p (h f) -> p h f", h=2), ALU.mult)\
                      .then_inc(s["smid_ok"], 1)
                    dve.wait_ge(s["ds_ok"], c + 1)
                    dve.wait_ge(s["smid_ok"], c + 1)
                    nc.vector.tensor_tensor(state_sum[:], bank[0][:, 0:D].rearrange("p (h f) -> p h f", h=2),
                                            state_mid[:], ALU.add).then_inc(s["ssum_ok"], 1)
                    dve.wait_ge(s["ssum_ok"], c + 1)
                    dve.wait_ge(s["end_ok"], c + 1)
                    nc.vector.tensor_tensor(state[:], state_sum[:], end_mask[:], ALU.mult)\
                      .then_inc(s["state_ok"], 1)
                    dve.wait_ge(s["otok_ok"], c + 1)
                    dve.wait_ge(s["dout_ok"], c + 1)
                    nc.vector.tensor_tensor(o_tok[:], bank[7][:, D:2 * D], decay_out[:], ALU.mult)\
                      .then_inc(s["o1_ok"], 1)
                    dve.wait_ge(s["o1_ok"], c + 1)
                    nc.vector.bn_stats(o_stats[:], o_tok[:]).then_inc(s["ost_ok"], 1)
                    dve.wait_ge(s["ost_ok"], 2 * c + 1)
                    nc.vector.bn_aggr(o_mom[:], o_stats[:]).then_inc(s["ost_ok"], 1)
                    dve.wait_ge(s["tf_ok"], c + 1)
                    nc.vector.scalar_tensor_tensor(f_gate[:], tanh_f[:], 1.0, bank[3][:, 0:D], ALU.add, ALU.mult)\
                      .then_inc(s["f1_ok"], 1)
                    dve.wait_ge(s["ors_ok"], c + 1)
                    nc.vector.tensor_scalar(o_norm[:], o_tok[:], o_mom[:, 0:1], o_rstd[:], ALU.subtract, ALU.mult)\
                      .then_inc(s["onorm_ok"], 1)
                    dve.wait_ge(s["obet_ok"], c + 1)
                    if c:
                        dve.wait_ge(s["ytp_ok"], c)
                    nc.vector.tensor_tensor(y_tok[:], o_bet[:], silu_g[:], ALU.mult).then_inc(s["y_ok"], 1)
                finish_chunk(NC - 1)
                dve.wait_ge(s["state_ok"], NC)
                nc.vector.memset(state[:], 0.0).then_inc(s["state_ok"], 1)

                dve.wait_ge(s["rs2"], 1)
                for c in range(NC):
                    nc.vector.tensor_scalar(xn[:, c, :], x[:, c, :], moments[:, c, 0:1], rstd[:, c:c + 1],
                                            ALU.subtract, ALU.mult).then_inc(s["xn2_ok"], 1)
                dve.wait_ge(s["v2p_ok"], 1)
                for g in range(2):
                    nc.vector.tensor_tensor(
                        v2[:, :, g, 0:DH],
                        bank[0][:].rearrange("p (w g d) -> p w g d", g=2, d=DH)[:, :, g, :],
                        bc_v2[:, g * DH:(g + 1) * DH].unsqueeze(1).broadcast_to([P, 2 * NC, DH]), ALU.add)\
                      .then_inc(s["v2_ok"], 1)
                dve.wait_ge(s["v2_ok"], 2)
                nc.vector.memset(v2[0:HALF, 0, :, 0:DH], 0.0).then_inc(s["v2_ok"], 1)
                nc.vector.memset(v2[P - HALF:P, 2 * NC - 1, :, 0:DH], 0.0).then_inc(s["v2_ok"], 1)
                dve.wait_ge(s["qk2_ok"], 8)
                nc.vector.tensor_copy(k2_bf[:, :, HALF:HALF + S], k2[:, :, HALF:HALF + S]).then_inc(s["kbf_ok"], 1)

                def attention_out(c):
                    dve.wait_ge(s["pv_ok"], 4 * c + 4)
                    o_bank = bank[7][:, 0:H * DV].rearrange("p (h d) -> p h d", d=DV)
                    nc.vector.reciprocal(rden[:], o_bank[:, :, DH]).then_inc(s["rden_ok"], 1)
                    dve.wait_ge(s["rden_ok"], c + 1)
                    if c:
                        dve.wait_ge(s["o2tp_ok"], c)
                    nc.vector.tensor_tensor(o2[:].rearrange("p (h d) -> p h d", d=DH), o_bank[:, :, 0:DH],
                                            rden[:].unsqueeze(2).broadcast_to([P, H, DH]), ALU.mult)\
                      .then_inc(s["o2_ok"], 1)

                def attention_bias(c):
                    dve.wait_ge(s["s2p_ok"], c + 1)
                    nc.vector.tensor_tensor(attn2[:, c, :], bank[0][:, D:2 * D], bc_o2[:], ALU.add)\
                      .then_inc(s["s2_ok"], 1)

                for c in range(NC):
                    for half in range(2):
                        dve.wait_ge(s["qx2_ok"], 2 * c + half + 1)
                        if c:
                            dve.wait_ge(s["sc_ok"], 8 * c)
                        nc.vector.tensor_copy(qx_bf[:, half * HH:(half + 1) * HH, :],
                                              qx[:, half * HH:(half + 1) * HH, :]).then_inc(s["qxb_ok"], 1)
                    if c:
                        attention_out(c - 1)
                    for r in range(HH):
                        dve.wait_ge(s["sc_ok"], 8 * c + r + 1)
                        if c and r == 0:
                            dve.wait_ge(s["dmax_ok"], 2 * c)
                        nc.vector.tensor_reduce(neg_max[:, 2 * r:2 * r + 2],
                                                bank[1 + r % 4][:, 0:2 * KW].rearrange("p (h k) -> p h k", k=KW),
                                                AX.X, ALU.max, negate=True).then_inc(s["max_ok"], 1)
                        if r % 4 == 3:
                            half = r // 4
                            dve.wait_ge(s["max_ok"], 8 * c + r + 1)
                            if c:
                                dve.wait_ge(s["stp_ok"], 4 * c - 2 + 2 * half)
                            nc.vector.tensor_tensor(
                                diag_max[:, half * HH:(half + 1) * HH, :],
                                same_q[:].unsqueeze(1).broadcast_to([P, HH, QB]),
                                neg_max[:, half * HH:(half + 1) * HH].unsqueeze(2).broadcast_to([P, HH, QB]),
                                ALU.mult).then_inc(s["dmax_ok"], 1)
                    if c:
                        attention_bias(c - 1)
                attention_out(NC - 1)
                attention_bias(NC - 1)
                for g in range(NG):
                    cols = slice(HALF + g * 512, HALF + (g + 1) * 512)
                    if g:
                        dve.wait_ge(s["h2p_ok"], MT * g)
                        dve.wait_ge(s["xl_ok"], g)
                    nc.vector.tensor_copy(xh[:], xt2[:, :, cols]).then_inc(s["xh_ok"], 1)
                    dve.wait_ge(s["tp_ok"], g + 1)
                    nc.vector.tensor_copy(t_hi[:], bank[0][:]).then_inc(s["thi_ok"], 1)
                    nc.vector.tensor_copy(t_st[0:64, :], bank[0][0:64, :]).then_inc(s["tst_ok"], 1)
                    dve.wait_ge(s["thi_ok"], g + 1)
                    nc.vector.tensor_tensor(t_st[64:128, :], bank[0][64:128, :], t_hi[64:128, :].bitcast(F32),
                                            ALU.subtract).then_inc(s["tst_ok"], 1)
                    for m in range(MT):
                        n = g * MT + m
                        dve.wait_ge(s["sqh_ok"], n + 1)
                        if n >= 2:
                            dve.wait_ge(s["pj_ok"], n - 1)
                        nc.vector.tensor_tensor(sq_lo[:, n % 2, :], sq[:, n % 2, :],
                                                sq_hi[:, n % 2, :].bitcast(F32), ALU.subtract)\
                          .then_inc(s["sql_ok"], 1)
                    for j in range(4):
                        c = 4 * g + j
                        dve.wait_ge(s["tf2_ok"], c + 1)
                        if c:
                            dve.wait_ge(s["f4_ok"], c)
                        nc.vector.scalar_tensor_tensor(f_gate[:], tanh_f[:], 1.0, bank[7 if c % 2 else 4][:, 0:D],
                                                       ALU.add, ALU.mult).then_inc(s["f3_ok"], 1)
                        dve.wait_ge(s["f3_ok"], c + 1)
                        dve.wait_ge(s["y2_ok"], c) if c else None
                        nc.vector.scalar_tensor_tensor(sf[:], f_gate[:], 0.5, attn2[:, c, :], ALU.mult, ALU.mult)\
                          .then_inc(s["f4_ok"], 1)
                        dve.wait_ge(s["f4_ok"], c + 1)
                        nc.vector.tensor_add(x[:, c, :], x[:, c, :], sf[:]).then_inc(s["y2_ok"], 1)

            @block.tensor
            def _(pe):
                for c in range(NC):
                    pe.wait_ge(s["xn_ok"], c + 1)
                    if c >= 2:
                        pe.wait_ge(s["xt_ok"], c - 1)
                    for k in range(KD):
                        mm = nc.tensor.transpose(bank[5 + c % 2][:, k * P:(k + 1) * P],
                                                 xn[:, c, k * P:(k + 1) * P], ident[:])
                    mm.then_inc(s["xtp_ok"], 1)

                def token_major(dst, c, w):
                    for k in range(KD):
                        mm = nc.tensor.matmul(dst, xt[:, k, c * P:(c + 1) * P], w[:, k, :], start=(k == 0),
                                              stop=(k == KD - 1))
                    return mm

                for i in range(NC // 2):
                    pe.wait_ge(s["xt_ok"], 2 * i + 2)
                    if i >= 2:
                        pe.wait_ge(s["zb_ok"], i - 1)
                    for b in range(2):
                        mm = token_major(bank[i % 2][:, b * D:(b + 1) * D], 2 * i + b, w_z)
                    mm.then_inc(s["zp_ok"], 1)
                for c in range(NC):
                    mm = token_major(bank[3][:, c * E:(c + 1) * E], c, w_gate)
                mm.then_inc(s["lg_ok"], 1)
                for n in range(8):
                    g, which, half = n // 4, n // 2 % 2, n % 2
                    if n >= 4:
                        pe.wait_ge(s["qk_ok"], n - 3)
                    w = w_k if which else w_q
                    for k in range(KD):
                        mm = nc.tensor.matmul(bank[4 + n % 4][:], w[:, k, half * P:(half + 1) * P],
                                              xt[:, k, g * 512:(g + 1) * 512], start=(k == 0), stop=(k == KD - 1))
                    mm.then_inc(s["qkp_ok"], 1)

                pe.wait_ge(s["gates_ok"], 1)
                for b in range(2):
                    for j in range(4):
                        mm = nc.tensor.transpose(bank[2 + b][:, j * P:(j + 1) * P], gates[:, 4 * b + j, :], ident[:])
                    mm.then_inc(s["gtp_ok"], 1)

                def output(c):
                    pe.wait_ge(s["y_ok"], c + 1)
                    for k in range(KD):
                        mm = nc.tensor.transpose(bank[7][:, k * P:(k + 1) * P], y_tok[:, k * P:(k + 1) * P],
                                                 ident[:])
                    mm.then_inc(s["ytp_ok"], 1)
                    pe.wait_ge(s["yt_ok"], c + 1)
                    pe.wait_ge(s["f1_ok"], c + 1)
                    for k in range(KD):
                        mm = nc.tensor.matmul(bank[3][:, D:2 * D], yt[:, k, :], w_out[:, k, :], start=(k == 0),
                                              stop=(k == KD - 1))
                    mm.then_inc(s["s_ok"], 1)

                for c in range(NC):
                    if c == 0:
                        pe.wait_ge(s["zb_ok"], NC // 2)
                    else:
                        pe.wait_ge(s["state_ok"], c)
                    token_major(bank[0][:], c, w_vg).then_inc(s["vg_ok"], 1)
                    if c:
                        pe.wait_ge(s["dout_ok"], c)
                    token_major(bank[1][:, 0:D], c, w_k).then_inc(s["kp_ok"], 1)
                    if c == 0:
                        pe.wait_ge(s["gt_ok"], 1)
                    else:
                        pe.wait_ge(s["hgt_ok"], c)
                    token_major(bank[2][:], c, w_down).then_inc(s["hp_ok"], 1)
                    if c:
                        output(c - 1)
                    for j in range(4):
                        if j < 2:
                            if c == 0:
                                pe.wait_ge(s["qk_ok"], 8)
                        if 4 * c + j >= 2:
                            pe.wait_ge(s["am_ok"], 4 * c + j - 1)
                        half = j // 2
                        pe.wait_ge(s["qx_ok"], 2 * c + half + 1)
                        nc.tensor.matmul(bank[5 + j % 2][:], kt[:, half, c * P:(c + 1) * P],
                                         qx[:, 4 * j:4 * j + 4, :], start=True, stop=True).then_inc(s["at_ok"], 1)
                    pe.wait_ge(s["gk_ok"], c // 2 + 1)
                    pe.wait_ge(s["ktok_ok"], c + 1)
                    if c:
                        pe.wait_ge(s["dst_ok"], c)
                    nc.tensor.matmul(bank[1][:, 0:D], cum_mid[:], gk[:, c, :], start=True, stop=True)
                    nc.tensor.matmul(bank[4][:, 0:D], first_half[:], gk[:, c, :], start=True, stop=True)
                    nc.tensor.matmul(bank[4][:, D:2 * D], second_half[:], gk[:, c, :], start=True, stop=True)\
                      .then_inc(s["cum_ok"], 1)
                    pe.wait_ge(s["hg_ok"], c + 1)
                    for j in range(EB // P):
                        mm = nc.tensor.transpose(bank[2][:, j * P:(j + 1) * P], hg[:, j * P:(j + 1) * P], ident[:])
                    mm.then_inc(s["hgtp_ok"], 1)
                    pe.wait_ge(s["vt_ok"], c + 1)
                    pe.wait_ge(s["smid_ok"], c + 1)
                    if c:
                        pe.wait_ge(s["o1_ok"], c)
                    for half in range(2):
                        nc.tensor.matmul(bank[7][:, half * P:(half + 1) * P], state_mid[:, half, :],
                                         qt[:, half, c * P:(c + 1) * P], start=True, stop=False,
                                         skip_group_check=True)
                        for h in range(HH):
                            pe.wait_ge(s["am_ok"], 4 * c + 2 * half + h // 4 + 1)
                            r = 32 * (h // 2)
                            lhs = vt[:, half * 4 + h // 2, 2 * (h % 2):2 * (h % 2) + 2, :]
                            mm = nc.tensor.matmul(bank[7][r:r + 32, half * P:(half + 1) * P], lhs,
                                                  am[:, half * HH + h, :], start=False, stop=(h % 2 == 1),
                                                  skip_group_check=True)
                    mm.then_inc(s["ot_ok"], 1)
                    pe.wait_ge(s["ktok_ok"], c + 1)
                    pe.wait_ge(s["sg_ok"], c + 1)
                    for half in range(2):
                        mm = nc.tensor.matmul(bank[0][:, half * P:(half + 1) * P], ktok[:, half * P:(half + 1) * P],
                                              vt[:, half * 4:half * 4 + 4, 0:4:3, :], start=True, stop=True)
                    mm.then_inc(s["ds_ok"], 1)
                    pe.wait_ge(s["hgt_ok"], c + 1)
                    if c == 0:
                        pe.wait_ge(s["gt_ok"], 2)
                    else:
                        pe.wait_ge(s["f2_ok"], c)
                    for j in range(EB // P):
                        nc.tensor.matmul(bank[3][:, 0:D], hgt[:, j, :], w_up[:, j, :], start=(j == 0), stop=False)
                    nc.tensor.matmul(bank[3][:, 0:D], gates_t[:, c, :], b_up[:], start=False, stop=True)\
                      .then_inc(s["f_ok"], 1)
                    pe.wait_ge(s["ots_ok"], c + 1)
                    for k in range(KD):
                        mm = nc.tensor.transpose(bank[7][:, D + k * P:D + (k + 1) * P], ot[:, k, :], ident[:])
                    mm.then_inc(s["otok_ok"], 1)
                output(NC - 1)

                for c in range(NC):
                    pe.wait_ge(s["xn2_ok"], c + 1)
                    if c >= 2:
                        pe.wait_ge(s["xt2_ok"], c - 1)
                    for k in range(KD):
                        mm = nc.tensor.transpose(bank[5 + c % 2][:, k * P:(k + 1) * P],
                                                 xn[:, c, k * P:(k + 1) * P], ident[:])
                    mm.then_inc(s["xt2p_ok"], 1)
                for n in range(8):
                    g, which, half = n // 4, n // 2 % 2, n % 2
                    pe.wait_ge(s["xt2_ok"], 4 * g + 4)
                    if n >= 4:
                        pe.wait_ge(s["qk2_ok"], n - 3)
                    elif n == 2:
                        pe.wait_ge(s["f2_ok"], NC)
                    for k in range(KD):
                        w = w_k2r[:, k, half].rearrange("p r d -> p (r d)") if which \
                            else w_q2[:, k, half * P:(half + 1) * P]
                        mm = nc.tensor.matmul(bank[1 + n % 4][:], w,
                                              xt2[:, k, HALF + g * 512:HALF + (g + 1) * 512], start=(k == 0),
                                              stop=(k == KD - 1))
                    mm.then_inc(s["qk2p_ok"], 1)
                for w in range(2 * NC):
                    for k in range(KD):
                        mm = nc.tensor.matmul(bank[0][:, w * 2 * DH:(w + 1) * 2 * DH],
                                              xt2[:, k, w * QB:w * QB + P], w_kv2[:, k, 1, :], start=(k == 0),
                                              stop=(k == KD - 1))
                mm.then_inc(s["v2p_ok"], 1)

                def attention_project(c):
                    pe.wait_ge(s["o2_ok"], c + 1)
                    if c:
                        pe.wait_ge(s["s2_ok"], c)
                    for k in range(KD):
                        mm = nc.tensor.transpose(bank[0][:, k * P:(k + 1) * P], o2[:, k * P:(k + 1) * P], ident[:])
                    mm.then_inc(s["o2tp_ok"], 1)
                    pe.wait_ge(s["o2t_ok"], c + 1)
                    for k in range(KD):
                        mm = nc.tensor.matmul(bank[0][:, D:2 * D], o2t[:, k, :], w_o2[:, k, :], start=(k == 0),
                                              stop=(k == KD - 1))
                    mm.then_inc(s["s2p_ok"], 1)

                def values(n):
                    c, g, b = n // 4, n // 2 % 2, n % 2
                    pe.wait_ge(s["pr_ok"], n + 1)
                    for h in range(HH):
                        col = (g * HH + h) * DV
                        mm = nc.tensor.matmul(bank[7][b * QB:(b + 1) * QB, col:col + DV], pr[:, n % 2, h, :],
                                              v2[:, 2 * c + b, g, :], start=True, stop=True)
                    mm.then_inc(s["pv_ok"], 1)

                pe.wait_ge(s["kbf_ok"], 1)
                pe.wait_ge(s["v2_ok"], 4)
                for c in range(NC):
                    for r in range(HH):
                        n = 8 * c + r
                        if n >= 4:
                            pe.wait_ge(s["max_ok"], n - 3)
                        pe.wait_ge(s["qxb_ok"], 2 * c + r // 4 + 1)
                        nc.tensor.matmul(bank[1 + r % 4][:, 0:2 * KW], ident_bf[:],
                                         chunk_band[:].unsqueeze(1).broadcast_to([P, 2, KW]), start=True,
                                         stop=False, skip_group_check=True)
                        for j in range(2):
                            mm = nc.tensor.matmul(bank[1 + r % 4][:, j * KW:(j + 1) * KW], qx_bf[:, 2 * r + j, :],
                                                  k2_bf[:, r // 4, c * P:c * P + KW], start=False, stop=True,
                                                  skip_group_check=True)
                        mm.then_inc(s["sc_ok"], 1)
                    if c:
                        attention_project(c - 1)
                    for u in range(4):
                        n, g, b = 4 * c + u, u // 2, u % 2
                        if n >= 2:
                            pe.wait_ge(s["pr_ok"], n - 1)
                        pe.wait_ge(s["dmax_ok"], 2 * c + g + 1)
                        st = bank[5 + n % 2][:]
                        nc.tensor.matmul(st, block_band[:, b, :], same_q[:].unsqueeze(1).broadcast_to([P, HH, QB]),
                                         start=True, stop=False)
                        nc.tensor.matmul(st, block_ones[:, b, :], diag_max[:, g * HH:(g + 1) * HH, :], start=False,
                                         stop=False)
                        nc.tensor.matmul(st, k2[:, g, c * P + b * QB:c * P + b * QB + P],
                                         qx[:, g * HH:(g + 1) * HH, b * QB:(b + 1) * QB], start=False, stop=True)\
                          .then_inc(s["stp_ok"], 1)
                        if u:
                            values(n - 1)
                    values(4 * c + 3)
                attention_project(NC - 1)

                def project(n):
                    pe.wait_ge(s["sql_ok"], n + 1)
                    m = n % MT
                    for o in range(KD):
                        for part in (sq_hi, sq_lo):
                            mm = nc.tensor.matmul(bank[5 + o][:], pj_t[:, m, o * P:(o + 1) * P], part[:, n % 2, :],
                                                  start=(m == 0 and part is sq_hi),
                                                  stop=(m == MT - 1 and part is sq_lo), skip_group_check=True)
                    mm.then_inc(s["pj_ok"], 1)

                for g in range(NG):
                    cols = slice(HALF + g * 512, HALF + (g + 1) * 512)
                    if g == 0:
                        pe.wait_ge(s["s2_ok"], NC)
                    for k in range(KD):
                        mm = nc.tensor.matmul(bank[0][:], w_low[:, k, :], xt2[:, k, cols], start=(k == 0),
                                              stop=(k == KD - 1))
                    mm.then_inc(s["tp_ok"], 1)
                    for m in range(MT):
                        n = g * MT + m
                        if n == 0:
                            pe.wait_ge(s["max_ok"], 8 * NC)
                        if n >= 3:
                            pe.wait_ge(s["relu_ok"], n - 2)
                        if m == 0:
                            pe.wait_ge(s["xl_ok"], g + 1)
                            pe.wait_ge(s["tst_ok"], 2 * g + 2)
                        hb2 = bank[1 + n % 3][:]
                        for part in (xh, xl):
                            for k in range(KD):
                                nc.tensor.matmul(hb2, fc_t[:, k, m * P:(m + 1) * P], part[:, k, :],
                                                 start=(part is xh and k == 0), stop=False)
                        nc.tensor.matmul(hb2, u_t[:, m * P:(m + 1) * P], t_st[:], start=False, stop=True)\
                          .then_inc(s["h2p_ok"], 1)
                        if m >= 2:
                            project(n - 2)
                    project(g * MT + MT - 2)
                    project(g * MT + MT - 1)
                    for j in range(4):
                        c = 4 * g + j
                        if j == 0:
                            pe.wait_ge(s["ft_ok"], 2 * g + 2)
                            if g == 0:
                                pe.wait_ge(s["o2_ok"], NC)
                        if c >= 2:
                            pe.wait_ge(s["f3_ok"], c - 1)
                        for k in range(KD):
                            mm = nc.tensor.transpose(bank[7 if c % 2 else 4][:, k * P:(k + 1) * P],
                                                     ft[:, k, j * P:(j + 1) * P], ident[:])
                        mm.then_inc(s["ftp_ok"], 1)

        nc.all_engine_barrier(sems_to_clear=range(first, last + 1))
    ctx.close()


_OUT = (16, S, D)


def kernel(**inputs):
    import concourse.bacc as bacc
    from concourse.bass_utils import run_bass_kernel_spmd

    nc = bacc.Bacc("TRN2", target_bir_lowering=False, num_devices=1)
    arrays, args = {}, {}
    for name, value in inputs.items():
        v = np.ascontiguousarray(value)
        v = v.reshape(v.shape or (1,))
        arrays[f"in_{name}"] = v
        args[name] = nc.dram_tensor(f"in_{name}", v.shape, mybir.dt.from_np(v.dtype), kind="ExternalInput").ap()
    out = nc.dram_tensor("out_0", _OUT, F32, kind="ExternalOutput").ap()
    build_program(nc, args, out, _OUT[0])
    result = run_bass_kernel_spmd(nc, [arrays], core_ids=[0])
    return result.results[0]["out_0"]
```

```python
from contextlib import ExitStack

import numpy as np
import concourse.bass as bass
from concourse import mybir

F32 = mybir.dt.float32
F32R = mybir.dt.float32r
BF16 = mybir.dt.bfloat16
U32 = mybir.dt.uint32
ALU = mybir.AluOpType
ACT = mybir.ActivationFunctionType
AX = mybir.AxisListType

P = 128
D = 256
KD = D // P
S = 1024
NC = S // P
NG = S // 512
H = 16
DH = D // H
HH = H // 2
E = 8
BN = 64
EB = E * BN
RANK = 16
QB = 64
WIN = 64
HALF = WIN // 2
KW = 192
HID = 1024
MT = HID // P
EPS = 1e-5
BIG = -1e30
DV = DH + 1


def build_program(nc, a, out, n_seq):
    ctx = ExitStack()
    ctx.enter_context(nc.allow_non_contiguous_dma(reason="small transposed weights"))

    def sb(name, shape, dt=F32):
        return ctx.enter_context(nc.sbuf_tensor(name, shape, dt))

    def sem(name):
        return ctx.enter_context(nc.semaphore(name))

    x_dram = a["L0_attn_x"].rearrange("b (c p) d -> (b c) p d", p=P)
    out_dram = out.rearrange("b (c p) d -> (b c) p d", p=P)

    ident = sb("ident", [P, P])
    ident_bf = sb("ident_bf", [P, P], BF16)
    causal = sb("causal", [P, P])
    cum_mid = sb("cum_mid", [P, P])
    first_half = sb("first_half", [P, P])
    second_half = sb("second_half", [P, P])
    head_block = sb("head_block", [P, P])
    head_mask = sb("head_mask", [P, HH])
    expert_no = sb("expert_no", [P, E])
    minus_half = sb("minus_half", [P, NC])
    same_q = sb("same_q", [P, QB], BF16)
    block_ones = sb("block_ones", [P, 2, P], BF16)
    block_band = sb("block_band", [P, 2, P], BF16)
    chunk_band = sb("chunk_band", [P, KW], BF16)

    w_vg = sb("w_vg", [P, KD, 2 * D])
    w_k = sb("w_k", [P, KD, D])
    w_q = sb("w_q", [P, KD, D])
    w_z = sb("w_z", [P, KD, D])
    w_out = sb("w_out", [P, KD, D])
    w_gate = sb("w_gate", [P, KD, E])
    w_down = sb("w_down", [P, KD, EB])
    w_up = sb("w_up", [P, EB // P, D])
    b_up = sb("b_up", [P, D])
    bc_gk = sb("bc_gk", [P, D])
    bc_gamma = sb("bc_gamma", [P, D])
    bc_beta = sb("bc_beta", [P, D])
    bc_down = sb("bc_down", [P, EB])
    gk1_t = sb("gk1_t", [RANK, D])
    gk2 = sb("gk2", [RANK, D])

    x = sb("x", [P, NC, D])
    xn = sb("xn", [P, NC, D])
    SH = S + 2 * HALF
    xt2 = sb("xt2", [P, KD, SH])
    xt = xt2[:, :, HALF:HALF + S]
    qt = sb("qt", [P, KD, S])
    k2 = sb("k2", [P, 2, SH])
    kt = k2[:, :, HALF:HALF + S]
    zb = sb("zb", [P, NC, D])
    gk = sb("gk", [P, NC, D])
    zact = sb("zact", [P, 2, D])
    stats = sb("stats", [P, NC, 6])
    moments = sb("moments", [P, NC, 2])
    veps = sb("veps", [P, NC])
    rstd = sb("rstd", [P, NC])
    logits = sb("logits", [P, NC, E])
    top = sb("top", [P, NC, E])
    top_i = sb("top_i", [P, NC, E], U32)
    top_f = sb("top_f", [P, NC, 2])
    gdiff = sb("gdiff", [P, NC])
    gexp = sb("gexp", [P, NC])
    gden = sb("gden", [P, NC])
    g_top = sb("g_top", [P, 2, NC])
    g_hit = sb("g_hit", [P, 2, NC, E])
    gates = sb("gates", [P, NC, P])

    qx = sb("qx", [P, 2, H, P])
    am = sb("am", [P, H, P])
    ktok = sb("ktok", [P, D])
    vt = sb("vt", [P, HH, 4, DH])
    decay_in = sb("decay_in", [P, 2, D])
    decay_out = sb("decay_out", [P, 2, D])
    decay_state = sb("decay_state", [P, 2, 2, D])
    end_mask = sb("end_mask", [P, 2, P])
    tanh_g = sb("tanh_g", [P, D])
    silu_g = sb("silu_g", [P, 2, D])
    hb = sb("hb", [P, EB])
    hg = sb("hg", [P, EB])
    hgt = sb("hgt", [P, EB // P, P])
    gates_t = sb("gates_t", [P, NC, P])
    state = sb("state", [P, 2, P])
    state_mid = sb("state_mid", [P, 2, P])
    state_sum = sb("state_sum", [P, 2, P])
    ot = sb("ot", [P, 2, P])
    o_tok = sb("o_tok", [P, D])
    o_stats = sb("o_stats", [P, 6])
    o_mom = sb("o_mom", [P, 2])
    o_veps = sb("o_veps", [P, 1])
    o_rstd = sb("o_rstd", [P, 1])
    o_norm = sb("o_norm", [P, D])
    o_gam = sb("o_gam", [P, D])
    o_bet = sb("o_bet", [P, D])
    y_tok = sb("y_tok", [P, D])
    yt = sb("yt", [P, KD, P])
    tanh_f = sb("tanh_f", [P, D])
    f_gate = sb("f_gate", [P, D])
    sf = sb("sf", [P, D])

    w_q2 = sb("w_q2", [P, KD, D])
    w_kv2 = sb("w_kv2", [P, KD, 2, 2 * DH])
    w_k2r = sb("w_k2r", [P, KD, 2, HH, DH])
    w_o2 = sb("w_o2", [P, KD, D])
    b_q2 = sb("b_q2", [P, 2])
    b_k2 = sb("b_k2", [P, 2])
    bc_v2 = sb("bc_v2", [P, 2 * DH])
    bc_o2 = sb("bc_o2", [P, D])
    v_nat = sb("v_nat", [RANK, D])
    fb_t = sb("fb_t", [RANK, RANK])
    ffn_gate = sb("ffn_gate", [P, 1])
    w_low = sb("w_low", [P, KD, P])
    scale_fc = sb("scale_fc", [P, MT])
    scale_pj = sb("scale_pj", [P, KD])
    thr = sb("thr", [P, 2, MT])
    rscale = sb("rscale", [P, MT])
    u_nat = sb("u_nat", [P, MT, RANK])
    u_hi = sb("u_hi", [P, MT, RANK], F32R)
    u_lo = sb("u_lo", [P, MT, RANK])
    fc_t = sb("fc_t", [P, KD, HID], F32R)
    pj_t = sb("pj_t", [P, MT, D], F32R)
    u_t = sb("u_t", [P, HID], F32R)

    xh = sb("xh", [P, NG, KD, 512], F32R)
    xl = sb("xl", [P, NG, KD, 512], F32R)
    q2 = qt
    x_next = qt[:].rearrange("p k t -> p (k t)").rearrange("p (c d) -> p c d", d=D)
    am_flat = am[:].rearrange("p h t -> p (h t)")
    k2_bf = am_flat[:, 0:SH].bitcast(BF16).rearrange("p (g k) -> p g k", g=2)
    v2 = sb("v2", [P, 2 * NC, 2, DV])
    qx_bf = gates_t[:].rearrange("p c t -> p (c t)").bitcast(BF16).rearrange("p (h t) -> p h t", t=P)
    neg_max = sb("neg_max", [P, 2, H])
    diag_max = [t.bitcast(BF16).rearrange("p (h q) -> p h q", q=QB)
                for t in (hg[:], hgt[:].rearrange("p j t -> p (j t)"))]
    pr = xn[:, 0:4, :].rearrange("p c d -> p (c d)").rearrange("p (b h q) -> p b h q", b=2, q=QB)
    rden = sb("rden", [P, H])
    o2 = am_flat[:, SH:SH + D]
    o2t = am_flat[:, SH + D:SH + 2 * D]
    attn2 = zb
    t_hi = hb[:].bitcast(F32R)
    t_st = sb("t_st", [P, 512], F32R)
    relu = qx[:, 0, 0:8, :].rearrange("p h t -> p (h t)").rearrange("p (b t) -> p b t", b=2)
    sq = qx[:, 0, 8:16, :].rearrange("p h t -> p (h t)").rearrange("p (b t) -> p b t", b=2)
    sq_hi = sb("sq_hi", [P, 2, 512], F32R)
    sq_lo = sb("sq_lo", [P, 2, 512], F32R)
    ft = gk[:, 0:4, :].rearrange("p c d -> p (c d)").rearrange("p (o t) -> p o t", o=KD)
    fc_nat, fc_ter, pj_nat, pj_ter = x, xn, qt, kt
    u_st = gates

    bank = [ctx.enter_context(nc.psum_tensor(f"bank{i}", [P, 512], F32)) for i in range(8)]

    w_sem, cst, prep, prep_done = sem("w_sem"), sem("cst"), sem("prep"), sem("prep_done")

    loads = [
        (w_vg[:, :, 0:D], a["L0_attn_Wv"].rearrange("(k p) n -> p k n", p=P)),
        (w_vg[:, :, D:2 * D], a["L0_attn_Wg"].rearrange("(k p) n -> p k n", p=P)),
        (w_k[:], a["L0_attn_Wk"].rearrange("(k p) n -> p k n", p=P)),
        (w_q[:], a["L0_attn_Wq"].rearrange("(k p) n -> p k n", p=P)),
        (w_out[:], a["L0_attn_Wout"].rearrange("(k p) n -> p k n", p=P)),
        (w_gate[:], a["L0_ffn_w_gate"].rearrange("(k p) n -> p k n", p=P)),
        (w_up[:], a["L0_ffn_Wu"].rearrange("(j e) b d -> (e b) j d", e=2)),
        (b_up[0:E, :], a["L0_ffn_bu"]),
        (bc_gk[:], a["L0_attn_bgk2"].partition_broadcast(P)),
        (bc_gamma[:], a["L0_attn_gamma"].partition_broadcast(P)),
        (bc_beta[:], a["L0_attn_beta"].partition_broadcast(P)),
        (bc_down[:], a["L0_ffn_bd"].rearrange("e b -> (e b)").partition_broadcast(P)),
        (gk1_t[:], a["L0_attn_Wgk1"].rearrange("n r -> r n")),
        (gk2[:], a["L0_attn_Wgk2"]),
    ]
    loads += [
        (w_q2[:], a["L1_attn_Wq"].rearrange("(k p) n -> p k n", p=P)),
        (w_kv2[:, :, 0, :], a["L1_attn_Wk"].rearrange("(k p) n -> p k n", p=P)),
        (w_kv2[:, :, 1, :], a["L1_attn_Wv"].rearrange("(k p) n -> p k n", p=P)),
        (w_o2[:], a["L1_attn_Wo"].rearrange("(k p) n -> p k n", p=P)),
        (b_q2[:], a["L1_attn_bq"].rearrange("(k p) -> p k", p=P)),
        (bc_v2[:], a["L1_attn_bv"].partition_broadcast(P)),
        (bc_o2[:], a["L1_attn_bo"].partition_broadcast(P)),
        (v_nat[:], a["L1_ffn_v"]),
        (fb_t[:], a["L1_ffn_fast_b"].rearrange("j i -> i j")),
        (ffn_gate[:], a["L1_ffn_gate"].partition_broadcast(P)),
        (u_nat[:], a["L1_ffn_u"].rearrange("(m p) r -> p m r", p=P)),
        (fc_nat[:], a["L1_ffn_w_fc"].rearrange("(m p) d -> p m d", p=P)),
        (pj_nat[:], a["L1_ffn_w_proj"].rearrange("(o p) h -> p o h", p=P)),
    ]
    for h in range(HH):
        loads.append((b_k2[h * DH:(h + 1) * DH, :], a["L1_attn_bk"].rearrange("(g d) -> d g", g=2)))
    for k in range(KD):
        loads.append((w_down[:, k, :].rearrange("p (e b) -> p e b", e=E),
                      a["L0_ffn_Wd"][:, k * P:(k + 1) * P, :].rearrange("e p b -> p e b")))

    with nc.Block() as block:

        @block.gpsimd
        def _(pool):
            done = [0]

            def link(ins):
                done[0] += 1
                ins.then_inc(cst, 1)
                pool.wait_ge(cst, done[0])

            def band(tile, lo, hi, width):
                link(nc.gpsimd.affine_select(out=tile, in_=tile, compare_op=ALU.is_ge, fill=BIG, base=0,
                                             pattern=[[1, width]], channel_multiplier=-1))
                link(nc.gpsimd.affine_select(out=tile, in_=tile, compare_op=ALU.is_ge, fill=BIG, base=WIN - 1,
                                             pattern=[[-1, width]], channel_multiplier=1))

            for t in (ident, ident_bf, second_half, same_q, block_ones, block_band, chunk_band, gates, vt,
                      state, xt2, k2, k2_bf, w_low):
                link(nc.gpsimd.memset(t[:], 0.0))
            for t in (causal, head_block, head_mask, first_half):
                link(nc.gpsimd.memset(t[:], 1.0))
            link(nc.gpsimd.memset(minus_half[:], -0.5))
            link(nc.gpsimd.memset(v2[:], 1.0))
            for t in (ident, ident_bf):
                link(nc.gpsimd.affine_select(out=t[:], in_=t[:], compare_op=ALU.not_equal, fill=1.0, base=0,
                                             pattern=[[-1, P]], channel_multiplier=1))
            for base in (0, -QB):
                link(nc.gpsimd.affine_select(out=same_q[:], in_=same_q[:], compare_op=ALU.not_equal, fill=1.0,
                                             base=base, pattern=[[-1, QB]], channel_multiplier=1))
            link(nc.gpsimd.affine_select(out=causal[:], in_=causal[:], compare_op=ALU.is_ge, fill=0.0, base=0,
                                         pattern=[[1, P]], channel_multiplier=-1))
            link(nc.gpsimd.tensor_copy(cum_mid[:], causal[:]))
            link(nc.gpsimd.tensor_scalar(cum_mid[0:QB, :], cum_mid[0:QB, :], -1.0, None, ALU.add))
            link(nc.gpsimd.memset(first_half[QB:P, :], 0.0))
            link(nc.gpsimd.memset(second_half[QB:P, :], 1.0))
            blocks = head_block[:].rearrange("p (h d) -> p h d", d=DH)
            for t, tail in ((blocks, [[0, DH]]), (head_mask[:], [])):
                link(nc.gpsimd.affine_select(out=t, in_=t, compare_op=ALU.is_ge, fill=0.0, base=0,
                                             pattern=[[-DH, HH]] + tail, channel_multiplier=1))
                link(nc.gpsimd.affine_select(out=t, in_=t, compare_op=ALU.is_ge, fill=0.0, base=DH - 1,
                                             pattern=[[DH, HH]] + tail, channel_multiplier=-1))
            for b in range(2):
                link(nc.gpsimd.memset(block_ones[QB * b:QB * (b + 1), b, :], 1.0))
                band(block_band[QB * b:QB * (b + 1), b, :], 0, 0, P)
            band(chunk_band[:], 0, 0, KW)
            for e in range(E):
                link(nc.gpsimd.memset(expert_no[:, e:e + 1], float(e)))

        @block.vector
        def _(dve):
            nc.vector.memset(b_up[:], 0.0).then_inc(prep, 1)
            dve.wait_ge(prep_done, 1)
            for k in range(KD):
                nc.vector.tensor_copy(w_z[:, k, :], bank[k][:, 0:D])

        @block.tensor
        def _(pe):
            pe.wait_ge(w_sem, 16 * len(loads))
            for k in range(KD):
                mm = nc.tensor.matmul(bank[k][:, 0:D], gk1_t[:, k * P:(k + 1) * P], gk2[:], start=True, stop=True)
            mm.then_inc(prep_done, 1)

        @block.sync
        def _(sp):
            sp.wait_ge(prep, 1)
            for dst, src in loads:
                sp.dma_start(dst, src).then_inc(w_sem, 16)
            sp.wait_ge(w_sem, 16 * len(loads))

    tern, tern_pe, tern_act, tern_clear = sem("tern"), sem("tern_pe"), sem("tern_act"), sem("tern_clear")
    with nc.Block() as block:

        @block.vector
        def _(dve):
            done = [0]

            def link(ins):
                done[0] += 1
                ins.then_inc(tern, 1)
                dve.wait_ge(tern, done[0])

            for k in range(KD):
                link(nc.vector.tensor_copy(w_k2r[:, k], w_kv2[:, k, 0, :].rearrange("p (g d) -> p g d", g=2)
                                           .unsqueeze(2).broadcast_to([P, 2, HH, DH])))
            for nat, ter, scale, n, width in ((fc_nat, fc_ter, scale_fc, MT, D), (pj_nat, pj_ter, scale_pj, KD, HID)):
                link(nc.vector.tensor_reduce(scale[:], nat[:], AX.X, ALU.add, apply_absolute_value=True))
                link(nc.vector.tensor_scalar(scale[:], scale[:], 1.0 / width, 1e-5, ALU.mult, ALU.max))
                link(nc.vector.tensor_scalar(thr[:, 0, 0:n], scale[:], 0.5, None, ALU.mult))
                link(nc.vector.tensor_scalar(thr[:, 1, 0:n], scale[:], -0.5, None, ALU.mult))
                for m in range(n):
                    link(nc.vector.tensor_scalar(ter[:, m, :], nat[:, m, :], thr[:, 1, m:m + 1], None, ALU.is_lt))
                    link(nc.vector.scalar_tensor_tensor(ter[:, m, :], nat[:, m, :], thr[:, 0, m:m + 1],
                                                        ter[:, m, :], ALU.is_gt, ALU.subtract))
            link(nc.vector.reciprocal(rscale[:], scale_fc[:]))
            link(nc.vector.tensor_tensor(u_nat[:], u_nat[:], rscale[:].unsqueeze(2).broadcast_to([P, MT, RANK]),
                                         ALU.mult))
            link(nc.vector.tensor_copy(u_hi[:], u_nat[:]))
            link(nc.vector.tensor_tensor(u_lo[:], u_nat[:], u_hi[:].bitcast(F32), ALU.subtract))
            for r in (0, 2):
                link(nc.vector.tensor_copy(u_st[:, :, 32 * r:32 * r + RANK], u_hi[:].bitcast(F32)))
                link(nc.vector.tensor_copy(u_st[:, :, 32 * r + 32:32 * r + 32 + RANK], u_lo[:]))
            dve.wait_ge(tern_pe, 1)
            for k in range(KD):
                for r in range(4):
                    link(nc.vector.tensor_scalar(w_low[:, k, 32 * r:32 * r + RANK], bank[k][:, 0:RANK],
                                                 ffn_gate[:], None, ALU.mult))

        n_ternary = 2 + 4 + 2 * MT + 4 + 2 * KD + 4 + 4

        @block.tensor
        def _(pe):
            for k in range(KD):
                mm = nc.tensor.matmul(bank[k][:, 0:RANK], v_nat[:, k * P:(k + 1) * P], fb_t[:], start=True,
                                      stop=True)
            mm.then_inc(tern_pe, 1)
            pe.wait_ge(tern, n_ternary)
            n = 0

            def turn(parts):
                nonlocal n
                if n >= 4:
                    pe.wait_ge(tern_act, n - 3)
                for j, part in enumerate(parts):
                    mm = nc.tensor.transpose(bank[2 + n % 4][:, j * P:(j + 1) * P], part, ident[:])
                mm.then_inc(tern_pe, 1)
                n += 1

            for k in range(KD):
                for m in range(0, MT, 4):
                    turn([fc_ter[:, m + j, k * P:(k + 1) * P] for j in range(4)])
            for m in range(0, MT, 2):
                turn([pj_ter[:, j % 2, (m + j // 2) * P:(m + j // 2 + 1) * P] for j in range(4)])
            for m in range(0, MT, 4):
                turn([u_st[:, m + j, :] for j in range(4)])

        @block.scalar
        def _(act):
            targets = [fc_t[:, k, m * P:(m + 4) * P] for k in range(KD) for m in range(0, MT, 4)]
            targets += [pj_t[:, m:m + 2, :].rearrange("p m d -> p (m d)") for m in range(0, MT, 2)]
            targets += [u_t[:, m * P:(m + 4) * P] for m in range(0, MT, 4)]
            for n, target in enumerate(targets):
                act.wait_ge(tern_pe, n + 2)
                nc.scalar.copy(target, bank[2 + n % 4][:]).then_inc(tern_act, 1)

        @block.gpsimd
        def _(pool):
            pool.wait_ge(tern_act, 10)
            nc.gpsimd.memset(gates[:], 0.0).then_inc(tern_clear, 1)

    names = ("xc_ok xtp_ok xt_ok zp_ok zb_ok zabs_ok zexp_ok zln_ok gk_ok lg_ok lgc_ok "
             "gsel gexp_ok gates_ok gtp_ok gt_ok qkp_ok qk_ok vg_ok kp_ok hp_ok hb_ok tg_ok sg_ok hg_ok ktok_ok "
             "qx_ok at_ok am_ok cum_ok din_ok dout_ok dst_ok vt_ok smid_ok end_ok ds_ok ssum_ok state_ok ot_ok "
             "ots_ok otok_ok o1_ok ost_ok ove_ok ors_ok onorm_ok ogam_ok obet_ok y_ok ytp_ok yt_ok s_ok hgtp_ok "
             "hgt_ok f_ok tf_ok f1_ok f2_ok x_ok out_sem "
             "st2 ve2 rs2 xn2_ok xt2p_ok xt2_ok qk2p_ok qk2_ok kbf_ok v2p_ok v2_ok qx2_ok qxb_ok sc_ok max_ok dmax_ok "
             "stp_ok pr_ok pv_ok rden_ok o2_ok o2tp_ok o2t_ok s2p_ok s2_ok xh_ok xl_ok tp_ok thi_ok tst_ok h2p_ok "
             "relu_ok sq_ok sqh_ok sql_ok pj_ok ft_ok ftp_ok tf2_ok f3_ok f4_ok y2_ok nst_ok nve_ok nrs_ok "
             "nxn_ok").split()
    s = {n: sem(n) for n in names}
    x_in = [sem(f"x_in{c}") for c in range(NC)]
    first, last = s[names[0]].num, x_in[-1].num

    def head_load(sp, index):
        for c in range(NC):
            sp.dma_start(x_next[:, c, :], x_dram[bass.ds(index * NC + c, 1), :, :].rearrange("o p d -> (o p) d"))\
              .then_inc(x_in[c], 16)

    def head_stats(dve, c):
        dve.wait_ge(x_in[c], 16)
        nc.vector.bn_stats(stats[:, c, :], x_next[:, c, :]).then_inc(s["nst_ok"], 1)

    def head_moments(dve):
        dve.wait_ge(s["nst_ok"], NC)
        for c in range(NC):
            nc.vector.bn_aggr(moments[:, c, :], stats[:, c, :]).then_inc(s["nst_ok"], 1)

    def head_rstd(pool):
        pool.wait_ge(s["nst_ok"], 2 * NC)
        nc.gpsimd.tensor_scalar(veps[:], moments[:, :, 1], EPS, None, ALU.add).then_inc(s["nve_ok"], 1)
        pool.wait_ge(s["nve_ok"], 1)
        nc.gpsimd.tensor_tensor(rstd[:], veps[:], minus_half[:], ALU.pow).then_inc(s["nrs_ok"], 1)

    def head_normalise(dve, c):
        if c == 0:
            dve.wait_ge(s["nrs_ok"], 1)
        nc.vector.tensor_scalar(xn[:, c, :], x_next[:, c, :], moments[:, c, 0:1], rstd[:, c:c + 1],
                                ALU.subtract, ALU.mult).then_inc(s["nxn_ok"], 1)

    def head_turn(pe, c):
        pe.wait_ge(s["nxn_ok"], c + 1)
        if c >= 2:
            pe.wait_ge(s["xt_ok"], c - 1)
        for k in range(KD):
            mm = nc.tensor.transpose(bank[c % 2][:, k * P:(k + 1) * P], xn[:, c, k * P:(k + 1) * P], ident[:])
        mm.then_inc(s["xtp_ok"], 1)

    def head_turned(act, c):
        act.wait_ge(s["xtp_ok"], c + 1)
        nc.scalar.copy(xt[:, :, c * P:(c + 1) * P], bank[c % 2][:, 0:D].rearrange("p (k t) -> p k t", k=KD))\
          .then_inc(s["xt_ok"], 1)

    with nc.Block() as block:

        @block.sync
        def _(sp):
            head_load(sp, 0)

        @block.vector
        def _(dve):
            for c in range(NC):
                head_stats(dve, c)
            head_moments(dve)
            for c in range(NC):
                head_normalise(dve, c)

        @block.gpsimd
        def _(pool):
            head_rstd(pool)

        @block.tensor
        def _(pe):
            for c in range(NC):
                head_turn(pe, c)

        @block.scalar
        def _(act):
            for c in range(NC):
                head_turned(act, c)

    nc.all_engine_barrier(sems_to_clear=range(first, last + 1))

    with nc.Fori(0, n_seq) as seq:
        with nc.Block() as block:

            @block.sync
            def _(sp):
                sp.wait_ge(s["qx2_ok"], 2 * NC)
                head_load(sp, (seq + 1) % n_seq)
                for c in range(NC):
                    sp.wait_ge(s["y2_ok"], c + 1)
                    sp.dma_start(out_dram[bass.ds(seq * NC + c, 1), :, :].rearrange("o p d -> (o p) d"),
                                 x[:, c, :]).then_inc(s["out_sem"], 16)
                sp.wait_ge(s["out_sem"], 16 * NC)
                for c in range(NC):
                    sp.wait_ge(x_in[c], 16)

            @block.gpsimd
            def _(pool):
                nc.gpsimd.tensor_copy(x[:], x_next[:]).then_inc(s["xc_ok"], 1)

                def head_queries(src, c, done):
                    for half in range(2):
                        nc.gpsimd.tensor_tensor(
                            qx[:, c % 2, half * HH:(half + 1) * HH, :],
                            src[:, half:half + 1, c * P:(c + 1) * P].broadcast_to([P, HH, P]),
                            head_mask[:].unsqueeze(2).broadcast_to([P, HH, P]), ALU.mult).then_inc(s[done], 1)

                def norm_affine(c):
                    pool.wait_ge(s["ost_ok"], 2 * c + 2)
                    nc.gpsimd.tensor_scalar(o_veps[:], o_mom[:, 1:2], EPS, None, ALU.add).then_inc(s["ove_ok"], 1)
                    pool.wait_ge(s["ove_ok"], c + 1)
                    if c:
                        pool.wait_ge(s["onorm_ok"], c)
                    nc.gpsimd.tensor_tensor(o_rstd[:], o_veps[:], minus_half[:, 0:1], ALU.pow)\
                      .then_inc(s["ors_ok"], 1)
                    pool.wait_ge(s["onorm_ok"], c + 1)
                    nc.gpsimd.tensor_tensor(o_gam[:], o_norm[:], bc_gamma[:], ALU.mult).then_inc(s["ogam_ok"], 1)
                    pool.wait_ge(s["ogam_ok"], c + 1)
                    if c:
                        pool.wait_ge(s["y_ok"], c)
                    nc.gpsimd.tensor_tensor(o_bet[:], o_gam[:], bc_beta[:], ALU.add).then_inc(s["obet_ok"], 1)

                pool.wait_ge(s["qk_ok"], 2)
                head_queries(qt, 0, "qx_ok")
                for c in range(NC):
                    if c:
                        norm_affine(c - 1)
                    pool.wait_ge(s["dst_ok"], c + 1)
                    if c:
                        pool.wait_ge(s["state_ok"], c)
                    nc.gpsimd.tensor_tensor(
                        end_mask[:], decay_state[:, c % 2, 1, :].rearrange("p (h f) -> p h f", h=2),
                        head_block[:].unsqueeze(1).broadcast_to([P, 2, P]), ALU.mult).then_inc(s["end_ok"], 1)
                    if c + 1 < NC:
                        if c + 1 == 4:
                            pool.wait_ge(s["qk_ok"], 6)
                        if c:
                            pool.wait_ge(s["at_ok"], 4 * c)
                        head_queries(qt, c + 1, "qx_ok")

                for part, (lo, hi) in enumerate(((0, NC - 1), (NC - 1, NC))):
                    pool.wait_ge(s["st2"], 2 * hi)
                    nc.gpsimd.tensor_scalar(veps[:, lo:hi], moments[:, lo:hi, 1], EPS, None, ALU.add)\
                      .then_inc(s["ve2"], 1)
                    pool.wait_ge(s["ve2"], part + 1)
                    nc.gpsimd.tensor_tensor(rstd[:, lo:hi], veps[:, lo:hi], minus_half[:, lo:hi], ALU.pow)\
                      .then_inc(s["rs2"], 1)
                    if part == 0:
                        norm_affine(NC - 1)
                for c in range(NC):
                    if c == 0:
                        pool.wait_ge(s["qk2_ok"], 2)
                    elif c == 4:
                        pool.wait_ge(s["qk2_ok"], 6)
                    if c >= 2:
                        pool.wait_ge(s["stp_ok"], 4 * (c - 1))
                    head_queries(q2, c, "qx2_ok")
                    if c in (1, 3):
                        g = c // 2
                        pool.wait_ge(s["xh_ok"], g + 1)
                        nc.gpsimd.tensor_tensor(xl[:, g], xt[:, :, g * 512:(g + 1) * 512], xh[:, g].bitcast(F32),
                                                ALU.subtract).then_inc(s["xl_ok"], 1)
                for n in range(NG * MT):
                    pool.wait_ge(s["relu_ok"], n + 1)
                    if n >= 2:
                        pool.wait_ge(s["sql_ok"], n - 1)
                    nc.gpsimd.tensor_tensor(sq[:, n % 2, :], relu[:, n % 2, :], relu[:, n % 2, :], ALU.mult)\
                      .then_inc(s["sq_ok"], 1)
                head_rstd(pool)

            @block.scalar
            def _(act):
                for i in range(NC // 2):
                    act.wait_ge(s["zb_ok"], i + 1)
                    if i:
                        act.wait_ge(s["gk_ok"], i)
                    nc.scalar.activation(zact[:], zb[:, 2 * i:2 * i + 2, :], ACT.Abs).then_inc(s["zabs_ok"], 1)
                    act.wait_ge(s["zabs_ok"], i + 1)
                    nc.scalar.activation(zact[:], zact[:], ACT.Exp, scale=-1.0).then_inc(s["zexp_ok"], 1)
                    act.wait_ge(s["zexp_ok"], i + 1)
                    nc.scalar.activation(zact[:], zact[:], ACT.Ln, bias=1.0).then_inc(s["zln_ok"], 1)
                act.wait_ge(s["gsel"], 1)
                nc.scalar.activation(gexp[:], gdiff[:], ACT.Exp).then_inc(s["gexp_ok"], 1)
                act.wait_ge(s["xc_ok"], 1)
                for n in range(8):
                    g, which, half = n // 4, n // 2 % 2, n % 2
                    act.wait_ge(s["qkp_ok"], n + 1)
                    nc.scalar.copy((kt if which else qt)[:, half, g * 512:(g + 1) * 512], bank[4 + n % 4][:])\
                      .then_inc(s["qk_ok"], 1)
                for b in range(2):
                    act.wait_ge(s["gtp_ok"], b + 1)
                    nc.scalar.copy(gates_t[:, 4 * b:4 * b + 4, :], bank[1 + b][:].rearrange("p (c t) -> p c t", t=P))\
                      .then_inc(s["gt_ok"], 1)

                def decays(c):
                    act.wait_ge(s["cum_ok"], c + 1)
                    if c >= 2:
                        act.wait_ge(s["vt_ok"], c - 1)
                    nc.scalar.activation(decay_in[:, c % 2, :], bank[3][:, 0:D], ACT.Exp, scale=-1.0 / 16)\
                      .then_inc(s["din_ok"], 1)
                    if c >= 2:
                        act.wait_ge(s["o1_ok"], c - 1)
                    nc.scalar.activation(decay_out[:, c % 2, :], bank[3][:, 0:D], ACT.Exp, scale=1.0 / 16)\
                      .then_inc(s["dout_ok"], 1)
                    if c >= 2:
                        act.wait_ge(s["end_ok"], c - 1)
                        act.wait_ge(s["smid_ok"], c - 1)
                    nc.scalar.activation(decay_state[:, c % 2], bank[4][:].rearrange("p (a f) -> p a f", a=2),
                                         ACT.Exp, scale=1.0 / 16).then_inc(s["dst_ok"], 1)

                def output_turned(c):
                    act.wait_ge(s["ytp_ok"], c + 1)
                    if c:
                        act.wait_ge(s["s_ok"], c)
                    nc.scalar.copy(yt[:], bank[7][:, 0:D].rearrange("p (k t) -> p k t", k=KD))\
                      .then_inc(s["yt_ok"], 1)

                decays(0)
                for c in range(NC):
                    act.wait_ge(s["vg_ok"], c + 1)
                    if c:
                        act.wait_ge(s["sg_ok"], c)
                    nc.scalar.activation(tanh_g[:], bank[0][:, D:2 * D], ACT.Tanh, scale=0.5)\
                      .then_inc(s["tg_ok"], 1)
                    act.wait_ge(s["kp_ok"], c + 1)
                    if c:
                        act.wait_ge(s["ds_ok"], c)
                    nc.scalar.copy(ktok[:], bank[1][:, 0:D]).then_inc(s["ktok_ok"], 1)
                    if c:
                        output_turned(c - 1)
                    act.wait_ge(s["hgtp_ok"], c + 1)
                    if c:
                        act.wait_ge(s["f_ok"], c)
                    nc.scalar.copy(hgt[:], bank[2][:].rearrange("p (j t) -> p j t", t=P)).then_inc(s["hgt_ok"], 1)
                    if c + 1 < NC:
                        decays(c + 1)
                    act.wait_ge(s["ot_ok"], c + 1)
                    if c:
                        act.wait_ge(s["otok_ok"], c)
                    nc.scalar.copy(ot[:], bank[7][:, 0:D].rearrange("p (k t) -> p k t", k=KD))\
                      .then_inc(s["ots_ok"], 1)
                    act.wait_ge(s["f_ok"], c + 1)
                    if c:
                        act.wait_ge(s["f1_ok"], c)
                    nc.scalar.activation(tanh_f[:], bank[5][:, 0:D], ACT.Tanh, scale=0.25).then_inc(s["tf_ok"], 1)

                def chunk_turned(c):
                    act.wait_ge(s["xt2p_ok"], c + 1)
                    nc.scalar.copy(xt[:, :, c * P:(c + 1) * P],
                                   bank[3 * (c % 2)][:, 0:D].rearrange("p (k t) -> p k t", k=KD))\
                      .then_inc(s["xt2_ok"], 1)

                def queries_keys(n):
                    g, which, half = n // 4, n // 2 % 2, n % 2
                    act.wait_ge(s["qk2p_ok"], n + 1)
                    dst, bias = (kt, b_k2) if which else (q2, b_q2)
                    nc.scalar.activation(dst[:, half, g * 512:(g + 1) * 512], bank[(1, 2, 4)[n % 3]][:],
                                         ACT.Identity, bias=bias[:, half:half + 1]).then_inc(s["qk2_ok"], 1)

                for c in range(NC - 1):
                    chunk_turned(c)
                for n in range(4):
                    queries_keys(n)
                output_turned(NC - 1)
                chunk_turned(NC - 1)
                for n in range(4, 8):
                    queries_keys(n)

                def attention_turned(c):
                    act.wait_ge(s["o2tp_ok"], c + 1)
                    if c:
                        act.wait_ge(s["s2p_ok"], c)
                    nc.scalar.copy(o2t, bank[0][:, 0:D])\
                      .then_inc(s["o2t_ok"], 1)

                def queries_bf(c, half):
                    act.wait_ge(s["qx2_ok"], 2 * c + half + 1)
                    if c:
                        act.wait_ge(s["sc_ok"], 8 * c)
                    nc.scalar.copy(qx_bf[:, half * HH:(half + 1) * HH, :],
                                   qx[:, c % 2, half * HH:(half + 1) * HH, :]).then_inc(s["qxb_ok"], 1)

                queries_bf(0, 0)
                queries_bf(0, 1)
                for c in range(NC):
                    for u in range(4):
                        n = 4 * c + u
                        act.wait_ge(s["stp_ok"], n + 1)
                        if n >= 2:
                            act.wait_ge(s["pv_ok"], n - 1)
                        nc.scalar.activation(pr[:, n % 2], bank[5 + n % 2][:].rearrange("p (h q) -> p h q", q=QB),
                                             ACT.Exp).then_inc(s["pr_ok"], 1)
                        if c and u == 0:
                            attention_turned(c - 1)
                        if c + 1 < NC and u >= 1 and u < 3:
                            queries_bf(c + 1, u - 1)
                attention_turned(NC - 1)

                def squares(n):
                    act.wait_ge(s["sq_ok"], n + 1)
                    if n >= 2:
                        act.wait_ge(s["pj_ok"], n - 1)
                    nc.scalar.copy(sq_hi[:, n % 2, :], sq[:, n % 2, :]).then_inc(s["sqh_ok"], 1)

                def ffn_scaled(g):
                    act.wait_ge(s["pj_ok"], (g + 1) * MT)
                    if g:
                        act.wait_ge(s["ftp_ok"], 4 * g)
                    for o in range(KD):
                        nc.scalar.activation(ft[:, o, :], bank[5 + o][:], ACT.Identity, scale=scale_pj[:, o:o + 1])\
                          .then_inc(s["ft_ok"], 1)

                def ffn_tanh(c):
                    act.wait_ge(s["ftp_ok"], c + 1)
                    if c:
                        act.wait_ge(s["f3_ok"], c)
                    nc.scalar.activation(tanh_f[:], bank[7 if c % 2 else 4][:, 0:D], ACT.Tanh, scale=0.5)\
                      .then_inc(s["tf2_ok"], 1)

                for n in range(NG * MT + 2):
                    if n < NG * MT:
                        act.wait_ge(s["h2p_ok"], n + 1)
                        if n >= 2:
                            act.wait_ge(s["sq_ok"], n - 1)
                        nc.scalar.activation(relu[:, n % 2, :], bank[1 + n % 3][:], ACT.Relu,
                                             scale=scale_fc[:, n % MT:n % MT + 1]).then_inc(s["relu_ok"], 1)
                    if 1 <= n <= NG * MT:
                        squares(n - 1)
                    if n == MT + 1:
                        ffn_scaled(0)
                    if MT + 2 <= n < MT + 6:
                        ffn_tanh(n - MT - 2)
                ffn_scaled(1)
                for c in range(NC):
                    head_turned(act, c)
                    if c % 2:
                        ffn_tanh(4 + c // 2)

            @block.vector
            def _(dve):
                for i in range(NC // 2):
                    dve.wait_ge(s["zp_ok"], i + 1)
                    nc.vector.tensor_tensor(zb[:, 2 * i:2 * i + 2, :],
                                            bank[i % 2][:].rearrange("p (a f) -> p a f", a=2),
                                            bc_gk[:].unsqueeze(1).broadcast_to([P, 2, D]), ALU.add)\
                      .then_inc(s["zb_ok"], 1)
                dve.wait_ge(s["lg_ok"], 1)
                nc.vector.tensor_copy(logits[:], bank[3][:, 0:NC * E].rearrange("p (c e) -> p c e", e=E))\
                  .then_inc(s["lgc_ok"], 1)
                for i in range(NC // 2):
                    dve.wait_ge(s["zln_ok"], i + 1)
                    nc.vector.scalar_tensor_tensor(gk[:, 2 * i:2 * i + 2, :], zb[:, 2 * i:2 * i + 2, :], 0.0,
                                                   zact[:], ALU.min, ALU.subtract).then_inc(s["gk_ok"], 1)
                dve.wait_ge(s["lgc_ok"], 1)
                for c in range(NC):
                    nc.vector.max(top[:, c, :], logits[:, c, :]).then_inc(s["lgc_ok"], 1)
                dve.wait_ge(s["lgc_ok"], 1 + NC)
                nc.vector.tensor_sub(gdiff[:], top[:, :, 1], top[:, :, 0]).then_inc(s["gsel"], 1)
                for c in range(NC):
                    nc.vector.max_index(top_i[:, c, :], top[:, c, :], logits[:, c, :]).then_inc(s["lgc_ok"], 1)
                dve.wait_ge(s["lgc_ok"], 1 + 2 * NC)
                nc.vector.tensor_copy(top_f[:], top_i[:, :, 0:2]).then_inc(s["gsel"], 1)
                dve.wait_ge(s["gexp_ok"], 1)
                nc.vector.tensor_scalar(gden[:], gexp[:], 1.0, None, ALU.add).then_inc(s["gsel"], 1)
                dve.wait_ge(s["gsel"], 3)
                nc.vector.reciprocal(g_top[:, 0, :], gden[:]).then_inc(s["gsel"], 1)
                dve.wait_ge(s["gsel"], 4)
                nc.vector.tensor_tensor(g_top[:, 1, :], gexp[:], g_top[:, 0, :], ALU.mult).then_inc(s["gsel"], 1)
                for r in range(2):
                    nc.vector.tensor_tensor(g_hit[:, r], top_f[:, :, r:r + 1].broadcast_to([P, NC, E]),
                                            expert_no[:].unsqueeze(1).broadcast_to([P, NC, E]), ALU.is_equal)\
                      .then_inc(s["gsel"], 1)
                dve.wait_ge(s["gsel"], 7)
                for r in range(2):
                    nc.vector.tensor_tensor(g_hit[:, r], g_hit[:, r],
                                            g_top[:, r, :].unsqueeze(2).broadcast_to([P, NC, E]), ALU.mult)\
                      .then_inc(s["gsel"], 1)
                dve.wait_ge(s["gsel"], 9)
                nc.vector.tensor_add(gates[:, :, 0:E], g_hit[:, 0], g_hit[:, 1]).then_inc(s["gates_ok"], 1)
                dve.wait_ge(s["gates_ok"], 1)
                dve.wait_ge(s["xc_ok"], 1)

                def gated_output(c):
                    dve.wait_ge(s["obet_ok"], c + 1)
                    dve.wait_ge(s["sg_ok"], c + 1)
                    if c:
                        dve.wait_ge(s["ytp_ok"], c)
                    nc.vector.tensor_tensor(y_tok[:], o_bet[:], silu_g[:, c % 2, :], ALU.mult)\
                      .then_inc(s["y_ok"], 1)

                def normalise_output(c):
                    dve.wait_ge(s["ors_ok"], c + 1)
                    if c:
                        dve.wait_ge(s["ogam_ok"], c)
                    nc.vector.tensor_scalar(o_norm[:], o_tok[:], o_mom[:, 0:1], o_rstd[:], ALU.subtract, ALU.mult)\
                      .then_inc(s["onorm_ok"], 1)

                def finish_chunk(c):
                    dve.wait_ge(s["s_ok"], c + 1)
                    dve.wait_ge(s["f1_ok"], c + 1)
                    if c:
                        dve.wait_ge(s["x_ok"], c)
                    nc.vector.scalar_tensor_tensor(sf[:], f_gate[:], 0.125, bank[6][:, 0:D], ALU.mult,
                                                   ALU.mult).then_inc(s["f2_ok"], 1)
                    dve.wait_ge(s["f2_ok"], c + 1)
                    nc.vector.tensor_add(x[:, c, :], x[:, c, :], sf[:]).then_inc(s["x_ok"], 1)
                    dve.wait_ge(s["x_ok"], c + 1)
                    nc.vector.bn_stats(stats[:, c, :], x[:, c, :]).then_inc(s["st2"], 1)
                    dve.wait_ge(s["st2"], 2 * c + 1)
                    nc.vector.bn_aggr(moments[:, c, :], stats[:, c, :]).then_inc(s["st2"], 1)

                def normalise2(c):
                    nc.vector.tensor_scalar(xn[:, c, :], x[:, c, :], moments[:, c, 0:1], rstd[:, c:c + 1],
                                            ALU.subtract, ALU.mult).then_inc(s["xn2_ok"], 1)

                for c in range(NC):
                    dve.wait_ge(s["tg_ok"], c + 1)
                    dve.wait_ge(s["din_ok"], c + 1)
                    if c:
                        dve.wait_ge(s["ds_ok"], c)
                    nc.vector.tensor_tensor(
                        vt[:, :, 0:4:3, :], bank[0][:, 0:D].rearrange("p (j e d) -> p j e d", e=2, d=DH),
                        decay_in[:, c % 2, :].rearrange("p (j e d) -> p j e d", e=2, d=DH), ALU.mult)\
                      .then_inc(s["vt_ok"], 1)
                    if c >= 2:
                        dve.wait_ge(s["y_ok"], c - 1)
                    nc.vector.scalar_tensor_tensor(silu_g[:, c % 2, :], tanh_g[:], 1.0, bank[0][:, D:2 * D],
                                                   ALU.add, ALU.mult).then_inc(s["sg_ok"], 1)
                    if c:
                        gated_output(c - 1)
                    dve.wait_ge(s["hp_ok"], c + 1)
                    if c:
                        dve.wait_ge(s["hg_ok"], c)
                    nc.vector.tensor_add(hb[:], bank[2][:], bc_down[:]).then_inc(s["hb_ok"], 1)
                    dve.wait_ge(s["hb_ok"], c + 1)
                    if c:
                        dve.wait_ge(s["hgtp_ok"], c)
                    nc.vector.scalar_tensor_tensor(
                        hg[:].rearrange("p (e b) -> p e b", e=E), hb[:].rearrange("p (e b) -> p e b", e=E), 0.0,
                        gates[:, c, 0:E].unsqueeze(2).broadcast_to([P, E, BN]), ALU.max, ALU.mult)\
                      .then_inc(s["hg_ok"], 1)
                    dve.wait_ge(s["dst_ok"], c + 1)
                    if c:
                        dve.wait_ge(s["state_ok"], c)
                        dve.wait_ge(s["ot_ok"], c)
                    nc.vector.tensor_tensor(state_mid[:], state[:],
                                            decay_state[:, c % 2, 0, :].rearrange("p (h f) -> p h f", h=2),
                                            ALU.mult).then_inc(s["smid_ok"], 1)
                    for j in range(4):
                        dve.wait_ge(s["at_ok"], 4 * c + j + 1)
                        nc.vector.tensor_tensor(am[:, 4 * j:4 * j + 4, :],
                                                bank[5 + j % 2][:].rearrange("p (h t) -> p h t", t=P),
                                                causal[:].unsqueeze(1).broadcast_to([P, 4, P]), ALU.mult)\
                          .then_inc(s["am_ok"], 1)
                    dve.wait_ge(s["ds_ok"], c + 1)
                    dve.wait_ge(s["smid_ok"], c + 1)
                    nc.vector.tensor_tensor(state_sum[:], bank[0][:, 0:D].rearrange("p (h f) -> p h f", h=2),
                                            state_mid[:], ALU.add).then_inc(s["ssum_ok"], 1)
                    dve.wait_ge(s["ssum_ok"], c + 1)
                    dve.wait_ge(s["end_ok"], c + 1)
                    nc.vector.tensor_tensor(state[:], state_sum[:], end_mask[:], ALU.mult)\
                      .then_inc(s["state_ok"], 1)
                    if c:
                        finish_chunk(c - 1)
                    dve.wait_ge(s["otok_ok"], c + 1)
                    dve.wait_ge(s["dout_ok"], c + 1)
                    if c:
                        dve.wait_ge(s["onorm_ok"], c)
                    nc.vector.tensor_tensor(o_tok[:], bank[7][:, D:2 * D], decay_out[:, c % 2, :], ALU.mult)\
                      .then_inc(s["o1_ok"], 1)
                    dve.wait_ge(s["o1_ok"], c + 1)
                    nc.vector.bn_stats(o_stats[:], o_tok[:]).then_inc(s["ost_ok"], 1)
                    dve.wait_ge(s["ost_ok"], 2 * c + 1)
                    nc.vector.bn_aggr(o_mom[:], o_stats[:]).then_inc(s["ost_ok"], 1)
                    dve.wait_ge(s["tf_ok"], c + 1)
                    nc.vector.scalar_tensor_tensor(f_gate[:], tanh_f[:], 1.0, bank[5][:, 0:D], ALU.add, ALU.mult)\
                      .then_inc(s["f1_ok"], 1)
                    if c == NC - 1:
                        dve.wait_ge(s["rs2"], 1)
                        for b in range(NC - 1):
                            normalise2(b)
                    normalise_output(c)
                gated_output(NC - 1)
                dve.wait_ge(s["state_ok"], NC)
                nc.vector.memset(state[:], 0.0).then_inc(s["state_ok"], 1)
                finish_chunk(NC - 1)

                dve.wait_ge(s["rs2"], 2)
                normalise2(NC - 1)
                dve.wait_ge(s["qk2_ok"], 8)
                nc.vector.memset(k2_bf[:, :, 0:HALF], 0.0).then_inc(s["kbf_ok"], 1)
                nc.vector.memset(k2_bf[:, :, HALF + S:SH], 0.0).then_inc(s["kbf_ok"], 1)
                nc.vector.tensor_copy(k2_bf[:, :, HALF:HALF + S], kt[:]).then_inc(s["kbf_ok"], 1)
                dve.wait_ge(s["v2p_ok"], 1)
                for g in range(2):
                    nc.vector.tensor_tensor(
                        v2[:, :, g, 0:DH],
                        bank[0][:].rearrange("p (w g d) -> p w g d", g=2, d=DH)[:, :, g, :],
                        bc_v2[:, g * DH:(g + 1) * DH].unsqueeze(1).broadcast_to([P, 2 * NC, DH]), ALU.add)\
                      .then_inc(s["v2_ok"], 1)
                dve.wait_ge(s["v2_ok"], 2)
                nc.vector.memset(v2[0:HALF, 0, :, 0:DH], 0.0).then_inc(s["v2_ok"], 1)
                nc.vector.memset(v2[P - HALF:P, 2 * NC - 1, :, 0:DH], 0.0).then_inc(s["v2_ok"], 1)

                def low_rank(g):
                    dve.wait_ge(s["tp_ok"], g + 1)
                    t_bank = bank[0 if g else 7]
                    nc.vector.tensor_copy(t_hi, t_bank[:]).then_inc(s["thi_ok"], 1)
                    if g:
                        dve.wait_ge(s["h2p_ok"], MT * g)
                    nc.vector.tensor_copy(t_st[0:64, :], t_bank[0:64, :]).then_inc(s["tst_ok"], 1)
                    dve.wait_ge(s["thi_ok"], g + 1)
                    nc.vector.tensor_tensor(t_st[64:128, :], t_bank[64:128, :], t_hi[64:128, :].bitcast(F32),
                                            ALU.subtract).then_inc(s["tst_ok"], 1)

                def maxima(c, half):
                    for r in range(4 * half, 4 * half + 4):
                        dve.wait_ge(s["sc_ok"], 8 * c + r + 1)
                        if c >= 2 and r == 0:
                            dve.wait_ge(s["dmax_ok"], 2 * c - 2)
                        nc.vector.tensor_reduce(neg_max[:, c % 2, 2 * r:2 * r + 2],
                                                bank[1 + r % 4][:, 0:2 * KW].rearrange("p (h k) -> p h k", k=KW),
                                                AX.X, ALU.max, negate=True).then_inc(s["max_ok"], 1)
                    dve.wait_ge(s["max_ok"], 8 * c + 4 * half + 4)
                    if c >= 2:
                        dve.wait_ge(s["stp_ok"], 4 * c - 6 + 2 * half)
                    nc.vector.tensor_tensor(
                        diag_max[c % 2][:, half * HH:(half + 1) * HH, :],
                        same_q[:].unsqueeze(1).broadcast_to([P, HH, QB]),
                        neg_max[:, c % 2, half * HH:(half + 1) * HH].unsqueeze(2).broadcast_to([P, HH, QB]),
                        ALU.mult).then_inc(s["dmax_ok"], 1)

                def attention_out(c):
                    dve.wait_ge(s["pv_ok"], 4 * c + 4)
                    if c:
                        dve.wait_ge(s["o2_ok"], c)
                    o_bank = bank[7][:, 0:H * DV].rearrange("p (h d) -> p h d", d=DV)
                    nc.vector.reciprocal(rden[:], o_bank[:, :, DH]).then_inc(s["rden_ok"], 1)
                    dve.wait_ge(s["rden_ok"], c + 1)
                    if c:
                        dve.wait_ge(s["o2tp_ok"], c)
                    nc.vector.tensor_tensor(o2.rearrange("p (h d) -> p h d", d=DH), o_bank[:, :, 0:DH],
                                            rden[:].unsqueeze(2).broadcast_to([P, H, DH]), ALU.mult)\
                      .then_inc(s["o2_ok"], 1)

                def attention_bias(c):
                    dve.wait_ge(s["s2p_ok"], c + 1)
                    nc.vector.tensor_tensor(attn2[:, c, :], bank[0][:, D:2 * D], bc_o2[:], ALU.add)\
                      .then_inc(s["s2_ok"], 1)

                maxima(0, 0)
                maxima(0, 1)
                low_rank(0)
                for g in range(NG):
                    nc.vector.tensor_copy(xh[:, g], xt[:, :, g * 512:(g + 1) * 512]).then_inc(s["xh_ok"], 1)
                for c in range(NC):
                    if c:
                        attention_out(c - 1)
                        attention_bias(c - 1)
                    if c + 1 < NC:
                        maxima(c + 1, 0)
                        maxima(c + 1, 1)
                attention_out(NC - 1)
                attention_bias(NC - 1)

                def finish2(c):
                    dve.wait_ge(s["tf2_ok"], c + 1)
                    if c:
                        dve.wait_ge(s["f4_ok"], c)
                    nc.vector.scalar_tensor_tensor(f_gate[:], tanh_f[:], 1.0, bank[7 if c % 2 else 4][:, 0:D],
                                                   ALU.add, ALU.mult).then_inc(s["f3_ok"], 1)
                    dve.wait_ge(s["f3_ok"], c + 1)
                    if c:
                        dve.wait_ge(s["y2_ok"], c)
                    nc.vector.scalar_tensor_tensor(sf[:], f_gate[:], 0.5, attn2[:, c, :], ALU.mult, ALU.mult)\
                      .then_inc(s["f4_ok"], 1)
                    dve.wait_ge(s["f4_ok"], c + 1)
                    nc.vector.tensor_add(x[:, c, :], x[:, c, :], sf[:]).then_inc(s["y2_ok"], 1)

                for n in range(NG * MT + 1):
                    if MT + 3 <= n < MT + 7:
                        finish2(n - MT - 3)
                    if n < NG * MT:
                        dve.wait_ge(s["sqh_ok"], n + 1)
                        if n >= 2:
                            dve.wait_ge(s["pj_ok"], n - 1)
                        nc.vector.tensor_tensor(sq_lo[:, n % 2, :], sq[:, n % 2, :],
                                                sq_hi[:, n % 2, :].bitcast(F32), ALU.subtract)\
                          .then_inc(s["sql_ok"], 1)
                    if n == MT - 2:
                        low_rank(1)
                    if n >= MT and n < 2 * MT:
                        head_stats(dve, n - MT)
                head_moments(dve)
                for c in range(NC):
                    head_normalise(dve, c)
                for c in range(4, NC):
                    finish2(c)

            @block.tensor
            def _(pe):
                def token_major(dst, c, w):
                    for k in range(KD):
                        mm = nc.tensor.matmul(dst, xt[:, k, c * P:(c + 1) * P], w[:, k, :], start=(k == 0),
                                              stop=(k == KD - 1))
                    return mm

                for i in range(NC // 2):
                    if i >= 2:
                        pe.wait_ge(s["zb_ok"], i - 1)
                    for b in range(2):
                        mm = token_major(bank[i % 2][:, b * D:(b + 1) * D], 2 * i + b, w_z)
                    mm.then_inc(s["zp_ok"], 1)
                for c in range(NC):
                    mm = token_major(bank[3][:, c * E:(c + 1) * E], c, w_gate)
                mm.then_inc(s["lg_ok"], 1)
                for n in range(8):
                    g, which, half = n // 4, n // 2 % 2, n % 2
                    if n >= 4:
                        pe.wait_ge(s["qk_ok"], n - 3)
                    w = w_k if which else w_q
                    for k in range(KD):
                        mm = nc.tensor.matmul(bank[4 + n % 4][:], w[:, k, half * P:(half + 1) * P],
                                              xt[:, k, g * 512:(g + 1) * 512], start=(k == 0), stop=(k == KD - 1))
                    mm.then_inc(s["qkp_ok"], 1)

                def cumulate(c):
                    pe.wait_ge(s["gk_ok"], c // 2 + 1)
                    if c == 0:
                        pe.wait_ge(s["lgc_ok"], 1)
                        pe.wait_ge(s["qk_ok"], 5)
                    else:
                        pe.wait_ge(s["dst_ok"], c)
                    nc.tensor.matmul(bank[3][:, 0:D], cum_mid[:], gk[:, c, :], start=True, stop=True)
                    nc.tensor.matmul(bank[4][:, 0:D], first_half[:], gk[:, c, :], start=True, stop=True)
                    nc.tensor.matmul(bank[4][:, D:2 * D], second_half[:], gk[:, c, :], start=True, stop=True)\
                      .then_inc(s["cum_ok"], 1)

                cumulate(0)
                pe.wait_ge(s["zb_ok"], NC // 2)
                pe.wait_ge(s["gates_ok"], 1)
                for b in range(2):
                    for j in range(4):
                        mm = nc.tensor.transpose(bank[1 + b][:, j * P:(j + 1) * P], gates[:, 4 * b + j, :], ident[:])
                    mm.then_inc(s["gtp_ok"], 1)

                def output_turn(c):
                    pe.wait_ge(s["y_ok"], c + 1)
                    for k in range(KD):
                        mm = nc.tensor.transpose(bank[7][:, k * P:(k + 1) * P], y_tok[:, k * P:(k + 1) * P],
                                                 ident[:])
                    mm.then_inc(s["ytp_ok"], 1)

                def output_project(c):
                    pe.wait_ge(s["yt_ok"], c + 1)
                    for k in range(KD):
                        mm = nc.tensor.matmul(bank[6][:, 0:D], yt[:, k, :], w_out[:, k, :], start=(k == 0),
                                              stop=(k == KD - 1))
                    mm.then_inc(s["s_ok"], 1)

                for c in range(NC):
                    if c:
                        pe.wait_ge(s["state_ok"], c)
                    token_major(bank[0][:], c, w_vg).then_inc(s["vg_ok"], 1)
                    pe.wait_ge(*((s["ktok_ok"], c) if c else (s["gt_ok"], 1)))
                    token_major(bank[1][:, 0:D], c, w_k).then_inc(s["kp_ok"], 1)
                    pe.wait_ge(*((s["hgt_ok"], c) if c else (s["gt_ok"], 2)))
                    token_major(bank[2][:], c, w_down).then_inc(s["hp_ok"], 1)
                    for j in range(4):
                        half = j // 2
                        if c == 0 and j == 0:
                            pe.wait_ge(s["qk_ok"], 8)
                        if j >= 2:
                            pe.wait_ge(s["am_ok"], 4 * c + j - 1)
                        elif j == 0 and c:
                            pe.wait_ge(s["f1_ok"], c)
                        elif j == 1 and c >= 2:
                            pe.wait_ge(s["f2_ok"], c - 1)
                        pe.wait_ge(s["qx_ok"], 2 * c + half + 1)
                        nc.tensor.matmul(bank[5 + j % 2][:], kt[:, half, c * P:(c + 1) * P],
                                         qx[:, c % 2, 4 * j:4 * j + 4, :], start=True, stop=True)\
                          .then_inc(s["at_ok"], 1)
                    if c:
                        output_turn(c - 1)
                    pe.wait_ge(s["hg_ok"], c + 1)
                    for j in range(EB // P):
                        mm = nc.tensor.transpose(bank[2][:, j * P:(j + 1) * P], hg[:, j * P:(j + 1) * P], ident[:])
                    mm.then_inc(s["hgtp_ok"], 1)
                    if c + 1 < NC:
                        cumulate(c + 1)
                    pe.wait_ge(s["am_ok"], 4 * c + 4)
                    if c:
                        output_project(c - 1)
                    pe.wait_ge(s["vt_ok"], c + 1)
                    pe.wait_ge(s["smid_ok"], c + 1)
                    for half in range(2):
                        nc.tensor.matmul(bank[7][:, half * P:(half + 1) * P], state_mid[:, half, :],
                                         qt[:, half, c * P:(c + 1) * P], start=True, stop=False,
                                         skip_group_check=True)
                        for e in range(2):
                            for j in range(4):
                                mm = nc.tensor.matmul(bank[7][32 * j:32 * j + 32, half * P:(half + 1) * P],
                                                      vt[:, half * 4 + j, 2 * e:2 * e + 2, :],
                                                      am[:, half * HH + 2 * j + e, :], start=False, stop=(e == 1),
                                                      skip_group_check=True)
                    mm.then_inc(s["ot_ok"], 1)
                    pe.wait_ge(s["ktok_ok"], c + 1)
                    pe.wait_ge(s["sg_ok"], c + 1)
                    for half in range(2):
                        mm = nc.tensor.matmul(bank[0][:, half * P:(half + 1) * P], ktok[:, half * P:(half + 1) * P],
                                              vt[:, half * 4:half * 4 + 4, 0:4:3, :], start=True, stop=True)
                    mm.then_inc(s["ds_ok"], 1)
                    pe.wait_ge(s["hgt_ok"], c + 1)
                    for j in range(EB // P):
                        nc.tensor.matmul(bank[5][:, 0:D], hgt[:, j, :], w_up[:, j, :], start=(j == 0), stop=False)
                    nc.tensor.matmul(bank[5][:, 0:D], gates_t[:, c, :], b_up[:], start=False, stop=True)\
                      .then_inc(s["f_ok"], 1)
                    pe.wait_ge(s["ots_ok"], c + 1)
                    for k in range(KD):
                        mm = nc.tensor.transpose(bank[7][:, D + k * P:D + (k + 1) * P], ot[:, k, :], ident[:])
                    mm.then_inc(s["otok_ok"], 1)

                def chunk_turn(c):
                    pe.wait_ge(s["xn2_ok"], c + 1)
                    if c >= 2:
                        pe.wait_ge(s["xt2_ok"], c - 1)
                    for k in range(KD):
                        mm = nc.tensor.transpose(bank[3 * (c % 2)][:, k * P:(k + 1) * P],
                                                 xn[:, c, k * P:(k + 1) * P], ident[:])
                    mm.then_inc(s["xt2p_ok"], 1)

                def queries_keys(n):
                    g, which, half = n // 4, n // 2 % 2, n % 2
                    pe.wait_ge(s["xt2_ok"], 4 * g + 4)
                    if n >= 3:
                        pe.wait_ge(s["qk2_ok"], n - 2)
                    for k in range(KD):
                        w = w_k2r[:, k, half].rearrange("p r d -> p (r d)") if which \
                            else w_q2[:, k, half * P:(half + 1) * P]
                        mm = nc.tensor.matmul(bank[(1, 2, 4)[n % 3]][:], w, xt[:, k, g * 512:(g + 1) * 512],
                                              start=(k == 0), stop=(k == KD - 1))
                    mm.then_inc(s["qk2p_ok"], 1)

                pe.wait_ge(s["state_ok"], NC)
                for c in range(NC - 1):
                    chunk_turn(c)
                for n in range(4):
                    queries_keys(n)
                output_turn(NC - 1)
                output_project(NC - 1)
                chunk_turn(NC - 1)
                for n in range(4, 8):
                    queries_keys(n)
                for w in range(2 * NC):
                    for k in range(KD):
                        mm = nc.tensor.matmul(bank[0][:, w * 2 * DH:(w + 1) * 2 * DH],
                                              xt2[:, k, w * QB:w * QB + P], w_kv2[:, k, 1, :], start=(k == 0),
                                              stop=(k == KD - 1))
                mm.then_inc(s["v2p_ok"], 1)

                def low_rank(g):
                    for k in range(KD):
                        mm = nc.tensor.matmul(bank[0 if g else 7][:], w_low[:, k, :],
                                              xt[:, k, g * 512:(g + 1) * 512], start=(k == 0), stop=(k == KD - 1))
                    mm.then_inc(s["tp_ok"], 1)

                def attention_turn(c):
                    pe.wait_ge(s["o2_ok"], c + 1)
                    if c:
                        pe.wait_ge(s["s2_ok"], c)
                    for k in range(KD):
                        mm = nc.tensor.transpose(bank[0][:, k * P:(k + 1) * P], o2[:, k * P:(k + 1) * P], ident[:])
                    mm.then_inc(s["o2tp_ok"], 1)

                def attention_project(c):
                    pe.wait_ge(s["o2t_ok"], c + 1)
                    for k in range(KD):
                        mm = nc.tensor.matmul(bank[0][:, D:2 * D], o2t[:, k * P:(k + 1) * P], w_o2[:, k, :],
                                              start=(k == 0), stop=(k == KD - 1))
                    mm.then_inc(s["s2p_ok"], 1)

                def rough_scores(c, half):
                    pe.wait_ge(s["qxb_ok"], 2 * c + half + 1)
                    for r in range(4 * half, 4 * half + 4):
                        n = 8 * c + r
                        if n >= 4:
                            pe.wait_ge(s["max_ok"], n - 3)
                        nc.tensor.matmul(bank[1 + r % 4][:, 0:2 * KW], ident_bf[:],
                                         chunk_band[:].unsqueeze(1).broadcast_to([P, 2, KW]), start=True,
                                         stop=False, skip_group_check=True)
                        for j in range(2):
                            mm = nc.tensor.matmul(bank[1 + r % 4][:, j * KW:(j + 1) * KW], qx_bf[:, 2 * r + j, :],
                                                  k2_bf[:, r // 4, c * P:c * P + KW], start=False, stop=True,
                                                  skip_group_check=True)
                        mm.then_inc(s["sc_ok"], 1)

                def scores(n):
                    c, g, b = n // 4, n // 2 % 2, n % 2
                    if n >= 2:
                        pe.wait_ge(s["pr_ok"], n - 1)
                    pe.wait_ge(s["dmax_ok"], 2 * c + g + 1)
                    st = bank[5 + n % 2][:]
                    nc.tensor.matmul(st, block_band[:, b, :], same_q[:].unsqueeze(1).broadcast_to([P, HH, QB]),
                                     start=True, stop=False)
                    nc.tensor.matmul(st, block_ones[:, b, :], diag_max[c % 2][:, g * HH:(g + 1) * HH, :],
                                     start=False, stop=False)
                    nc.tensor.matmul(st, k2[:, g, c * P + b * QB:c * P + b * QB + P],
                                     qx[:, c % 2, g * HH:(g + 1) * HH, b * QB:(b + 1) * QB], start=False, stop=True)\
                      .then_inc(s["stp_ok"], 1)

                def values(n):
                    c, g, b = n // 4, n // 2 % 2, n % 2
                    pe.wait_ge(s["pr_ok"], n + 1)
                    if n % 4 == 0 and c:
                        pe.wait_ge(s["o2_ok"], c)
                    for h in range(HH):
                        col = (g * HH + h) * DV
                        mm = nc.tensor.matmul(bank[7][b * QB:(b + 1) * QB, col:col + DV], pr[:, n % 2, h, :],
                                              v2[:, 2 * c + b, g, :], start=True, stop=True)
                    mm.then_inc(s["pv_ok"], 1)

                pe.wait_ge(s["kbf_ok"], 3)
                rough_scores(0, 0)
                rough_scores(0, 1)
                pe.wait_ge(s["yt_ok"], NC)
                low_rank(0)
                pe.wait_ge(s["tst_ok"], 2)
                pe.wait_ge(s["v2_ok"], 4)
                for c in range(NC):
                    scores(4 * c)
                    if c:
                        attention_turn(c - 1)
                    scores(4 * c + 1)
                    values(4 * c)
                    if c:
                        attention_project(c - 1)
                    if c + 1 < NC:
                        rough_scores(c + 1, 0)
                    scores(4 * c + 2)
                    values(4 * c + 1)
                    if c + 1 < NC:
                        rough_scores(c + 1, 1)
                    scores(4 * c + 3)
                    values(4 * c + 2)
                    values(4 * c + 3)

                def hidden(n, part):
                    g, m = n // MT, n % MT
                    h_bank = bank[1 + n % 3][:]
                    if part == 0:
                        if n >= 3:
                            pe.wait_ge(s["relu_ok"], n - 2)
                        if m == 0:
                            pe.wait_ge(s["xl_ok"], g + 1)
                        for t in (xh, xl):
                            for k in range(KD):
                                nc.tensor.matmul(h_bank, fc_t[:, k, m * P:(m + 1) * P], t[:, g, k, :],
                                                 start=(t is xh and k == 0), stop=False)
                    else:
                        if m == 0:
                            pe.wait_ge(s["tst_ok"], 2 * g + 2)
                        nc.tensor.matmul(h_bank, u_t[:, m * P:(m + 1) * P], t_st[:], start=False, stop=True)\
                          .then_inc(s["h2p_ok"], 1)

                def project(n):
                    m = n % MT
                    pe.wait_ge(s["sql_ok"], n + 1)
                    if n == MT:
                        pe.wait_ge(s["ft_ok"], KD)
                    for o in range(KD):
                        for part in (sq_hi, sq_lo):
                            mm = nc.tensor.matmul(bank[5 + o][:], pj_t[:, m, o * P:(o + 1) * P], part[:, n % 2, :],
                                                  start=(m == 0 and part is sq_hi),
                                                  stop=(m == MT - 1 and part is sq_lo), skip_group_check=True)
                    mm.then_inc(s["pj_ok"], 1)

                def ffn_turn(c):
                    if c % 4 == 0:
                        pe.wait_ge(s["ft_ok"], KD * (c // 4 + 1))
                    if c >= 2:
                        pe.wait_ge(s["f3_ok"], c - 1)
                    j = c % 4
                    for k in range(KD):
                        mm = nc.tensor.transpose(bank[7 if c % 2 else 4][:, k * P:(k + 1) * P],
                                                 ft[:, k, j * P:(j + 1) * P], ident[:])
                    mm.then_inc(s["ftp_ok"], 1)

                for n in range(NG * MT):
                    hidden(n, 0)
                    if n == MT:
                        project(n - 2)
                    hidden(n, 1)
                    if n == 0:
                        attention_turn(NC - 1)
                    if n == 1:
                        attention_project(NC - 1)
                    if n == 4:
                        pe.wait_ge(s["s2_ok"], NC)
                        low_rank(1)
                    if n >= 2 and n != MT:
                        project(n - 2)
                    if MT + 2 <= n < MT + 6:
                        ffn_turn(n - MT - 2)
                project(NG * MT - 2)
                project(NG * MT - 1)
                pe.wait_ge(s["tst_ok"], 4)
                pe.wait_ge(s["relu_ok"], NG * MT)
                for c in range(NC):
                    head_turn(pe, c)
                    if c % 2:
                        ffn_turn(4 + c // 2)

        nc.all_engine_barrier(sems_to_clear=range(first, last + 1))
    ctx.close()


_OUT = (16, S, D)


def kernel(**inputs):
    import concourse.bacc as bacc
    from concourse.bass_utils import run_bass_kernel_spmd

    nc = bacc.Bacc("TRN2", target_bir_lowering=False, num_devices=1, dynamic_dma_scratch_size=1024)
    arrays, args = {}, {}
    for name, value in inputs.items():
        v = np.ascontiguousarray(value)
        v = v.reshape(v.shape or (1,))
        arrays[f"in_{name}"] = v
        args[name] = nc.dram_tensor(f"in_{name}", v.shape, mybir.dt.from_np(v.dtype), kind="ExternalInput").ap()
    out = nc.dram_tensor("out_0", _OUT, F32, kind="ExternalOutput").ap()
    build_program(nc, args, out, _OUT[0])
    result = run_bass_kernel_spmd(nc, [arrays], core_ids=[0])
    return result.results[0]["out_0"]
```

```python
from contextlib import ExitStack

import numpy as np
import concourse.bass as bass
from concourse import mybir

F32 = mybir.dt.float32
F32R = mybir.dt.float32r
BF16 = mybir.dt.bfloat16
U32 = mybir.dt.uint32
ALU = mybir.AluOpType
ACT = mybir.ActivationFunctionType
AX = mybir.AxisListType

P = 128
D = 256
KD = D // P
S = 1024
NC = S // P
NG = S // 512
H = 16
DH = D // H
HH = H // 2
E = 8
BN = 64
EB = E * BN
RANK = 16
QB = 64
WIN = 64
HALF = WIN // 2
KW = 192
HID = 1024
MT = HID // P
EPS = 1e-5
BIG = -1e30
DV = DH + 1


def build_program(nc, a, out, n_seq):
    ctx = ExitStack()
    ctx.enter_context(nc.allow_non_contiguous_dma(reason="small transposed weights"))

    def sb(name, shape, dt=F32):
        return ctx.enter_context(nc.sbuf_tensor(name, shape, dt))

    def sem(name):
        return ctx.enter_context(nc.semaphore(name))

    x_dram = a["L0_attn_x"].rearrange("b (c p) d -> (b c) p d", p=P)
    out_dram = out.rearrange("b (c p) d -> (b c) p d", p=P)

    ident = sb("ident", [P, P])
    causal = sb("causal", [P, P])
    cumulator = sb("cumulator", [P, 3, P], F32R)
    head_block = sb("head_block", [P, P])
    head_mask = sb("head_mask", [P, HH])
    expert_no = sb("expert_no", [P, E])
    minus_half = sb("minus_half", [P, NC])
    minus_same = sb("minus_same", [P, QB], BF16)
    same_q = sb("same_q", [P, QB], BF16)
    band_or_one = sb("band_or_one", [P, 2, P], BF16)
    chunk_band = sb("chunk_band", [P, KW], BF16)

    w_vg = sb("w_vg", [P, KD, 2 * D])
    w_k = sb("w_k", [P, KD, D])
    w_q = sb("w_q", [P, KD, D])
    w_z = sb("w_z", [P, KD, D + E])
    w_out = sb("w_out", [P, KD, D])
    w_down = sb("w_down", [P, KD, EB])
    w_up = sb("w_up", [P, EB // P, D])
    b_up = sb("b_up", [P, D], F32R)
    bc_gk = sb("bc_gk", [P, D])
    bc_gamma = sb("bc_gamma", [P, D])
    bc_beta = sb("bc_beta", [P, D])
    bc_down = sb("bc_down", [P, EB])

    x = sb("x", [P, NC, D])
    xn = sb("xn", [P, NC, D])
    SH = S + 2 * HALF
    xt2 = sb("xt2", [P, KD, SH])
    xt = xt2[:, :, HALF:HALF + S]
    qt = sb("qt", [P, KD, S])
    k2 = sb("k2", [P, 2, SH])
    kt = k2[:, :, HALF:HALF + S]
    attn2 = sb("attn2", [P, NC, D])
    stats = sb("stats", [P, NC, 6])
    moments = sb("moments", [P, NC, 2])
    veps = sb("veps", [P, NC])
    rstd = sb("rstd", [P, NC])
    logits = sb("logits", [P, NC, E])
    top = sb("top", [P, NC, E])
    top_i = sb("top_i", [P, NC, E], U32)
    top_f = sb("top_f", [P, NC, 2])
    gdiff = sb("gdiff", [P, NC])
    gexp = sb("gexp", [P, NC])
    gden = sb("gden", [P, NC])
    g_top = sb("g_top", [P, 2, NC])
    g_hit = sb("g_hit", [P, 2, NC, E])
    g_all = sb("g_all", [P, NC, E])
    g_hi = sb("g_hi", [P, NC, E], F32R)
    gates = sb("gates", [P, NC, P])

    qx = sb("qx", [P, 2, H, P])
    am = sb("am", [P, H, P])
    ktok = sb("ktok", [P, D])
    vt = sb("vt", [P, HH, 4, DH])
    decay_in = sb("decay_in", [P, 2, D])
    decay_out = sb("decay_out", [P, 2, D])
    decay_state = sb("decay_state", [P, 2, 2, D])
    end_mask = sb("end_mask", [P, 2, P])
    tanh_g = sb("tanh_g", [P, D])
    silu_g = sb("silu_g", [P, 2, D])
    hb = sb("hb", [P, EB])
    hg = sb("hg", [P, EB])
    hgt = sb("hgt", [P, EB // P, P])
    gates_t = sb("gates_t", [P, NC, P], F32R)
    state = sb("state", [P, 2, P])
    state_mid = sb("state_mid", [P, 2, P])
    state_sum = sb("state_sum", [P, 2, P])
    ot = sb("ot", [P, 2, P])
    o_tok = sb("o_tok", [P, D])
    o_stats = sb("o_stats", [P, 6])
    o_mom = sb("o_mom", [P, 2])
    o_veps = sb("o_veps", [P, 1])
    o_rstd = sb("o_rstd", [P, 1])
    o_norm = sb("o_norm", [P, D])
    o_gam = sb("o_gam", [P, D])
    o_bet = sb("o_bet", [P, D])
    y_tok = sb("y_tok", [P, D])
    yt = sb("yt", [P, KD, P])
    tanh_f = sb("tanh_f", [P, D])
    f_gate = sb("f_gate", [P, D])
    sf = sb("sf", [P, D])

    w_q2 = sb("w_q2", [P, KD, D])
    w_kv2 = sb("w_kv2", [P, KD, 2, 2 * DH])
    w_k2r = sb("w_k2r", [P, KD, 2, HH, DH])
    w_o2 = sb("w_o2", [P, KD, D])
    b_q2 = sb("b_q2", [P, 2])
    b_k2 = sb("b_k2", [P, 2])
    bc_v2 = sb("bc_v2", [P, 2 * DH])
    bc_o2 = sb("bc_o2", [P, D])
    fb_t = sb("fb_t", [RANK, RANK])
    ffn_gate = sb("ffn_gate", [P, 1])
    w_low = sb("w_low", [P, KD, P])
    scale_fc = sb("scale_fc", [P, MT])
    scale_pj = sb("scale_pj", [P, KD])
    thr = sb("thr", [P, 2, MT])
    rscale = sb("rscale", [P, MT])
    u_nat = sb("u_nat", [P, MT, RANK])
    u_hi = sb("u_hi", [P, MT, RANK], F32R)
    u_lo = sb("u_lo", [P, MT, RANK])
    fc_t = sb("fc_t", [P, KD, HID], F32R)
    pj_t = sb("pj_t", [P, MT, D], F32R)
    u_t = sb("u_t", [P, HID], F32R)

    xh = sb("xh", [P, NG, KD, 512], F32R)
    xl = sb("xl", [P, NG, KD, 512], F32R)
    gk_hi = xh[:].rearrange("p g k t -> p (g k t)").rearrange("p (c d) -> p c d", d=D)
    gk_lo = xl[:].rearrange("p g k t -> p (g k t)").rearrange("p (c d) -> p c d", d=D)
    q2 = qt
    x_next = qt[:].rearrange("p k t -> p (k t)").rearrange("p (c d) -> p c d", d=D)
    am_flat = am[:].rearrange("p h t -> p (h t)")
    k2_bf = am_flat[:, 0:SH].bitcast(BF16).rearrange("p (g k) -> p g k", g=2)
    v2 = sb("v2", [P, 2 * NC, 2, DV])
    qx_bf = decay_state[:].rearrange("p b a d -> p (b a d)").bitcast(BF16).rearrange("p (h t) -> p h t", t=P)
    row_max = sb("row_max", [P, 2, H])
    shift = sb("shift", [P, 2, 2, H, QB], BF16)
    pr = xn[:, 0:4, :].rearrange("p c d -> p (c d)").rearrange("p (b h q) -> p b h q", b=2, q=QB)
    rden = sb("rden", [P, H])
    o2 = am_flat[:, SH:SH + D]
    o2t = am_flat[:, SH + D:SH + 2 * D]
    t_hi = hb[:].bitcast(F32R)
    t_st = sb("t_st", [P, NG, 512], F32R)
    qx_flat = qx[:].rearrange("p b h t -> p (b h t)")
    relu = qx_flat[:, 0:3 * 512].rearrange("p (b t) -> p b t", b=3)
    sq = qx_flat[:, 3 * 512:6 * 512].rearrange("p (b t) -> p b t", b=3)
    sq_hi = sb("sq_hi", [P, 3, 512], F32R)
    sq_lo = sb("sq_lo", [P, 3, 512], F32R)
    ft = kt[:, :, 0:512]
    z, zact, gk = am_flat.rearrange("p (c d) -> p c d", d=D), xn, attn2
    gk1_t, gk2, v_nat = (am_flat[0:RANK, i * D:(i + 1) * D] for i in range(3))
    b_nat = am_flat[:, 3 * D + 3 * P:4 * D + 3 * P]
    cum_mid, first_half, second_half = (am_flat[:, 3 * D + i * P:3 * D + (i + 1) * P] for i in range(3))
    fc_nat, fc_ter, pj_ter = x, xn, kt
    pj_nat = attn2[:].rearrange("p c d -> p (c d)").rearrange("p (o h) -> p o h", o=KD)
    u_st = gates

    bank = [ctx.enter_context(nc.psum_tensor(f"bank{i}", [P, 512], F32)) for i in range(8)]

    w_sem, nat_sem, b_sem, cst, cleared = sem("w_sem"), sem("nat_sem"), sem("b_sem"), sem("cst"), sem("cleared")
    prep, prep_done, tern = sem("prep"), sem("prep_done"), sem("tern")

    loads = [
        (w_vg[:, :, 0:D], a["L0_attn_Wv"].rearrange("(k p) n -> p k n", p=P)),
        (w_vg[:, :, D:2 * D], a["L0_attn_Wg"].rearrange("(k p) n -> p k n", p=P)),
        (w_k[:], a["L0_attn_Wk"].rearrange("(k p) n -> p k n", p=P)),
        (w_q[:], a["L0_attn_Wq"].rearrange("(k p) n -> p k n", p=P)),
        (w_out[:], a["L0_attn_Wout"].rearrange("(k p) n -> p k n", p=P)),
        (w_z[:, :, D:D + E], a["L0_ffn_w_gate"].rearrange("(k p) n -> p k n", p=P)),
        (w_up[:], a["L0_ffn_Wu"].rearrange("(j e) b d -> (e b) j d", e=2)),
        (bc_gk[:], a["L0_attn_bgk2"].partition_broadcast(P)),
        (bc_gamma[:], a["L0_attn_gamma"].partition_broadcast(P)),
        (bc_beta[:], a["L0_attn_beta"].partition_broadcast(P)),
        (bc_down[:], a["L0_ffn_bd"].rearrange("e b -> (e b)").partition_broadcast(P)),
        (gk1_t[:], a["L0_attn_Wgk1"].rearrange("n r -> r n")),
        (gk2[:], a["L0_attn_Wgk2"]),
    ]
    loads += [
        (w_q2[:], a["L1_attn_Wq"].rearrange("(k p) n -> p k n", p=P)),
        (w_kv2[:, :, 0, :], a["L1_attn_Wk"].rearrange("(k p) n -> p k n", p=P)),
        (w_kv2[:, :, 1, :], a["L1_attn_Wv"].rearrange("(k p) n -> p k n", p=P)),
        (w_o2[:], a["L1_attn_Wo"].rearrange("(k p) n -> p k n", p=P)),
        (b_q2[:], a["L1_attn_bq"].rearrange("(k p) -> p k", p=P)),
        (bc_v2[:], a["L1_attn_bv"].partition_broadcast(P)),
        (bc_o2[:], a["L1_attn_bo"].partition_broadcast(P)),
        (v_nat[:], a["L1_ffn_v"]),
        (fb_t[:], a["L1_ffn_fast_b"].rearrange("j i -> i j")),
        (ffn_gate[:], a["L1_ffn_gate"].partition_broadcast(P)),
    ]
    nat_loads = [
        (fc_nat[:], a["L1_ffn_w_fc"].rearrange("(m p) d -> p m d", p=P)),
        (pj_nat, a["L1_ffn_w_proj"].rearrange("(o p) h -> p o h", p=P)),
        (u_nat[:], a["L1_ffn_u"].rearrange("(m p) r -> p m r", p=P)),
    ]
    for h in range(HH):
        loads.append((b_k2[h * DH:(h + 1) * DH, :], a["L1_attn_bk"].rearrange("(g d) -> d g", g=2)))
    for k in range(KD):
        loads.append((w_down[:, k, :].rearrange("p (e b) -> p e b", e=E),
                      a["L0_ffn_Wd"][:, k * P:(k + 1) * P, :].rearrange("e p b -> p e b")))

    names = ("xc_ok xtp_ok xt_ok zp_ok z_ok zabs_ok zexp_ok zln_ok gk_ok "
             "top_ok gsel gexp_ok gates_ok gtp_ok gt_ok qkp_ok qk_ok vg_ok kp_ok hp_ok hb_ok tg_ok sg_ok hg_ok ktok_ok "
             "qx_ok at_ok am_ok cum_ok din_ok dout_ok dst_ok vt_ok smid_ok end_ok ds_ok ssum_ok state_ok ot_ok "
             "ots_ok otok_ok o1_ok ost_ok ove_ok ors_ok onorm_ok ogam_ok obet_ok y_ok ytp_ok yt_ok s_ok hgtp_ok "
             "hgt_ok f_ok tf_ok f1_ok f2_ok x_ok "
             "st2 ve2 rs2 xn2_ok xt2p_ok xt2_ok qk2p_ok qk2_ok kbf_ok v2p_ok v2_ok qx2_ok qxb_ok sc_ok max_ok dmax_ok "
             "stp_ok pr_ok pv_ok rden_ok o2_ok o2tp_ok o2t_ok s2p_ok s2_ok xh_ok xl_ok tp_ok thi_ok tst_ok h2p_ok "
             "relu_ok sq_ok sqh_ok sql_ok pj_ok ft_ok ftp_ok tf2_ok f3_ok f4_ok y2_ok gkh_ok gkl_ok nst_ok nve_ok nrs_ok "
             "nxn_ok").split()
    s = {n: sem(n) for n in names}
    turn_banks = (0, 3, 0, 3, 0, 3, 0, 7)
    qk_banks = (1, 2, 4, 1, 5, 6, 5, 6)
    x_in = [sem(f"x_in{c}") for c in range(NC)]
    out_done = sem("out_done")
    first, last = s[names[0]].num, x_in[-1].num

    head_banks = {"before": ((4, 5, 6, 7, 4, 5, 6, 7), (0, 1, 2, 3, 0, 1, 2, 3)),
                  "body": ((0, 0, 0, 0, 0, 0, 0, 0), (0, 0, 0, 0, 1, 2, 3, 1))}

    def head_load(sp, index):
        for c in range(NC):
            sp.dma_start(x_next[:, c, :], x_dram[bass.ds(index * NC + c, 1), :, :].rearrange("o p d -> (o p) d"))\
              .then_inc(x_in[c], 16)

    def head_stats(dve, c):
        dve.wait_ge(x_in[c], 16)
        nc.vector.bn_stats(stats[:, c, :], x_next[:, c, :]).then_inc(s["nst_ok"], 1)

    def head_moments(dve):
        dve.wait_ge(s["nst_ok"], NC)
        for c in range(NC):
            nc.vector.bn_aggr(moments[:, c, :], stats[:, c, :]).then_inc(s["nst_ok"], 1)

    def head_rstd(pool):
        pool.wait_ge(s["nst_ok"], 2 * NC)
        nc.gpsimd.tensor_scalar(veps[:], moments[:, :, 1], EPS, None, ALU.add).then_inc(s["nve_ok"], 1)
        pool.wait_ge(s["nve_ok"], 1)
        nc.gpsimd.tensor_tensor(rstd[:], veps[:], minus_half[:], ALU.pow).then_inc(s["nrs_ok"], 1)

    def head_normalise(dve, c):
        if c == 0:
            dve.wait_ge(s["nrs_ok"], 1)
        nc.vector.tensor_scalar(xn[:, c, :], x_next[:, c, :], moments[:, c, 0:1], rstd[:, c:c + 1],
                                ALU.subtract, ALU.mult).then_inc(s["nxn_ok"], 1)

    def head_turn(pe, c, where="body"):
        turned = bank[head_banks[where][0][c]]
        pe.wait_ge(s["nxn_ok"], c + 1)
        if where == "before":
            if c >= 4:
                pe.wait_ge(s["xt_ok"], c - 3)
        elif c > 4:
            pe.wait_ge(s["xt_ok"], c)
        elif c:
            pe.wait_ge(s["z_ok"], 2 * c)
        for k in range(KD):
            mm = nc.tensor.transpose(turned[:, k * P:(k + 1) * P], xn[:, c, k * P:(k + 1) * P], ident[:])
        mm.then_inc(s["xtp_ok"], 1)

    def head_turned(act, c, where="body"):
        turned = bank[head_banks[where][0][c]]
        act.wait_ge(s["xtp_ok"], c + 1)
        nc.scalar.copy(xt[:, :, c * P:(c + 1) * P], turned[:, 0:D].rearrange("p (k t) -> p k t", k=KD))\
          .then_inc(s["xt_ok"], 1)

    def head_project(pe, c, where="body"):
        out = bank[head_banks[where][1][c]]
        pe.wait_ge(s["xt_ok"], c + 1)
        if where == "before" and c >= 4:
            pe.wait_ge(s["z_ok"], 2 * (c - 3))
        elif c == 7:
            pe.wait_ge(s["z_ok"], 10)
        for cols in (slice(0, D), slice(D, D + E)):
            for k in range(KD):
                mm = nc.tensor.matmul(out[:, cols], xt[:, k, c * P:(c + 1) * P], w_z[:, k, cols],
                                      start=(k == 0), stop=(k == KD - 1))
        mm.then_inc(s["zp_ok"], 1)

    def head_logits(dve, c, where="body"):
        out = bank[head_banks[where][1][c]]
        dve.wait_ge(s["zp_ok"], c + 1)
        nc.vector.tensor_tensor(z[:, c, :], out[:, 0:D], bc_gk[:], ALU.add).then_inc(s["z_ok"], 1)
        nc.vector.tensor_copy(logits[:, c, :], out[:, D:D + E]).then_inc(s["z_ok"], 1)

    with nc.Block() as block:

        @block.gpsimd
        def _(pool):
            done = [0]

            def link(ins):
                done[0] += 1
                ins.then_inc(cst, 1)
                pool.wait_ge(cst, done[0])

            def band(tile, width):
                link(nc.gpsimd.affine_select(out=tile, in_=tile, compare_op=ALU.is_ge, fill=BIG, base=0,
                                             pattern=[[1, width]], channel_multiplier=-1))
                link(nc.gpsimd.affine_select(out=tile, in_=tile, compare_op=ALU.is_ge, fill=BIG, base=WIN - 1,
                                             pattern=[[-1, width]], channel_multiplier=1))

            for t in (ident, second_half, same_q, band_or_one, chunk_band, gates, vt,
                      state, xt2, k2, w_low):
                link(nc.gpsimd.memset(t[:], 0.0))
            for t in (causal, head_block, head_mask, first_half):
                link(nc.gpsimd.memset(t[:], 1.0))
            nc.gpsimd.memset(minus_half[:], -0.5).then_inc(cleared, 1)
            link(nc.gpsimd.memset(v2[:], 1.0))
            link(nc.gpsimd.affine_select(out=ident[:], in_=ident[:], compare_op=ALU.not_equal, fill=1.0, base=0,
                                         pattern=[[-1, P]], channel_multiplier=1))
            for base in (0, -QB):
                link(nc.gpsimd.affine_select(out=same_q[:], in_=same_q[:], compare_op=ALU.not_equal, fill=1.0,
                                             base=base, pattern=[[-1, QB]], channel_multiplier=1))
            link(nc.gpsimd.affine_select(out=causal[:], in_=causal[:], compare_op=ALU.is_ge, fill=0.0, base=0,
                                         pattern=[[1, P]], channel_multiplier=-1))
            link(nc.gpsimd.tensor_copy(cum_mid[:], causal[:]))
            link(nc.gpsimd.tensor_scalar(cum_mid[0:QB, :], cum_mid[0:QB, :], -1.0, None, ALU.add))
            link(nc.gpsimd.memset(first_half[QB:P, :], 0.0))
            link(nc.gpsimd.memset(second_half[QB:P, :], 1.0))
            for i, t in enumerate((cum_mid, first_half, second_half)):
                link(nc.gpsimd.tensor_copy(cumulator[:, i, :], t[:]))
            blocks = head_block[:].rearrange("p (h d) -> p h d", d=DH)
            for t, tail in ((blocks, [[0, DH]]), (head_mask[:], [])):
                link(nc.gpsimd.affine_select(out=t, in_=t, compare_op=ALU.is_ge, fill=0.0, base=0,
                                             pattern=[[-DH, HH]] + tail, channel_multiplier=1))
                link(nc.gpsimd.affine_select(out=t, in_=t, compare_op=ALU.is_ge, fill=0.0, base=DH - 1,
                                             pattern=[[DH, HH]] + tail, channel_multiplier=-1))
            for b in range(2):
                link(nc.gpsimd.memset(band_or_one[QB * b:QB * (b + 1), b, :], 1.0))
                rest = slice(QB * (1 - b), QB * (2 - b))
                band(band_or_one[rest, b, :], P)
            link(nc.gpsimd.tensor_scalar(minus_same[:], same_q[:], -1.0, None, ALU.mult))
            band(chunk_band[:], KW)
            for e in range(E):
                link(nc.gpsimd.memset(expert_no[:, e:e + 1], float(e)))

        @block.vector
        def _(dve):
            nc.vector.memset(b_nat, 0.0).then_inc(prep, 1)
            done = [0]

            def link(ins):
                done[0] += 1
                ins.then_inc(tern, 1)
                dve.wait_ge(tern, done[0])

            dve.wait_ge(nat_sem, 16 * len(nat_loads))
            dve.wait_ge(cleared, 1)
            for nat, ter, scale, n, width in ((fc_nat[:], fc_ter, scale_fc, MT, D), (pj_nat, pj_ter, scale_pj, KD, HID)):
                link(nc.vector.tensor_reduce(scale[:], nat, AX.X, ALU.add, apply_absolute_value=True))
                link(nc.vector.tensor_scalar(scale[:], scale[:], 1.0 / width, 1e-5, ALU.mult, ALU.max))
                link(nc.vector.tensor_scalar(thr[:, 0, 0:n], scale[:], 0.5, None, ALU.mult))
                link(nc.vector.tensor_scalar(thr[:, 1, 0:n], scale[:], -0.5, None, ALU.mult))
                for m in range(n):
                    link(nc.vector.tensor_scalar(ter[:, m, :], nat[:, m, :], thr[:, 1, m:m + 1], None, ALU.is_lt))
                    link(nc.vector.scalar_tensor_tensor(ter[:, m, :], nat[:, m, :], thr[:, 0, m:m + 1],
                                                        ter[:, m, :], ALU.is_gt, ALU.subtract))
            link(nc.vector.reciprocal(rscale[:], scale_fc[:]))
            link(nc.vector.tensor_tensor(u_nat[:], u_nat[:], rscale[:].unsqueeze(2).broadcast_to([P, MT, RANK]),
                                         ALU.mult))
            link(nc.vector.tensor_copy(u_hi[:], u_nat[:]))
            link(nc.vector.tensor_tensor(u_lo[:], u_nat[:], u_hi[:].bitcast(F32), ALU.subtract))
            for r in (0, 2):
                link(nc.vector.tensor_copy(u_st[:, :, 32 * r:32 * r + RANK], u_hi[:].bitcast(F32)))
                link(nc.vector.tensor_copy(u_st[:, :, 32 * r + 32:32 * r + 32 + RANK], u_lo[:]))
            dve.wait_ge(b_sem, 16 * 4)
            link(nc.vector.tensor_copy(b_up[:], b_nat))
            for r in (1, 3):
                rows = slice(32 * r, 32 * r + 32)
                link(nc.vector.tensor_tensor(b_up[rows, :], b_nat[rows, :], b_up[rows, :].bitcast(F32),
                                             ALU.subtract))
            dve.wait_ge(prep_done, 2)
            for k in range(KD):
                nc.vector.tensor_copy(w_z[:, k, 0:D], bank[k][:, 0:D])
            for k in range(KD):
                for r in range(4):
                    nc.vector.tensor_scalar(w_low[:, k, 32 * r:32 * r + RANK], bank[2 + k][:, 0:RANK],
                                            ffn_gate[:], None, ALU.mult)
            for k in range(KD):
                nc.vector.tensor_copy(w_k2r[:, k], w_kv2[:, k, 0, :].rearrange("p (g d) -> p g d", g=2)
                                      .unsqueeze(2).broadcast_to([P, 2, HH, DH]))

        @block.tensor
        def _(pe):
            pe.wait_ge(w_sem, 16 * len(loads))
            for k in range(KD):
                mm = nc.tensor.matmul(bank[k][:, 0:D], gk1_t[:, k * P:(k + 1) * P], gk2[:], start=True, stop=True)
            mm.then_inc(prep_done, 1)
            for k in range(KD):
                mm = nc.tensor.matmul(bank[2 + k][:, 0:RANK], v_nat[:, k * P:(k + 1) * P], fb_t[:], start=True,
                                      stop=True)
            mm.then_inc(prep_done, 1)

        @block.sync
        def _(sp):
            for dst, src in nat_loads:
                sp.dma_start(dst, src).then_inc(nat_sem, 16)
            sp.wait_ge(prep, 1)
            for r in range(4):
                sp.dma_start(b_nat[32 * r:32 * r + E, :], a["L0_ffn_bu"]).then_inc(b_sem, 16)
            for dst, src in loads:
                sp.dma_start(dst, src).then_inc(w_sem, 16)
            head_load(sp, 0)
            sp.wait_ge(w_sem, 16 * len(loads))

    tern_pe, tern_act, tern_clear = sem("tern_pe"), sem("tern_act"), sem("tern_clear")
    with nc.Block() as block:

        @block.tensor
        def _(pe):
            n = 0

            def turn(parts):
                nonlocal n
                if n >= 4:
                    pe.wait_ge(tern_act, n - 3)
                for j, part in enumerate(parts):
                    mm = nc.tensor.transpose(bank[2 + n % 4][:, j * P:(j + 1) * P], part, ident[:])
                mm.then_inc(tern_pe, 1)
                n += 1

            for k in range(KD):
                for m in range(0, MT, 4):
                    turn([fc_ter[:, m + j, k * P:(k + 1) * P] for j in range(4)])
            for m in range(0, MT, 2):
                turn([pj_ter[:, j % 2, (m + j // 2) * P:(m + j // 2 + 1) * P] for j in range(4)])
            for m in range(0, MT, 4):
                turn([u_st[:, m + j, :] for j in range(4)])

        @block.scalar
        def _(act):
            for b in range(2):
                rest = slice(QB * (1 - b), QB * (2 - b))
                for parity in range(2):
                    nc.scalar.copy(shift[rest, parity, b, :, :],
                                   same_q[rest, :].unsqueeze(1).broadcast_to([QB, H, QB]))
            targets = [fc_t[:, k, m * P:(m + 4) * P] for k in range(KD) for m in range(0, MT, 4)]
            targets += [pj_t[:, m:m + 2, :].rearrange("p m d -> p (m d)") for m in range(0, MT, 2)]
            targets += [u_t[:, m * P:(m + 4) * P] for m in range(0, MT, 4)]
            for n, target in enumerate(targets):
                act.wait_ge(tern_pe, n + 1)
                nc.scalar.copy(target, bank[2 + n % 4][:]).then_inc(tern_act, 1)

        @block.gpsimd
        def _(pool):
            pool.wait_ge(tern_act, 10)
            nc.gpsimd.memset(gates[:], 0.0).then_inc(tern_clear, 1)
            head_rstd(pool)

        @block.vector
        def _(dve):
            for c in range(NC):
                head_stats(dve, c)
            head_moments(dve)

    with nc.Block() as block:

        @block.vector
        def _(dve):
            for c in range(NC):
                head_normalise(dve, c)
            for c in range(NC):
                head_logits(dve, c, "before")

        @block.gpsimd
        def _(pool):
            nc.gpsimd.memset(attn2[:, 0, 0:1], 0.0).then_inc(out_done, 1)

        @block.tensor
        def _(pe):
            for c in range(NC + 1):
                if c < NC:
                    head_turn(pe, c, "before")
                if c:
                    head_project(pe, c - 1, "before")

        @block.scalar
        def _(act):
            for c in range(NC):
                head_turned(act, c, "before")

    nc.all_engine_barrier(sems_to_clear=range(first, last + 1))

    with nc.Fori(0, n_seq) as seq:
        with nc.Block() as block:

            @block.sync
            def _(sp):
                sp.wait_ge(out_done, seq * (16 * NC) + 1)
                for c in range(NC):
                    sp.dma_start(x[:, c, :], x_dram[bass.ds(seq * NC + c, 1), :, :].rearrange("o p d -> (o p) d"))\
                      .then_inc(s["xc_ok"], 16)
                sp.wait_ge(s["qx2_ok"], 2 * NC)
                head_load(sp, (seq + 1) % n_seq)
                for c in range(NC):
                    sp.wait_ge(s["y2_ok"], c + 1)
                    sp.dma_start(out_dram[bass.ds(seq * NC + c, 1), :, :].rearrange("o p d -> (o p) d"),
                                 x[:, c, :]).then_inc(out_done, 16)

            @block.gpsimd
            def _(pool):

                def head_queries(src, c, done):
                    for half in range(2):
                        nc.gpsimd.tensor_tensor(
                            qx[:, c % 2, half * HH:(half + 1) * HH, :],
                            src[:, half:half + 1, c * P:(c + 1) * P].broadcast_to([P, HH, P]),
                            head_mask[:].unsqueeze(2).broadcast_to([P, HH, P]), ALU.mult).then_inc(s[done], 1)

                def norm_affine(c):
                    pool.wait_ge(s["ost_ok"], 2 * c + 2)
                    nc.gpsimd.tensor_scalar(o_veps[:], o_mom[:, 1:2], EPS, None, ALU.add).then_inc(s["ove_ok"], 1)
                    pool.wait_ge(s["ove_ok"], c + 1)
                    if c:
                        pool.wait_ge(s["onorm_ok"], c)
                    nc.gpsimd.tensor_tensor(o_rstd[:], o_veps[:], minus_half[:, 0:1], ALU.pow)\
                      .then_inc(s["ors_ok"], 1)
                    pool.wait_ge(s["onorm_ok"], c + 1)
                    nc.gpsimd.tensor_tensor(o_gam[:], o_norm[:], bc_gamma[:], ALU.mult).then_inc(s["ogam_ok"], 1)
                    pool.wait_ge(s["ogam_ok"], c + 1)
                    if c:
                        pool.wait_ge(s["y_ok"], c)
                    nc.gpsimd.tensor_tensor(o_bet[:], o_gam[:], bc_beta[:], ALU.add).then_inc(s["obet_ok"], 1)

                def decay_low(i):
                    pool.wait_ge(s["gkh_ok"], i + 1)
                    nc.gpsimd.tensor_tensor(gk_lo[:, 2 * i:2 * i + 2, :], gk[:, 2 * i:2 * i + 2, :],
                                            gk_hi[:, 2 * i:2 * i + 2, :].bitcast(F32), ALU.subtract)\
                      .then_inc(s["gkl_ok"], 1)

                def rstd2(part, lo, hi):
                    pool.wait_ge(s["st2"], 2 * hi)
                    nc.gpsimd.tensor_scalar(veps[:, lo:hi], moments[:, lo:hi, 1], EPS, None, ALU.add)\
                      .then_inc(s["ve2"], 1)
                    pool.wait_ge(s["ve2"], part + 1)
                    nc.gpsimd.tensor_tensor(rstd[:, lo:hi], veps[:, lo:hi], minus_half[:, lo:hi], ALU.pow)\
                      .then_inc(s["rs2"], 1)

                pool.wait_ge(s["qk_ok"], 2)
                head_queries(qt, 0, "qx_ok")
                for i in range(NC // 2):
                    decay_low(i)
                for c in range(NC):
                    if c == NC - 1:
                        rstd2(0, 0, NC - 2)
                    if c:
                        norm_affine(c - 1)
                    if c + 1 < NC:
                        pool.wait_ge(s["dst_ok"], c + 1)
                        if c:
                            pool.wait_ge(s["state_ok"], c)
                        nc.gpsimd.tensor_tensor(
                            end_mask[:], decay_state[:, c % 2, 1, :].rearrange("p (h f) -> p h f", h=2),
                            head_block[:].unsqueeze(1).broadcast_to([P, 2, P]), ALU.mult).then_inc(s["end_ok"], 1)
                        if c + 1 == 4:
                            pool.wait_ge(s["qk_ok"], 6)
                        if c:
                            pool.wait_ge(s["at_ok"], 4 * c)
                        head_queries(qt, c + 1, "qx_ok")

                rstd2(1, NC - 2, NC - 1)
                norm_affine(NC - 1)
                rstd2(2, NC - 1, NC)
                pool.wait_ge(s["qk2_ok"], 2)
                head_queries(q2, 0, "qx2_ok")
                for c in range(1, NC):
                    if c == 4:
                        pool.wait_ge(s["qk2_ok"], 6)
                    if c >= 2:
                        pool.wait_ge(s["stp_ok"], 4 * (c - 1))
                    head_queries(q2, c, "qx2_ok")
                    if c in (3, 5):
                        g = c // 4
                        pool.wait_ge(s["xh_ok"], g + 1)
                        nc.gpsimd.tensor_tensor(xl[:, g], xt[:, :, g * 512:(g + 1) * 512], xh[:, g].bitcast(F32),
                                                ALU.subtract).then_inc(s["xl_ok"], 1)
                for n in range(NG * MT):
                    pool.wait_ge(s["relu_ok"], n + 1)
                    if n >= 3:
                        pool.wait_ge(s["sql_ok"], n - 2)
                    nc.gpsimd.tensor_tensor(sq[:, n % 3, :], relu[:, n % 3, :], relu[:, n % 3, :], ALU.mult)\
                      .then_inc(s["sq_ok"], 1)
                    if n == 5:
                        head_rstd(pool)

            @block.scalar
            def _(act):
                def pair(t, i):
                    return t[:, 2 * i:2 * i + 2, :]


                def first_queries_keys(n):
                    g, which, half = n // 4, n // 2 % 2, n % 2
                    act.wait_ge(s["qkp_ok"], n + 1)
                    nc.scalar.copy((kt if which else qt)[:, half, g * 512:(g + 1) * 512], bank[4 + n % 4][:])\
                      .then_inc(s["qk_ok"], 1)
                for i in range(NC // 2):
                    nc.scalar.activation(pair(zact, i), pair(z, i), ACT.Abs).then_inc(s["zabs_ok"], 1)
                for i in range(NC // 2):
                    act.wait_ge(s["zabs_ok"], i + 1)
                    nc.scalar.activation(pair(zact, i), pair(zact, i), ACT.Exp, scale=-1.0)\
                      .then_inc(s["zexp_ok"], 1)
                act.wait_ge(s["top_ok"], NC + 1)
                nc.scalar.activation(gexp[:], gdiff[:], ACT.Exp).then_inc(s["gexp_ok"], 1)
                first_queries_keys(0)
                first_queries_keys(1)
                for i in range(NC // 2):
                    act.wait_ge(s["zexp_ok"], i + 1)
                    nc.scalar.activation(pair(zact, i), pair(zact, i), ACT.Ln, bias=1.0).then_inc(s["zln_ok"], 1)
                for n in range(2, 8):
                    first_queries_keys(n)
                for b in range(2):
                    act.wait_ge(s["gtp_ok"], b + 1)
                    nc.scalar.copy(gates_t[:, 4 * b:4 * b + 4, :], bank[1 + b][:].rearrange("p (c t) -> p c t", t=P))\
                      .then_inc(s["gt_ok"], 1)

                def decays(c):
                    act.wait_ge(s["cum_ok"], c + 1)
                    if c >= 2:
                        act.wait_ge(s["vt_ok"], c - 1)
                    nc.scalar.activation(decay_in[:, c % 2, :], bank[3][:, 0:D], ACT.Exp, scale=-1.0 / 16)\
                      .then_inc(s["din_ok"], 1)
                    if c >= 2:
                        act.wait_ge(s["o1_ok"], c - 1)
                    nc.scalar.activation(decay_out[:, c % 2, :], bank[3][:, 0:D], ACT.Exp, scale=1.0 / 16)\
                      .then_inc(s["dout_ok"], 1)
                    if c >= 2:
                        act.wait_ge(s["end_ok"], c - 1)
                        act.wait_ge(s["smid_ok"], c - 1)
                    nc.scalar.activation(decay_state[:, c % 2], bank[4][:].rearrange("p (a f) -> p a f", a=2),
                                         ACT.Exp, scale=1.0 / 16).then_inc(s["dst_ok"], 1)

                def output_turned(c):
                    act.wait_ge(s["ytp_ok"], c + 1)
                    if c:
                        act.wait_ge(s["s_ok"], c)
                    nc.scalar.copy(yt[:], bank[7][:, 0:D].rearrange("p (k t) -> p k t", k=KD))\
                      .then_inc(s["yt_ok"], 1)

                decays(0)
                for c in range(NC):
                    act.wait_ge(s["vg_ok"], c + 1)
                    if c:
                        act.wait_ge(s["sg_ok"], c)
                    nc.scalar.activation(tanh_g[:], bank[0][:, D:2 * D], ACT.Tanh, scale=0.5)\
                      .then_inc(s["tg_ok"], 1)
                    if c + 1 < NC:
                        act.wait_ge(s["kp_ok"], c + 1)
                        if c:
                            act.wait_ge(s["ds_ok"], c)
                        nc.scalar.copy(ktok[:], bank[1][:, 0:D]).then_inc(s["ktok_ok"], 1)
                    if c:
                        output_turned(c - 1)
                    act.wait_ge(s["hgtp_ok"], c + 1)
                    if c:
                        act.wait_ge(s["f_ok"], c)
                    nc.scalar.copy(hgt[:], bank[2][:].rearrange("p (j t) -> p j t", t=P)).then_inc(s["hgt_ok"], 1)
                    if c + 1 < NC:
                        decays(c + 1)
                    act.wait_ge(s["ot_ok"], c + 1)
                    if c:
                        act.wait_ge(s["otok_ok"], c)
                    nc.scalar.copy(ot[:], bank[7][:, 0:D].rearrange("p (k t) -> p k t", k=KD))\
                      .then_inc(s["ots_ok"], 1)
                    act.wait_ge(s["f_ok"], c + 1)
                    if c:
                        act.wait_ge(s["f1_ok"], c)
                    nc.scalar.activation(tanh_f[:], bank[5][:, 0:D], ACT.Tanh, scale=0.25).then_inc(s["tf_ok"], 1)

                def chunk_turned(c):
                    act.wait_ge(s["xt2p_ok"], c + 1)
                    nc.scalar.copy(xt[:, :, c * P:(c + 1) * P],
                                   bank[turn_banks[c]][:, 0:D].rearrange("p (k t) -> p k t", k=KD))\
                      .then_inc(s["xt2_ok"], 1)

                def queries_keys(n):
                    g, which, half = n // 4, n // 2 % 2, n % 2
                    act.wait_ge(s["qk2p_ok"], n + 1)
                    dst, bias = (kt, b_k2) if which else (q2, b_q2)
                    nc.scalar.activation(dst[:, half, g * 512:(g + 1) * 512], bank[qk_banks[n]][:],
                                         ACT.Identity, bias=bias[:, half:half + 1]).then_inc(s["qk2_ok"], 1)

                for c in range(NC - 1):
                    chunk_turned(c)
                queries_keys(0)
                output_turned(NC - 1)
                for n in range(1, 4):
                    queries_keys(n)
                chunk_turned(NC - 1)

                def attention_turned(c):
                    act.wait_ge(s["o2tp_ok"], c + 1)
                    if c:
                        act.wait_ge(s["s2p_ok"], c)
                    nc.scalar.copy(o2t, bank[0][:, 0:D])\
                      .then_inc(s["o2t_ok"], 1)

                def queries_bf(c, half):
                    act.wait_ge(s["qx2_ok"], 2 * c + half + 1)
                    if c:
                        act.wait_ge(s["sc_ok"], 8 * c)
                    nc.scalar.copy(qx_bf[:, half * HH:(half + 1) * HH, :],
                                   qx[:, c % 2, half * HH:(half + 1) * HH, :]).then_inc(s["qxb_ok"], 1)

                queries_bf(0, 0)
                queries_bf(0, 1)
                for n in range(4, 8):
                    queries_keys(n)
                for c in range(NC):
                    for u in range(4):
                        n = 4 * c + u
                        act.wait_ge(s["stp_ok"], n + 1)
                        if n >= 2:
                            act.wait_ge(s["pv_ok"], n - 1)
                        nc.scalar.activation(pr[:, n % 2], bank[5 + n % 2][:].rearrange("p (h q) -> p h q", q=QB),
                                             ACT.Exp).then_inc(s["pr_ok"], 1)
                        if c and u == 0:
                            attention_turned(c - 1)
                        if c + 1 < NC and u >= 1 and u < 3:
                            queries_bf(c + 1, u - 1)
                attention_turned(NC - 1)

                def squares(n):
                    act.wait_ge(s["sq_ok"], n + 1)
                    if n >= 3:
                        act.wait_ge(s["pj_ok"], n - 2)
                    nc.scalar.copy(sq_hi[:, n % 3, :], sq[:, n % 3, :]).then_inc(s["sqh_ok"], 1)

                def ffn_scaled(g):
                    act.wait_ge(s["pj_ok"], (g + 1) * MT)
                    if g:
                        act.wait_ge(s["ftp_ok"], 4 * g)
                    for o in range(KD):
                        nc.scalar.activation(ft[:, o, :], bank[5 + o][:], ACT.Identity, scale=scale_pj[:, o:o + 1])\
                          .then_inc(s["ft_ok"], 1)

                def ffn_tanh(c):
                    act.wait_ge(s["ftp_ok"], c + 1)
                    if c:
                        act.wait_ge(s["f3_ok"], c)
                    nc.scalar.activation(tanh_f[:], bank[7 if c % 2 else 4][:, 0:D], ACT.Tanh, scale=0.5)\
                      .then_inc(s["tf2_ok"], 1)

                for n in range(NG * MT + 2):
                    if MT + 2 <= n < MT + 2 + NC:
                        head_turned(act, n - MT - 2)
                    if n < NG * MT:
                        act.wait_ge(s["h2p_ok"], n + 1)
                        if n >= 3:
                            act.wait_ge(s["sq_ok"], n - 2)
                        nc.scalar.activation(relu[:, n % 3, :], bank[1 + n % 3][:], ACT.Relu,
                                             scale=scale_fc[:, n % MT:n % MT + 1]).then_inc(s["relu_ok"], 1)
                    if 1 <= n <= NG * MT:
                        squares(n - 1)
                    if n == MT + 2:
                        ffn_scaled(0)
                    if MT + 3 <= n < MT + 7:
                        ffn_tanh(n - MT - 3)
                ffn_scaled(1)
                for c in range(4, NC):
                    ffn_tanh(c)

            @block.vector
            def _(dve):
                for c in range(NC):
                    nc.vector.max(top[:, c, :], logits[:, c, :]).then_inc(s["top_ok"], 1)
                dve.wait_ge(s["top_ok"], NC)
                nc.vector.tensor_sub(gdiff[:], top[:, :, 1], top[:, :, 0]).then_inc(s["top_ok"], 1)
                for c in range(NC):
                    nc.vector.max_index(top_i[:, c, :], top[:, c, :], logits[:, c, :]).then_inc(s["top_ok"], 1)
                dve.wait_ge(s["top_ok"], 2 * NC + 1)
                nc.vector.tensor_copy(top_f[:], top_i[:, :, 0:2]).then_inc(s["gsel"], 1)
                dve.wait_ge(s["gexp_ok"], 1)
                nc.vector.tensor_scalar(gden[:], gexp[:], 1.0, None, ALU.add).then_inc(s["gsel"], 1)
                dve.wait_ge(s["gsel"], 2)
                nc.vector.reciprocal(g_top[:, 0, :], gden[:]).then_inc(s["gsel"], 1)
                dve.wait_ge(s["gsel"], 3)
                nc.vector.tensor_tensor(g_top[:, 1, :], gexp[:], g_top[:, 0, :], ALU.mult).then_inc(s["gsel"], 1)
                for r in range(2):
                    nc.vector.tensor_tensor(g_hit[:, r], top_f[:, :, r:r + 1].broadcast_to([P, NC, E]),
                                            expert_no[:].unsqueeze(1).broadcast_to([P, NC, E]), ALU.is_equal)\
                      .then_inc(s["gsel"], 1)
                dve.wait_ge(s["gsel"], 6)
                for r in range(2):
                    nc.vector.tensor_tensor(g_hit[:, r], g_hit[:, r],
                                            g_top[:, r, :].unsqueeze(2).broadcast_to([P, NC, E]), ALU.mult)\
                      .then_inc(s["gsel"], 1)
                dve.wait_ge(s["gsel"], 8)
                nc.vector.tensor_add(g_all[:], g_hit[:, 0], g_hit[:, 1]).then_inc(s["gates_ok"], 1)
                dve.wait_ge(s["gates_ok"], 1)
                nc.vector.tensor_copy(g_hi[:], g_all[:]).then_inc(s["gates_ok"], 1)
                dve.wait_ge(s["gates_ok"], 2)
                for r in range(4):
                    cols = slice(32 * r, 32 * r + E)
                    if r < 2:
                        ins = nc.vector.tensor_copy(gates[:, :, cols], g_hi[:].bitcast(F32))
                    else:
                        ins = nc.vector.tensor_tensor(gates[:, :, cols], g_all[:], g_hi[:].bitcast(F32), ALU.subtract)
                    ins.then_inc(s["gates_ok"], 1)
                for i in range(NC // 2):
                    two = slice(2 * i, 2 * i + 2)
                    dve.wait_ge(s["zln_ok"], i + 1)
                    nc.vector.scalar_tensor_tensor(gk[:, two, :], z[:, two, :], 0.0, zact[:, two, :], ALU.min,
                                                   ALU.subtract).then_inc(s["gk_ok"], 1)
                    dve.wait_ge(s["gk_ok"], i + 1)
                    nc.vector.tensor_copy(gk_hi[:, two, :], gk[:, two, :]).then_inc(s["gkh_ok"], 1)
                dve.wait_ge(s["xc_ok"], 16 * NC)

                def gated_output(c):
                    dve.wait_ge(s["obet_ok"], c + 1)
                    dve.wait_ge(s["sg_ok"], c + 1)
                    if c:
                        dve.wait_ge(s["ytp_ok"], c)
                    nc.vector.tensor_tensor(y_tok[:], o_bet[:], silu_g[:, c % 2, :], ALU.mult)\
                      .then_inc(s["y_ok"], 1)

                def normalise_output(c):
                    dve.wait_ge(s["ors_ok"], c + 1)
                    if c:
                        dve.wait_ge(s["ogam_ok"], c)
                    nc.vector.tensor_scalar(o_norm[:], o_tok[:], o_mom[:, 0:1], o_rstd[:], ALU.subtract, ALU.mult)\
                      .then_inc(s["onorm_ok"], 1)

                def finish_chunk(c):
                    dve.wait_ge(s["s_ok"], c + 1)
                    dve.wait_ge(s["f1_ok"], c + 1)
                    if c:
                        dve.wait_ge(s["x_ok"], c)
                    nc.vector.scalar_tensor_tensor(sf[:], f_gate[:], 0.125, bank[6][:, 0:D], ALU.mult,
                                                   ALU.mult).then_inc(s["f2_ok"], 1)
                    dve.wait_ge(s["f2_ok"], c + 1)
                    nc.vector.tensor_add(x[:, c, :], x[:, c, :], sf[:]).then_inc(s["x_ok"], 1)
                    dve.wait_ge(s["x_ok"], c + 1)
                    nc.vector.bn_stats(stats[:, c, :], x[:, c, :]).then_inc(s["st2"], 1)
                    dve.wait_ge(s["st2"], 2 * c + 1)
                    nc.vector.bn_aggr(moments[:, c, :], stats[:, c, :]).then_inc(s["st2"], 1)

                def normalise2(c):
                    nc.vector.tensor_scalar(xn[:, c, :], x[:, c, :], moments[:, c, 0:1], rstd[:, c:c + 1],
                                            ALU.subtract, ALU.mult).then_inc(s["xn2_ok"], 1)

                def causal_scores(c, j):
                    dve.wait_ge(s["at_ok"], 4 * c + j + 1)
                    if c and j == 0:
                        dve.wait_ge(s["ot_ok"], c)
                    nc.vector.tensor_tensor(am[:, 4 * j:4 * j + 4, :],
                                            bank[5 + j % 2][:].rearrange("p (h t) -> p h t", t=P),
                                            causal[:].unsqueeze(1).broadcast_to([P, 4, P]), ALU.mult)\
                      .then_inc(s["am_ok"], 1)

                for c in range(NC):
                    dve.wait_ge(s["tg_ok"], c + 1)
                    dve.wait_ge(s["din_ok"], c + 1)
                    if c:
                        dve.wait_ge(s["ds_ok"], c)
                    nc.vector.tensor_tensor(
                        vt[:, :, 0:4:3, :], bank[0][:, 0:D].rearrange("p (j e d) -> p j e d", e=2, d=DH),
                        decay_in[:, c % 2, :].rearrange("p (j e d) -> p j e d", e=2, d=DH), ALU.mult)\
                      .then_inc(s["vt_ok"], 1)
                    if c >= 2:
                        dve.wait_ge(s["y_ok"], c - 1)
                    nc.vector.scalar_tensor_tensor(silu_g[:, c % 2, :], tanh_g[:], 1.0, bank[0][:, D:2 * D],
                                                   ALU.add, ALU.mult).then_inc(s["sg_ok"], 1)
                    dve.wait_ge(s["hp_ok"], c + 1)
                    if c:
                        dve.wait_ge(s["hg_ok"], c)
                    nc.vector.tensor_add(hb[:], bank[2][:], bc_down[:]).then_inc(s["hb_ok"], 1)
                    if c:
                        gated_output(c - 1)
                    causal_scores(c, 0)
                    causal_scores(c, 1)
                    dve.wait_ge(s["hb_ok"], c + 1)
                    if c:
                        dve.wait_ge(s["hgtp_ok"], c)
                    nc.vector.scalar_tensor_tensor(
                        hg[:].rearrange("p (e b) -> p e b", e=E), hb[:].rearrange("p (e b) -> p e b", e=E), 0.0,
                        g_all[:, c, :].unsqueeze(2).broadcast_to([P, E, BN]), ALU.max, ALU.mult)\
                      .then_inc(s["hg_ok"], 1)
                    causal_scores(c, 2)
                    dve.wait_ge(s["dst_ok"], c + 1)
                    if c:
                        dve.wait_ge(s["state_ok"], c)
                        dve.wait_ge(s["ot_ok"], c)
                    nc.vector.tensor_tensor(state_mid[:], state[:],
                                            decay_state[:, c % 2, 0, :].rearrange("p (h f) -> p h f", h=2),
                                            ALU.mult).then_inc(s["smid_ok"], 1)
                    causal_scores(c, 3)
                    if c + 1 < NC:
                        dve.wait_ge(s["ds_ok"], c + 1)
                        dve.wait_ge(s["smid_ok"], c + 1)
                        nc.vector.tensor_tensor(state_sum[:], bank[0][:, 0:D].rearrange("p (h f) -> p h f", h=2),
                                                state_mid[:], ALU.add).then_inc(s["ssum_ok"], 1)
                        dve.wait_ge(s["ssum_ok"], c + 1)
                        dve.wait_ge(s["end_ok"], c + 1)
                        nc.vector.tensor_tensor(state[:], state_sum[:], end_mask[:], ALU.mult)\
                          .then_inc(s["state_ok"], 1)
                    else:
                        dve.wait_ge(s["rs2"], 1)
                        for b in range(NC - 2):
                            normalise2(b)
                    if c:
                        finish_chunk(c - 1)
                    dve.wait_ge(s["otok_ok"], c + 1)
                    dve.wait_ge(s["dout_ok"], c + 1)
                    if c:
                        dve.wait_ge(s["onorm_ok"], c)
                    nc.vector.tensor_tensor(o_tok[:], bank[7][:, D:2 * D], decay_out[:, c % 2, :], ALU.mult)\
                      .then_inc(s["o1_ok"], 1)
                    dve.wait_ge(s["o1_ok"], c + 1)
                    nc.vector.bn_stats(o_stats[:], o_tok[:]).then_inc(s["ost_ok"], 1)
                    dve.wait_ge(s["ost_ok"], 2 * c + 1)
                    nc.vector.bn_aggr(o_mom[:], o_stats[:]).then_inc(s["ost_ok"], 1)
                    dve.wait_ge(s["tf_ok"], c + 1)
                    nc.vector.scalar_tensor_tensor(f_gate[:], tanh_f[:], 1.0, bank[5][:, 0:D], ALU.add, ALU.mult)\
                      .then_inc(s["f1_ok"], 1)
                    if c == NC - 1:
                        dve.wait_ge(s["rs2"], 2)
                        normalise2(NC - 2)
                    normalise_output(c)
                dve.wait_ge(s["smid_ok"], NC)
                nc.vector.memset(state[:], 0.0).then_inc(s["state_ok"], 1)
                gated_output(NC - 1)

                def keys_bf(g):
                    dve.wait_ge(s["qk2_ok"], 4 * g + 4)
                    pad = HALF + S if g else 0
                    nc.vector.memset(k2_bf[:, :, pad:pad + HALF], 0.0).then_inc(s["kbf_ok"], 1)
                    lo = HALF + g * 512
                    nc.vector.tensor_copy(k2_bf[:, :, lo:lo + 512], k2[:, :, lo:lo + 512]).then_inc(s["kbf_ok"], 1)

                finish_chunk(NC - 1)
                dve.wait_ge(s["rs2"], 3)
                normalise2(NC - 1)
                def low_rank(g):
                    dve.wait_ge(s["tp_ok"], g + 1)
                    t_bank = bank[0 if g else 5]
                    nc.vector.tensor_copy(t_hi, t_bank[:]).then_inc(s["thi_ok"], 1)
                    nc.vector.tensor_copy(t_st[0:64, g, :], t_bank[0:64, :]).then_inc(s["tst_ok"], 1)
                    dve.wait_ge(s["thi_ok"], g + 1)
                    nc.vector.tensor_tensor(t_st[64:128, g, :], t_bank[64:128, :], t_hi[64:128, :].bitcast(F32),
                                            ALU.subtract).then_inc(s["tst_ok"], 1)

                def largest(c, r):
                    dve.wait_ge(s["sc_ok"], 8 * c + r + 1)
                    if c >= 2 and r == 0:
                        dve.wait_ge(s["dmax_ok"], 4 * c - 4)
                    for j in range(2):
                        rough = bank[1 + r % 4][:, j * KW:(j + 1) * KW]
                        ins = nc.vector.tensor_tensor_reduce(
                            out=rough, in0=rough, in1=chunk_band[:], scale=1.0, scalar=BIG, op0=ALU.add,
                            op1=ALU.max, accum_out=row_max[:, c % 2, 2 * r + j:2 * r + j + 1])
                    ins.then_inc(s["max_ok"], 1)

                def diagonal(c, half):
                    heads = slice(half * HH, (half + 1) * HH)
                    dve.wait_ge(s["max_ok"], 8 * c + 4 * half + 4)
                    if c >= 2:
                        dve.wait_ge(s["stp_ok"], 4 * c - 6 + 2 * half)
                    for b in range(2):
                        rows = slice(b * QB, (b + 1) * QB)
                        nc.vector.tensor_tensor(
                            shift[rows, c % 2, b, heads, :], minus_same[rows, :].unsqueeze(1).broadcast_to([QB, HH, QB]),
                            row_max[rows, c % 2, heads].unsqueeze(2).broadcast_to([QB, HH, QB]), ALU.mult)\
                          .then_inc(s["dmax_ok"], 1)

                def attention_out(c):
                    dve.wait_ge(s["pv_ok"], 4 * c + 4)
                    if c:
                        dve.wait_ge(s["o2_ok"], c)
                    o_bank = bank[7][:, 0:H * DV].rearrange("p (h d) -> p h d", d=DV)
                    nc.vector.reciprocal(rden[:], o_bank[:, :, DH]).then_inc(s["rden_ok"], 1)
                    dve.wait_ge(s["rden_ok"], c + 1)
                    if c:
                        dve.wait_ge(s["o2tp_ok"], c)
                    nc.vector.tensor_tensor(o2.rearrange("p (h d) -> p h d", d=DH), o_bank[:, :, 0:DH],
                                            rden[:].unsqueeze(2).broadcast_to([P, H, DH]), ALU.mult)\
                      .then_inc(s["o2_ok"], 1)

                def attention_bias(c):
                    dve.wait_ge(s["s2p_ok"], c + 1)
                    nc.vector.tensor_tensor(attn2[:, c, :], bank[0][:, D:2 * D], bc_o2[:], ALU.add)\
                      .then_inc(s["s2_ok"], 1)

                low_rank(0)
                keys_bf(0)
                for half in range(2):
                    for r in range(4 * half, 4 * half + 4):
                        largest(0, r)
                    diagonal(0, half)
                dve.wait_ge(s["v2p_ok"], 1)
                even = bank[0][:, 0:(NC + 1) * 2 * DH].rearrange("p (w g d) -> p w g d", g=2, d=DH)
                for g in range(2):
                    for dst, src, parity, first in ((slice(0, P), slice(0, P), 0, 0), (slice(0, QB), slice(QB, P), 1, 0),
                                                    (slice(QB, P), slice(0, QB), 1, 1)):
                        rows = dst.stop - dst.start
                        nc.vector.tensor_tensor(
                            v2[dst, parity:2 * NC:2, g, 0:DH], even[src, first:first + NC, g, :],
                            bc_v2[src, g * DH:(g + 1) * DH].unsqueeze(1).broadcast_to([rows, NC, DH]), ALU.add)\
                          .then_inc(s["v2_ok"], 1)
                dve.wait_ge(s["v2_ok"], 6)
                nc.vector.memset(v2[0:HALF, 0, :, 0:DH], 0.0).then_inc(s["v2_ok"], 1)
                nc.vector.memset(v2[P - HALF:P, 2 * NC - 1, :, 0:DH], 0.0).then_inc(s["v2_ok"], 1)
                for c in range(NC):
                    if c:
                        attention_bias(c - 1)
                    if c + 1 < NC:
                        for r in range(4):
                            largest(c + 1, r)
                        diagonal(c + 1, 0)
                        largest(c + 1, 4)
                        largest(c + 1, 5)
                    attention_out(c)
                    if c + 1 < NC:
                        largest(c + 1, 6)
                        largest(c + 1, 7)
                        diagonal(c + 1, 1)
                    if c == 0:
                        keys_bf(1)
                    if c in (1, 2):
                        g = c - 1
                        nc.vector.tensor_copy(xh[:, g], xt[:, :, g * 512:(g + 1) * 512]).then_inc(s["xh_ok"], 1)
                attention_bias(NC - 1)

                def finish2(c):
                    dve.wait_ge(s["tf2_ok"], c + 1)
                    if c:
                        dve.wait_ge(s["f4_ok"], c)
                    nc.vector.scalar_tensor_tensor(f_gate[:], tanh_f[:], 1.0, bank[7 if c % 2 else 4][:, 0:D],
                                                   ALU.add, ALU.mult).then_inc(s["f3_ok"], 1)
                    dve.wait_ge(s["f3_ok"], c + 1)
                    if c:
                        dve.wait_ge(s["y2_ok"], c)
                    nc.vector.scalar_tensor_tensor(sf[:], f_gate[:], 0.5, attn2[:, c, :], ALU.mult, ALU.mult)\
                      .then_inc(s["f4_ok"], 1)
                    dve.wait_ge(s["f4_ok"], c + 1)
                    nc.vector.tensor_add(x[:, c, :], x[:, c, :], sf[:]).then_inc(s["y2_ok"], 1)

                for n in range(NG * MT + 1):
                    if MT + 2 <= n < MT + 6:
                        head_logits(dve, n - MT - 2)
                    if MT + 3 <= n < MT + 7:
                        finish2(n - MT - 3)
                    if n < NG * MT:
                        dve.wait_ge(s["sqh_ok"], n + 1)
                        if n >= 3:
                            dve.wait_ge(s["pj_ok"], n - 2)
                        nc.vector.tensor_tensor(sq_lo[:, n % 3, :], sq[:, n % 3, :],
                                                sq_hi[:, n % 3, :].bitcast(F32), ALU.subtract)\
                          .then_inc(s["sql_ok"], 1)
                    if n == 1:
                        low_rank(1)
                    if n < 4:
                        head_stats(dve, 2 * n)
                        head_stats(dve, 2 * n + 1)
                    if n == 4:
                        head_moments(dve)
                    if 7 <= n < 11:
                        head_normalise(dve, 2 * (n - 7))
                        head_normalise(dve, 2 * (n - 7) + 1)
                head_logits(dve, 4)
                finish2(4)
                finish2(5)
                head_logits(dve, 5)
                finish2(6)
                finish2(7)
                head_logits(dve, 6)
                head_logits(dve, 7)

            @block.tensor
            def _(pe):
                def token_major(dst, c, w):
                    for k in range(KD):
                        mm = nc.tensor.matmul(dst, xt[:, k, c * P:(c + 1) * P], w[:, k, :], start=(k == 0),
                                              stop=(k == KD - 1))
                    return mm

                for n in range(8):
                    g, which, half = n // 4, n // 2 % 2, n % 2
                    if n >= 4:
                        pe.wait_ge(s["qk_ok"], n - 3)
                    w = w_k if which else w_q
                    for k in range(KD):
                        mm = nc.tensor.matmul(bank[4 + n % 4][:], w[:, k, half * P:(half + 1) * P],
                                              xt[:, k, g * 512:(g + 1) * 512], start=(k == 0), stop=(k == KD - 1))
                    mm.then_inc(s["qkp_ok"], 1)

                def cumulate(c):
                    pe.wait_ge(s["gkl_ok"], c // 2 + 1)
                    if c == 0:
                        pe.wait_ge(s["qk_ok"], 5)
                    else:
                        pe.wait_ge(s["dst_ok"], c)
                    for i, out in enumerate((bank[3][:, 0:D], bank[4][:, 0:D], bank[4][:, D:2 * D])):
                        nc.tensor.matmul(out, cumulator[:, i, :], gk_hi[:, c, :], start=True, stop=False)
                        mm = nc.tensor.matmul(out, cumulator[:, i, :], gk_lo[:, c, :], start=False, stop=True)
                    mm.then_inc(s["cum_ok"], 1)

                cumulate(0)
                pe.wait_ge(s["gates_ok"], 6)
                for b in range(2):
                    for j in range(4):
                        mm = nc.tensor.transpose(bank[1 + b][:, j * P:(j + 1) * P], gates[:, 4 * b + j, :], ident[:])
                    mm.then_inc(s["gtp_ok"], 1)

                def output_turn(c):
                    pe.wait_ge(s["y_ok"], c + 1)
                    for k in range(KD):
                        mm = nc.tensor.transpose(bank[7][:, k * P:(k + 1) * P], y_tok[:, k * P:(k + 1) * P],
                                                 ident[:])
                    mm.then_inc(s["ytp_ok"], 1)

                def attention_token_major(c):
                    pe.wait_ge(s["ots_ok"], c + 1)
                    for k in range(KD):
                        mm = nc.tensor.transpose(bank[7][:, D + k * P:D + (k + 1) * P], ot[:, k, :], ident[:])
                    mm.then_inc(s["otok_ok"], 1)

                def output_project(c):
                    pe.wait_ge(s["yt_ok"], c + 1)
                    for k in range(KD):
                        mm = nc.tensor.matmul(bank[6][:, 0:D], yt[:, k, :], w_out[:, k, :], start=(k == 0),
                                              stop=(k == KD - 1))
                    mm.then_inc(s["s_ok"], 1)

                for c in range(NC):
                    if c:
                        pe.wait_ge(s["state_ok"], c)
                    token_major(bank[0][:], c, w_vg).then_inc(s["vg_ok"], 1)
                    if c + 1 < NC:
                        pe.wait_ge(*((s["ktok_ok"], c) if c else (s["gt_ok"], 1)))
                        if c == 0 or c == 4:
                            pe.wait_ge(s["qk_ok"], 8 if c else 4)
                        for half in range(2):
                            mm = nc.tensor.transpose(bank[1][:, half * P:(half + 1) * P],
                                                     kt[:, half, c * P:(c + 1) * P], ident[:])
                        mm.then_inc(s["kp_ok"], 1)
                    pe.wait_ge(*((s["hgt_ok"], c) if c else (s["gt_ok"], 2)))
                    token_major(bank[2][:], c, w_down).then_inc(s["hp_ok"], 1)
                    for j in range(4):
                        half = j // 2
                        if c == 0 and j == 0:
                            pe.wait_ge(s["qk_ok"], 8)
                        if j >= 2:
                            pe.wait_ge(s["am_ok"], 4 * c + j - 1)
                        elif j == 0 and c:
                            pe.wait_ge(s["f1_ok"], c)
                        elif j == 1 and c >= 2:
                            pe.wait_ge(s["f2_ok"], c - 1)
                        pe.wait_ge(s["qx_ok"], 2 * c + half + 1)
                        nc.tensor.matmul(bank[5 + j % 2][:], kt[:, half, c * P:(c + 1) * P],
                                         qx[:, c % 2, 4 * j:4 * j + 4, :], start=True, stop=True)\
                          .then_inc(s["at_ok"], 1)
                    if c:
                        output_turn(c - 1)
                    pe.wait_ge(s["hg_ok"], c + 1)
                    for j in range(EB // P):
                        mm = nc.tensor.transpose(bank[2][:, j * P:(j + 1) * P], hg[:, j * P:(j + 1) * P], ident[:])
                    mm.then_inc(s["hgtp_ok"], 1)
                    if c + 1 < NC:
                        cumulate(c + 1)
                    pe.wait_ge(s["am_ok"], 4 * c + 4)
                    if c:
                        output_project(c - 1)
                    pe.wait_ge(s["vt_ok"], c + 1)
                    pe.wait_ge(s["smid_ok"], c + 1)
                    for half in range(2):
                        nc.tensor.matmul(bank[7][:, half * P:(half + 1) * P], state_mid[:, half, :],
                                         qt[:, half, c * P:(c + 1) * P], start=True, stop=False,
                                         skip_group_check=True)
                        for e in range(2):
                            for j in range(4):
                                mm = nc.tensor.matmul(bank[7][32 * j:32 * j + 32, half * P:(half + 1) * P],
                                                      vt[:, half * 4 + j, 2 * e:2 * e + 2, :],
                                                      am[:, half * HH + 2 * j + e, :], start=False, stop=(e == 1),
                                                      skip_group_check=True)
                    mm.then_inc(s["ot_ok"], 1)
                    if c + 1 < NC:
                        pe.wait_ge(s["ktok_ok"], c + 1)
                        pe.wait_ge(s["sg_ok"], c + 1)
                        for half in range(2):
                            mm = nc.tensor.matmul(bank[0][:, half * P:(half + 1) * P],
                                                  ktok[:, half * P:(half + 1) * P],
                                                  vt[:, half * 4:half * 4 + 4, 0:4:3, :], start=True, stop=True)
                        mm.then_inc(s["ds_ok"], 1)
                    pe.wait_ge(s["hgt_ok"], c + 1)
                    for j in range(EB // P):
                        nc.tensor.matmul(bank[5][:, 0:D], hgt[:, j, :], w_up[:, j, :], start=(j == 0), stop=False)
                        if j == 1 and c == NC - 1:
                            attention_token_major(c)
                    nc.tensor.matmul(bank[5][:, 0:D], gates_t[:, c, :], b_up[:], start=False, stop=True)\
                      .then_inc(s["f_ok"], 1)
                    if c < NC - 1:
                        attention_token_major(c)

                def chunk_turn(c):
                    pe.wait_ge(s["xn2_ok"], c + 1)
                    if c >= 2:
                        pe.wait_ge(s["xt2_ok"], c - 1)
                    for k in range(KD):
                        mm = nc.tensor.transpose(bank[turn_banks[c]][:, k * P:(k + 1) * P],
                                                 xn[:, c, k * P:(k + 1) * P], ident[:])
                    mm.then_inc(s["xt2p_ok"], 1)

                def queries_keys(n):
                    g, which, half = n // 4, n // 2 % 2, n % 2
                    pe.wait_ge(s["xt2_ok"], 4 * g + 4)
                    if n == 3:
                        pe.wait_ge(s["qk2_ok"], 1)
                    elif n == 4:
                        pe.wait_ge(s["tst_ok"], 2)
                    elif n == 5:
                        pe.wait_ge(s["f2_ok"], NC)
                    elif n >= 6:
                        pe.wait_ge(s["qk2_ok"], n - 1)
                    for k in range(KD):
                        w = w_k2r[:, k, half].rearrange("p r d -> p (r d)") if which \
                            else w_q2[:, k, half * P:(half + 1) * P]
                        mm = nc.tensor.matmul(bank[qk_banks[n]][:], w, xt[:, k, g * 512:(g + 1) * 512],
                                              start=(k == 0), stop=(k == KD - 1))
                    mm.then_inc(s["qk2p_ok"], 1)

                def window_values(lo, hi):
                    for j in range(lo, hi):
                        rows = P if j < NC else QB
                        for k in range(KD):
                            mm = nc.tensor.matmul(bank[0][0:rows, j * 2 * DH:(j + 1) * 2 * DH],
                                                  xt2[:, k, j * P:j * P + rows], w_kv2[:, k, 1, :],
                                                  start=(k == 0), stop=(k == KD - 1))
                    return mm

                def low_rank(g):
                    for k in range(KD):
                        mm = nc.tensor.matmul(bank[0 if g else 5][:], w_low[:, k, :],
                                              xt[:, k, g * 512:(g + 1) * 512], start=(k == 0), stop=(k == KD - 1))
                    mm.then_inc(s["tp_ok"], 1)

                def attention_turn(c):
                    pe.wait_ge(s["o2_ok"], c + 1)
                    if c:
                        pe.wait_ge(s["s2_ok"], c)
                    for k in range(KD):
                        mm = nc.tensor.transpose(bank[0][:, k * P:(k + 1) * P], o2[:, k * P:(k + 1) * P], ident[:])
                    mm.then_inc(s["o2tp_ok"], 1)

                def attention_project(c):
                    pe.wait_ge(s["o2t_ok"], c + 1)
                    for k in range(KD):
                        mm = nc.tensor.matmul(bank[0][:, D:2 * D], o2t[:, k * P:(k + 1) * P], w_o2[:, k, :],
                                              start=(k == 0), stop=(k == KD - 1))
                    mm.then_inc(s["s2p_ok"], 1)

                def rough_scores(c, r):
                    n = 8 * c + r
                    pe.wait_ge(s["qxb_ok"], 2 * c + r // 4 + 1)
                    if n >= 4:
                        pe.wait_ge(s["max_ok"], n - 3)
                    for j in range(2):
                        mm = nc.tensor.matmul(bank[1 + r % 4][:, j * KW:(j + 1) * KW], qx_bf[:, 2 * r + j, :],
                                              k2_bf[:, r // 4, c * P:c * P + KW], start=True, stop=True)
                    mm.then_inc(s["sc_ok"], 1)

                def scores(n):
                    c, g, b = n // 4, n // 2 % 2, n % 2
                    if n >= 2:
                        pe.wait_ge(s["pr_ok"], n - 1)
                    pe.wait_ge(s["dmax_ok"], 4 * c + 2 * g + b + 1)
                    st = bank[5 + n % 2][:]
                    nc.tensor.matmul(st, band_or_one[:, b, :], shift[:, c % 2, b, g * HH:(g + 1) * HH, :],
                                     start=True, stop=False)
                    nc.tensor.matmul(st, k2[:, g, c * P + b * QB:c * P + b * QB + P],
                                     qx[:, c % 2, g * HH:(g + 1) * HH, b * QB:(b + 1) * QB], start=False, stop=True)\
                      .then_inc(s["stp_ok"], 1)

                def values(n):
                    c, g, b = n // 4, n // 2 % 2, n % 2
                    pe.wait_ge(s["pr_ok"], n + 1)
                    if n % 4 == 0 and c:
                        pe.wait_ge(s["o2_ok"], c)
                    for h in range(HH):
                        col = (g * HH + h) * DV
                        mm = nc.tensor.matmul(bank[7][b * QB:(b + 1) * QB, col:col + DV], pr[:, n % 2, h, :],
                                              v2[:, 2 * c + b, g, :], start=True, stop=True)
                    mm.then_inc(s["pv_ok"], 1)

                pe.wait_ge(s["sg_ok"], NC)
                pe.wait_ge(s["dout_ok"], NC)
                for c in range(NC - 1):
                    chunk_turn(c)
                queries_keys(0)
                output_turn(NC - 1)
                queries_keys(1)
                output_project(NC - 1)
                queries_keys(2)
                queries_keys(3)
                pe.wait_ge(s["f1_ok"], NC)
                low_rank(0)
                chunk_turn(NC - 1)
                window_values(0, 7)
                queries_keys(4)
                pe.wait_ge(s["kbf_ok"], 2)
                for r in range(4):
                    rough_scores(0, r)
                queries_keys(5)
                for r in range(4, 8):
                    rough_scores(0, r)
                queries_keys(6)
                queries_keys(7)
                window_values(7, NC + 1).then_inc(s["v2p_ok"], 1)
                pe.wait_ge(s["qk2_ok"], 8)
                for c in range(NC):
                    scores(4 * c)
                    if c:
                        attention_turn(c - 1)
                    scores(4 * c + 1)
                    if c == 0:
                        pe.wait_ge(s["v2_ok"], 8)
                    values(4 * c)
                    if c:
                        attention_project(c - 1)
                    if c == 2:
                        pe.wait_ge(s["kbf_ok"], 4)
                    if c + 1 < NC:
                        rough_scores(c + 1, 0)
                        rough_scores(c + 1, 1)
                    scores(4 * c + 2)
                    values(4 * c + 1)
                    if c + 1 < NC:
                        rough_scores(c + 1, 2)
                        rough_scores(c + 1, 3)
                    scores(4 * c + 3)
                    values(4 * c + 2)
                    if c + 1 < NC:
                        rough_scores(c + 1, 4)
                        rough_scores(c + 1, 5)
                    values(4 * c + 3)
                    if c + 1 < NC:
                        rough_scores(c + 1, 6)
                        rough_scores(c + 1, 7)

                def hidden(n, part):
                    g, m = n // MT, n % MT
                    h_bank = bank[1 + n % 3][:]
                    if part == 0:
                        if n >= 3:
                            pe.wait_ge(s["relu_ok"], n - 2)
                        if m == 0:
                            pe.wait_ge(s["xl_ok"], g + 1)
                        for t in (xh, xl):
                            for k in range(KD):
                                nc.tensor.matmul(h_bank, fc_t[:, k, m * P:(m + 1) * P], t[:, g, k, :],
                                                 start=(t is xh and k == 0), stop=False)
                    else:
                        if m == 0:
                            pe.wait_ge(s["tst_ok"], 2 * g + 2)
                        nc.tensor.matmul(h_bank, u_t[:, m * P:(m + 1) * P], t_st[:, g, :], start=False, stop=True)\
                          .then_inc(s["h2p_ok"], 1)

                def project(n):
                    m = n % MT
                    pe.wait_ge(s["sql_ok"], n + 1)
                    if n == MT:
                        pe.wait_ge(s["ft_ok"], KD)
                    for o in range(KD):
                        for part in (sq_hi, sq_lo):
                            mm = nc.tensor.matmul(bank[5 + o][:], pj_t[:, m, o * P:(o + 1) * P], part[:, n % 3, :],
                                                  start=(m == 0 and part is sq_hi),
                                                  stop=(m == MT - 1 and part is sq_lo), skip_group_check=True)
                    mm.then_inc(s["pj_ok"], 1)

                def ffn_turn(c):
                    if c % 4 == 0:
                        pe.wait_ge(s["ft_ok"], KD * (c // 4 + 1))
                    if c >= 2:
                        pe.wait_ge(s["f3_ok"], c - 1)
                    j = c % 4
                    for k in range(KD):
                        mm = nc.tensor.transpose(bank[7 if c % 2 else 4][:, k * P:(k + 1) * P],
                                                 ft[:, k, j * P:(j + 1) * P], ident[:])
                    mm.then_inc(s["ftp_ok"], 1)

                for n in range(NG * MT):
                    hidden(n, 0)
                    if n >= MT + 2:
                        head_turn(pe, n - MT - 2)
                    hidden(n, 1)
                    if n == 0:
                        attention_turn(NC - 1)
                    if n == 1:
                        attention_project(NC - 1)
                    if n == 2:
                        pe.wait_ge(s["s2_ok"], NC)
                        low_rank(1)
                    if n >= 3:
                        project(n - 3)
                    if MT + 2 <= n < MT + 6:
                        head_project(pe, n - MT - 2)
                    if MT + 3 <= n < MT + 7:
                        ffn_turn(n - MT - 3)
                project(NG * MT - 3)
                head_turn(pe, 6)
                project(NG * MT - 2)
                head_turn(pe, 7)
                project(NG * MT - 1)
                pe.wait_ge(s["relu_ok"], NG * MT)
                head_project(pe, 4)
                ffn_turn(4)
                ffn_turn(5)
                head_project(pe, 5)
                ffn_turn(6)
                ffn_turn(7)
                head_project(pe, 6)
                head_project(pe, 7)

        nc.all_engine_barrier(sems_to_clear=range(first, last + 1))

    with nc.Block() as block:

        @block.sync
        def _(sp):
            sp.wait_ge(out_done, 16 * NC * n_seq + 1)
    ctx.close()


_OUT = (16, S, D)


def kernel(**inputs):
    import concourse.bacc as bacc
    from concourse.bass_utils import run_bass_kernel_spmd

    nc = bacc.Bacc("TRN2", target_bir_lowering=False, num_devices=1, dynamic_dma_scratch_size=1024)
    arrays, args = {}, {}
    for name, value in inputs.items():
        v = np.ascontiguousarray(value)
        v = v.reshape(v.shape or (1,))
        arrays[f"in_{name}"] = v
        args[name] = nc.dram_tensor(f"in_{name}", v.shape, mybir.dt.from_np(v.dtype), kind="ExternalInput").ap()
    out = nc.dram_tensor("out_0", _OUT, F32, kind="ExternalOutput").ap()
    build_program(nc, args, out, _OUT[0])
    result = run_bass_kernel_spmd(nc, [arrays], core_ids=[0])
    return result.results[0]["out_0"]
```
